# Optimizing a Trainium2 kernel written in Bass

```python
import numpy as np
import jax
import jax.numpy as jnp

def _softmax(x, axis=-1):
    return jax.nn.softmax(x, axis=axis)

def _gelu(x):
    return jax.nn.gelu(x, approximate=True)

def _silu(x):
    return jax.nn.silu(x)

def _sigmoid(x):
    return jax.nn.sigmoid(x)

def _layernorm(x, axis=-1, eps=1e-05):
    m = jnp.mean(x, axis=axis, keepdims=True)
    v = jnp.var(x, axis=axis, keepdims=True)
    return (x - m) / jnp.sqrt(v + eps)

def _scatter_add(tgt, idx, src, axis=0):
    return tgt.at[idx].add(src)

def _segment_sum(src, seg, n):
    return jax.ops.segment_sum(src, seg, n)
kernel_name = 'mk_xattn_ffn_d1_seqx_r8_d12426'

def setup_inputs(seed: int=0):
    np.random.seed(seed)
    _w = jnp.asarray

    def _rec_inputs():
        import jax
        import jax.numpy as jnp
        _rk = jax.random.key(seed)
        x = 7.22e-05 + 1 * jax.random.normal(jax.random.fold_in(_rk, 1), (64, 64, 256), jnp.float32)
        _lenS = 64 - jax.random.randint(jax.random.fold_in(_rk, 7), (64,), 0, max(1, 64 // 4) + 1, jnp.int32)
        _lenS2 = 64 - jax.random.randint(jax.random.fold_in(_rk, 8), (64,), 0, max(1, 64 // 4) + 1, jnp.int32)
        _ctx_512P = jax.random.normal(jax.random.fold_in(_rk, 11), (64, 16, 64), jnp.float32)
        _ctx_512c = jax.random.dirichlet(jax.random.fold_in(_rk, 511), 0.3 * jnp.ones((16,), jnp.float32), (64, 64))
        _ctx_512t = jnp.einsum('bsk,bkd->bsd', _ctx_512c, _ctx_512P)
        _ctx_512t = _ctx_512t * jax.lax.rsqrt(jnp.mean(jnp.square(_ctx_512t)) + 1e-12) * 0.953939
        ctx_512 = -0.000514642 + 1.00011 * (_ctx_512t + 0.3 * jax.random.normal(jax.random.fold_in(_rk, 611), (64, 64, 64), jnp.float32))
        return (x, ctx_512)
    x, ctx_512 = _rec_inputs()

    def _L0_xattn_setup():
        import jax, jax.numpy as jnp
        import numpy as np
        N_HEADS = 16
        N_KV_HEADS = 4
        ROPE_THETA = 10000.0
        EPS = 1e-05

        def _rms_norm(x, w):
            var = jnp.mean(x * x, axis=-1, keepdims=True)
            return x * jax.lax.rsqrt(var + EPS) * w

        def _rope_sin_cos(T, head_dim, dtype):
            inv_freq = 1.0 / ROPE_THETA ** (jnp.arange(0, head_dim, 2, dtype=jnp.float32) / head_dim)
            t = jnp.arange(T, dtype=jnp.float32)
            freqs = jnp.outer(t, inv_freq)
            emb = jnp.concatenate([freqs, freqs], -1)
            return (jnp.sin(emb).astype(dtype)[None, None], jnp.cos(emb).astype(dtype)[None, None])

        def _rotate_half(x):
            h = x.shape[-1] // 2
            x1, x2 = (x[..., :h], x[..., h:])
            return jnp.concatenate([-x2, x1], axis=-1)
        key = jax.random.key(seed)
        ks = jax.random.split(key, 6)
        B, T, C = (2, 256, 256)
        Ckv = C // N_HEADS * N_KV_HEADS
        return {'q': jax.random.normal(ks[0], (B, T, C), jnp.float32), 'k': jax.random.normal(ks[1], (B, T, Ckv), jnp.float32), 'v': jax.random.normal(ks[2], (B, T, Ckv), jnp.float32), 'q_norm_w': jnp.ones((C,), jnp.float32), 'k_norm_w': jnp.ones((Ckv,), jnp.float32), 'w_out': jax.random.normal(ks[3], (C, C), jnp.float32) * C ** (-0.5)}
    _L0_xattn_all = _L0_xattn_setup()
    _L0_xattn_in = {k: v for k, v in _L0_xattn_all.items() if k in ('q_norm_w', 'k_norm_w', 'w_out')}
    del _L0_xattn_all

    def _L0_ffn_setup():
        import jax, jax.numpy as jnp
        import numpy as np
        E = 16
        K = 2
        D = 256
        I = 176
        CAP = 128
        VOCAB = 16160
        key = jax.random.key(seed)
        ks = jax.random.split(key, 11)
        B, S = (4, 128)
        sd = 1.0 / np.sqrt(D)
        si = 1.0 / np.sqrt(I)
        return {'x': jax.random.normal(ks[0], (B, S, D), jnp.float32), 'input_ids': jax.random.randint(ks[1], (B, S), 0, VOCAB, dtype=jnp.int64), 'gate_w': jax.random.normal(ks[2], (E, D), jnp.float32) * sd, 'gate_b': jax.random.normal(ks[3], (E,), jnp.float32) * 0.01, 'W1': jax.random.normal(ks[4], (E, I, D), jnp.float32) * sd, 'W3': jax.random.normal(ks[5], (E, I, D), jnp.float32) * sd, 'W2': jax.random.normal(ks[6], (E, D, I), jnp.float32) * si, 'Ws1': jax.random.normal(ks[7], (I, D), jnp.float32) * sd, 'Ws3': jax.random.normal(ks[8], (I, D), jnp.float32) * sd, 'Ws2': jax.random.normal(ks[9], (D, I), jnp.float32) * si}
    _L0_ffn_all = _L0_ffn_setup()
    _L0_ffn_in = {k: v for k, v in _L0_ffn_all.items() if k in ('input_ids', 'gate_w', 'gate_b', 'W1', 'W3', 'W2', 'Ws1', 'Ws3', 'Ws2')}
    del _L0_ffn_all
    return {'x': x, 'ctx_512': ctx_512, 'L0_xattn_q_norm_w': _L0_xattn_in['q_norm_w'], 'L0_xattn_k_norm_w': _L0_xattn_in['k_norm_w'], 'L0_xattn_w_out': _L0_xattn_in['w_out'], 'L0_ffn_input_ids': _L0_ffn_in['input_ids'], 'L0_ffn_gate_w': _L0_ffn_in['gate_w'], 'L0_ffn_gate_b': _L0_ffn_in['gate_b'], 'L0_ffn_W1': _L0_ffn_in['W1'], 'L0_ffn_W3': _L0_ffn_in['W3'], 'L0_ffn_W2': _L0_ffn_in['W2'], 'L0_ffn_Ws1': _L0_ffn_in['Ws1'], 'L0_ffn_Ws3': _L0_ffn_in['Ws3'], 'L0_ffn_Ws2': _L0_ffn_in['Ws2']}

def reference(x, ctx_512, L0_xattn_q_norm_w, L0_xattn_k_norm_w, L0_xattn_w_out, L0_ffn_input_ids, L0_ffn_gate_w, L0_ffn_gate_b, L0_ffn_W1, L0_ffn_W3, L0_ffn_W2, L0_ffn_Ws1, L0_ffn_Ws3, L0_ffn_Ws2):
    import jax
    import jax.numpy as jnp

    def _L0_xattn_ref(q, k, v, q_norm_w, k_norm_w, w_out):
        import jax, jax.numpy as jnp
        import numpy as np
        N_HEADS = 16
        N_KV_HEADS = 4
        ROPE_THETA = 10000.0
        EPS = 1e-05

        def _rms_norm(x, w):
            var = jnp.mean(x * x, axis=-1, keepdims=True)
            return x * jax.lax.rsqrt(var + EPS) * w

        def _rope_sin_cos(T, head_dim, dtype):
            inv_freq = 1.0 / ROPE_THETA ** (jnp.arange(0, head_dim, 2, dtype=jnp.float32) / head_dim)
            t = jnp.arange(T, dtype=jnp.float32)
            freqs = jnp.outer(t, inv_freq)
            emb = jnp.concatenate([freqs, freqs], -1)
            return (jnp.sin(emb).astype(dtype)[None, None], jnp.cos(emb).astype(dtype)[None, None])

        def _rotate_half(x):
            h = x.shape[-1] // 2
            x1, x2 = (x[..., :h], x[..., h:])
            return jnp.concatenate([-x2, x1], axis=-1)
        B, T, C = q.shape
        hd = C // N_HEADS
        g = N_HEADS // N_KV_HEADS
        q = _rms_norm(q, q_norm_w)
        k = _rms_norm(k, k_norm_w)
        q = q.reshape(B, T, N_HEADS, hd).transpose(0, 2, 1, 3)
        k = k.reshape(B, T, N_KV_HEADS, hd).transpose(0, 2, 1, 3)
        v = v.reshape(B, T, N_KV_HEADS, hd).transpose(0, 2, 1, 3)
        sin, cos = _rope_sin_cos(T, hd, q.dtype)
        q = q * cos + _rotate_half(q) * sin
        k = k * cos + _rotate_half(k) * sin
        qg = q.reshape(B, N_KV_HEADS, g, T, hd)
        scale = 1.0 / jnp.sqrt(jnp.asarray(hd, q.dtype))
        scores = jnp.einsum('bgnqd,bgkd->bgnqk', qg, k) * scale
        causal = jnp.tril(jnp.ones((T, T), bool))
        scores = jnp.where(causal, scores, jnp.asarray(-1e+30, scores.dtype))
        attn = jax.nn.softmax(scores, axis=-1)
        out = jnp.einsum('bgnqk,bgkd->bgnqd', attn, v)
        out = out.reshape(B, N_HEADS, T, hd).transpose(0, 2, 1, 3).reshape(B, T, C)
        return out @ w_out.T

    def _L0_ffn_ref(x, input_ids, gate_w, gate_b, W1, W3, W2, Ws1, Ws3, Ws2):
        import jax, jax.numpy as jnp
        import numpy as np
        E = 16
        K = 2
        D = 256
        I = 176
        CAP = 128
        VOCAB = 16160
        shape = x.shape
        xt = x.reshape(-1, D)
        T = xt.shape[0]
        logits = xt.astype(jnp.float32) @ gate_w.astype(jnp.float32).T
        scores = jnp.sqrt(jax.nn.softplus(logits))
        _, idx = jax.lax.top_k(scores + gate_b, K)
        w = jnp.take_along_axis(scores, idx, axis=1)
        w = w / jnp.sum(w, axis=1, keepdims=True)
        e = idx.reshape(-1)
        onehot = jax.nn.one_hot(e, E, dtype=jnp.int32)
        pos = jnp.sum(onehot * (jnp.cumsum(onehot, axis=0) - 1), axis=1)
        valid = pos < CAP
        posc = jnp.where(valid, pos, 0)
        x_pairs = jnp.repeat(xt, K, axis=0)
        x_pairs = jnp.where(valid[:, None], x_pairs, 0.0)
        buf = jnp.zeros((E, CAP, D), xt.dtype).at[e, posc].add(x_pairs)
        g = jnp.einsum('ecd,eid->eci', buf, W1).astype(jnp.float32)
        u = jnp.einsum('ecd,eid->eci', buf, W3).astype(jnp.float32)
        h = (jax.nn.silu(g) * u).astype(xt.dtype)
        out = jnp.einsum('eci,edi->ecd', h, W2)
        y_pairs = out[e, posc] * (w.reshape(-1) * valid)[:, None]
        y = y_pairs.reshape(T, K, D).sum(axis=1)
        gs = jax.nn.silu((xt @ Ws1.T).astype(jnp.float32))
        us = (xt @ Ws3.T).astype(jnp.float32)
        shared = (gs * us).astype(xt.dtype) @ Ws2.T
        return (y + shared).astype(x.dtype).reshape(shape)
    x = x + _L0_xattn_ref(_layernorm(x, axis=-1), ctx_512, ctx_512, L0_xattn_q_norm_w, L0_xattn_k_norm_w, L0_xattn_w_out)
    x = x + _L0_ffn_ref(_layernorm(x, axis=-1), L0_ffn_input_ids, L0_ffn_gate_w, L0_ffn_gate_b, L0_ffn_W1, L0_ffn_W3, L0_ffn_W2, L0_ffn_Ws1, L0_ffn_Ws3, L0_ffn_Ws2)
    return x

_drawn_inputs = setup_inputs


def setup_inputs(seed=0):
    import zlib

    import numpy as np

    out = dict(_drawn_inputs(seed))
    spreads = {'L0_xattn_q_norm_w': (1.0, 0.2), 'L0_xattn_k_norm_w': (1.0, 0.2)}
    factors = {}
    for name, (base, spread) in spreads.items():
        noise = np.random.default_rng([zlib.crc32(name.encode()), seed]).standard_normal(out[name].shape)
        drawn = base * np.exp(spread * noise) if base else spread * noise
        out[name] = jnp.asarray(drawn.astype(out[name].dtype))
    for name, factor in factors.items():
        out[name] = (out[name] * factor).astype(out[name].dtype)
    return out
```

```python
import concourse.bass as bass
from concourse import mybir
from contextlib import ExitStack


RC = {"desc": 0, "tri": 16, "ia": 144, "ib": 160, "rev": 168, "tok": 200, "blk": 232, "sel": 240}


def xattn_moe_kernel(
    nc: bass.Bass,
    x: bass.AP,
    ctx: bass.AP,
    wq_norm: bass.AP,
    wk_norm: bass.AP,
    w_out: bass.AP,
    gate_w: bass.AP,
    gate_b: bass.AP,
    w13: bass.AP,
    w2: bass.AP,
    ws13: bass.AP,
    ws2: bass.AP,
    const_rope: bass.AP,
    const_attn: bass.AP,
    const_pick: bass.AP,
    const_route: bass.AP,
    out: bass.AP,
):
    f32, bf16, i32 = mybir.dt.float32, mybir.dt.bfloat16, mybir.dt.int32
    ALU = mybir.AluOpType
    ACT = mybir.ActivationFunctionType
    AX = mybir.AxisListType

    P = 128
    TOK, D = x.shape
    TILES = TOK // P
    S = 64
    G, NH, NL, HD = 4, 2, 2, 16
    KV = G * HD
    E = gate_b.shape[-1]
    CAP = 128
    I2 = w13.shape[-1]
    I = I2 // 2
    IA, IB = 112, I - 112
    LN_EPS = 1e-5
    RMS_EPS = 1e-5
    FAR = 8192.0
    BLOCKS = TOK // 512
    WRING = 4

    with ExitStack() as ctx_all:
        def keep(stack, name, shape, dt):
            return stack.enter_context(nc.sbuf_tensor(name, shape, dt))

        def sem(name):
            return ctx_all.enter_context(nc.semaphore(name))

        z_rows = nc.dram_tensor("z_rows", [TOK, D], f32).ap()
        X = keep(ctx_all, "X", [P, TILES, D], f32)
        ZT = keep(ctx_all, "ZT", [P, 2, TOK], f32)
        ident = keep(ctx_all, "ident", [P, P], f32)
        GW = keep(ctx_all, "GW", [P, 2, 32], f32)
        WS13 = keep(ctx_all, "WS13", [P, 2, I2], f32)
        WS2 = keep(ctx_all, "WS2", [P, 2, D], f32)
        rc = keep(ctx_all, "rc", [P, const_route.shape[1]], f32)

        at = ExitStack()
        C = keep(at, "C", [P, TILES, KV], f32)
        ropec = keep(at, "ropec", [P, 2, P], f32)
        wqn = keep(at, "wqn", [P, 2, NL], f32)
        wkn = keep(at, "wkn", [P, 2], f32)
        kmask = keep(at, "kmask", [P, G], f32)
        ropet = keep(at, "ropet", [P, 2, 3, P], f32)
        attc = keep(at, "attc", [P, const_attn.shape[1]], f32)
        pickf = keep(at, "pickf", [80, const_pick.shape[1]], f32)
        identb = keep(at, "identb", [P, P], bf16)
        pick = keep(at, "pick", [80, 8, P], bf16)
        WO = keep(at, "WO", [P, NL, D], f32)
        stats = keep(at, "stats", [P, 2, 3, 6], f32)
        mv = keep(at, "mv", [P, 2, 3, 2], f32)
        var_in = keep(at, "var_in", [P, 2, 3], f32)
        negmean = keep(at, "negmean", [P, 2, 3], f32)
        shift = keep(at, "shift", [P, 2, 3], f32)
        zero = keep(at, "zero", [P, 8], f32)
        veps = keep(at, "veps", [P, 2], f32)
        rstd = keep(at, "rstd", [P, 2, 3], f32)
        neghalf = keep(at, "neghalf", [P, 3], f32)
        XH = keep(at, "XH", [P, 2, 2, D], f32)
        KH = keep(at, "KH", [P, 2, 2, P], f32)
        rp = keep(at, "rp", [P, 2, 3 * P], f32)
        QKT = keep(at, "QKT", [P, 2, 3, P], f32)
        KBD = keep(at, "KBD", [P, 2, 2, G * S], f32)
        QA = keep(at, "QA", [P, 2, NH, 2, P], bf16)
        KA = keep(at, "KA", [P, 2, 2, G * S], bf16)
        MX = keep(at, "MX", [P, 2, 16], bf16)
        MM = keep(at, "MM", [80, 2, P], bf16)
        PT = keep(at, "PT", [P, 2, NH, 2, 2, P], f32)
        VBD = keep(at, "VBD", [P, 2, 2, 2, 2, HD], f32)
        logsum = keep(at, "logsum", [P, 2 * P], f32)
        rsum = keep(at, "rsum", [P, 2 * P], f32)
        OT = keep(at, "OT", [P, 2, NL, 2, S], f32)
        Z = keep(at, "Z", [P, 2, D], f32)
        at.close()

        ff = ctx_all.enter_context(ExitStack())
        GA = keep(ff, "GA", [P, 2, 512], f32)
        UA = keep(ff, "UA", [P, 2, 512], f32)
        H = keep(ff, "H", [P, 2, 2, 512], f32)
        DS = keep(ff, "DS", [P, 2, 2, 512], f32)
        OUTB = keep(ff, "OUTB", [P, 2, 2, 512], f32)
        LS = keep(ff, "LS", [P, 2, 512], f32)
        GB = keep(ff, "GB", [P, E], f32)
        RW = [keep(ff, f"RW{i}", [P, TILES * E], f32) for i in range(7)]
        RS = [keep(ff, f"RS{i}", [P, TILES], f32) for i in range(4)]
        MB = keep(ff, "MB", [P, TILES * E], bf16)
        trib = keep(ff, "trib", [P, P], bf16)
        onesb = keep(ff, "onesb", [P, P], bf16)
        cnt = keep(ff, "cnt", [P, E], f32)
        slot_i = keep(ff, "slot_i", [P, TILES * E], i32)
        ab_i = keep(ff, "ab_i", [P, 2, TILES * E], i32)
        HT = TILES // 4
        OA = keep(ff, "OA", [P, 2, HT * E, 16], f32)
        OBV = keep(ff, "OBV", [P, 2, 2, HT * E, 8], f32)
        OBE = keep(ff, "OBE", [P, HT * E, 8], f32)
        dg = keep(ff, "dg", [P, 4, 8, 8], f32)
        dr = keep(ff, "dr", [P, 4, 8], f32)
        lay = keep(ff, "lay", [P, 4, 8, 16], f32)
        idx = keep(ff, "idx", [P, E], i32)
        wslot = keep(ff, "wslot", [P, E], f32)
        W13 = keep(ff, "W13", [P, WRING, 2, I2], f32)
        W2 = keep(ff, "W2", [P, WRING, 2, D], f32)
        XG = keep(ff, "XG", [P, WRING, D], f32)
        XE = keep(ff, "XE", [P, 2, 2, P], f32)
        SE = keep(ff, "SE", [P, 2, 2, P], f32)
        HE = keep(ff, "HE", [P, 2, 2, P], f32)
        YE = keep(ff, "YE", [P, WRING, D], f32)

        PS = ctx_all.enter_context(nc.psum_tensor("PS", [P, 8, 512], f32))
        B = [PS[:, i, :] for i in range(8)]

        plain_ps, swap_ps, max_ps, sc_ps, pv_ps, mix_ps = B[0], B[1], (B[2], B[3]), (B[4], B[5]), B[6], B[7]
        mixb = mix_ps[:, 256:320].bitcast(bf16)

        x_in = [sem(f"x_in{i}") for i in range(4)]
        rope_in, attc_in, wout_in, ws_in, rc_in = (sem(n) for n in ("rope_in", "attc_in", "wout_in", "ws_in", "rc_in"))
        v_in = [sem(f"v_in{i}") for i in range(2)]
        zero_done, setup_pool = sem("zero_done"), sem("setup_pool")
        const_b, tables = sem("const_b"), sem("tables")
        stats_done, aggr_done, var_done = sem("stats_done"), sem("aggr_done"), sem("var_done")
        veps_done = sem("veps_done")
        rstd_done, xhat_done, khat_done = sem("rstd_done"), sem("xhat_done"), sem("khat_done")
        shift_done, swap_done = sem("shift_done"), sem("swap_done")
        qk_transposed, roped, qkt_done = sem("qk_transposed"), sem("roped"), sem("qkt_done")
        kbd_done = [sem(f"kbd_done{b}") for b in range(2)]
        ka_done, qa_done, max_scored, max_done = sem("ka_done"), sem("qa_done"), sem("max_scored"), sem("max_done")
        max_transposed, mm_done, scored, probs_done = sem("max_transposed"), sem("mm_done"), sem("scored"), sem("probs_done")
        pv_done, log_done, rsum_done, ot_done = sem("pv_done"), sem("log_done"), sem("rsum_done"), sem("ot_done")
        projected, x1_done, z_stats, z_aggr, z_var = sem("projected"), sem("x1_done"), sem("z_stats"), sem("z_aggr"), sem("z_var")
        z_done, z_transposed, zt_done = sem("z_done"), sem("z_transposed"), sem("zt_done")
        z_stored = [sem(f"z_stored{i}") for i in range(2)]

        def after(eng, s, n):
            if not isinstance(n, int) or n > 0:
                eng.wait_ge(s, n)

        def half(u, q):
            return (u - q) // 2 + 1 if isinstance(u, int) else None

        FIRST, LOOP0, LOOP1, LAST = -2, 8, 30, TILES + 7
        X_CHUNKS = [(0, 1), (1, 4), (4, 8), (8, TILES)]

        def pipeline(eng, body):
            for t in range(FIRST, LOOP0):
                body(t, t % 2, t // 2)
            with eng.Fori(0, (LOOP1 - LOOP0) // 2) as i:
                for p in range(2):
                    body(i * 2 + (LOOP0 + p), p, i + LOOP0 // 2)
            for t in range(LOOP1, LAST):
                body(t, t % 2, t // 2)

        def active(t, lag):
            return not isinstance(t, int) or 0 <= t - lag < TILES

        def x_loaded(eng, t, lag):
            if isinstance(t, int):
                for c, (lo, _) in enumerate(X_CHUNKS):
                    if t - lag == lo:
                        eng.wait_ge(x_in[c], 32)

        def key_blocks(eng, u, q, b):
            eng.wait_ge(qkt_done, u + 1)
            after(eng, scored, u - 1)
            after(eng, ka_done, u - 1)
            eng.tensor_tensor(KBD[:, q, b, :].rearrange("p (g k) -> p g k", g=G),
                              QKT[:, q, NL, b * S:(b + 1) * S].unsqueeze(1).to_broadcast([P, G, S]),
                              kmask[:, :].unsqueeze(2).to_broadcast([P, G, S]), ALU.mult).then_inc(kbd_done[b], 1)

        block = ctx_all.enter_context(nc.Block())

        lg_done, ls_done, lt_done, l_done = sem("lg_done"), sem("ls_done"), sem("lt_done"), sem("l_done")
        rt = sem("rt")
        exp_done, ln_done, sqrt_done = sem("exp_done"), sem("ln_done"), sem("sqrt_done")
        mask_done, prefix_done, cnt_done = sem("mask_done"), sem("prefix_done"), sem("cnt_done")
        hot_done, dispatched, lay_done, listed, lists_done = (
            sem("hot_done"), sem("dispatched"), sem("lay_done"), sem("listed"), sem("lists_done"))
        gu_done, silu_done, h_done, dn_done, dn_copied, res_done = (
            sem("gu_done"), sem("silu_done"), sem("h_done"), sem("dn_done"), sem("dn_copied"), sem("res_done"))
        res_stored = [sem(f"res_stored{i}") for i in range(2)]
        w_in = [sem(f"w_in{i}") for i in range(WRING)]
        xg_in = [sem(f"xg_in{i}") for i in range(WRING)]
        xe_t, xe_done, ge_done, se_done, he_done, ye_ps, ye_done = (
            sem("xe_t"), sem("xe_done"), sem("ge_done"), sem("se_done"), sem("he_done"), sem("ye_ps"), sem("ye_done"))
        added = sem("added")

        ctx_v = ctx.rearrange("(n k) (gp g2 d) -> n k gp g2 d", k=S, gp=2, g2=2)

        @block.sync
        def _(sp):
            x_v = x.rearrange("(n p) c -> p n c", p=P)
            c_v = ctx.rearrange("(n p) c -> p n c", p=P)

            def load_x(c):
                lo, hi = X_CHUNKS[c]
                sp.dma_start(C[:, lo:hi, :], c_v[:, lo:hi, :]).then_inc(x_in[c], 16)
                sp.dma_start(X[:, lo:hi, :], x_v[:, lo:hi, :]).then_inc(x_in[c], 16)

            load_x(0)
            sp.dma_start(ident[:, :], const_rope[:, 0:P]).then_inc(rope_in, 16)
            sp.dma_start(ropec[:, :, :], const_rope[:, P:3 * P].rearrange("p (a b) -> p a b", a=2)).then_inc(rope_in, 16)
            sp.dma_start(kmask[:, :], const_rope[:, 3 * P:3 * P + G]).then_inc(rope_in, 16)
            sp.dma_start(wqn[:, :, :], wq_norm).then_inc(rope_in, 16)
            sp.dma_start(wkn[:, :], wk_norm).then_inc(rope_in, 16)
            load_x(1)
            sp.dma_start(attc[:, :], const_attn).then_inc(attc_in, 16)
            sp.dma_start(pickf[:, :], const_pick).then_inc(attc_in, 16)
            load_x(2)
            sp.dma_start(WO[:, :, :], w_out).then_inc(wout_in, 16)
            load_x(3)
            sp.dma_start(rc[:, :], const_route).then_inc(rc_in, 16)
            sp.dma_start(WS13[:, :, :], ws13).then_inc(ws_in, 16)
            sp.dma_start(WS2[0:IA, 0, :], ws2[0:IA, :]).then_inc(ws_in, 16)
            sp.dma_start(WS2[0:IB, 1, :], ws2[IA:I, :]).then_inc(ws_in, 16)
            sp.dma_start(GW[:, :, 0:E], gate_w).then_inc(ws_in, 16)

            def body(t, p, i2):
                if active(t, 2):
                    u, q = t - 2, p
                    if isinstance(t, int) and t == 2:
                        sp.wait_ge(zero_done, 1)
                    after(sp, pv_done, u - 1)
                    for g2 in range(2):
                        for b in range(2):
                            sp.dma_start(VBD[g2 * S:(g2 + 1) * S, q, b, :, g2, :],
                                         ctx_v[u * 2 + b, :, :, g2, :]).then_inc(v_in[q], 16)
                if active(t, 6):
                    u, q = t - 6, p
                    sp.wait_ge(z_done, u + 1)
                    sp.dma_start(z_rows[bass.ds(u * P, P), :] if not isinstance(u, int) else z_rows[u * P:(u + 1) * P, :],
                                 Z[:, q, :]).then_inc(z_stored[q], 16)

            pipeline(sp, body)
            sp.wait_ge(zt_done, TILES)
            sp.wait_ge(z_stored[0], 16 * (TILES // 2))
            sp.wait_ge(z_stored[1], 16 * (TILES // 2))
            sp.dma_start(GB[:, :], gate_b.to_broadcast([P, E])).then_inc(rc_in, 16)

            def load_w(e, r):
                sp.dma_start(W13[:, r, :, :], w13[e, :, :, :]).then_inc(w_in[r], 16)
                sp.dma_start(W2[0:IA, r, 0, :], w2[e, 0:IA, :]).then_inc(w_in[r], 16)
                sp.dma_start(W2[0:IB, r, 1, :], w2[e, IA:I, :]).then_inc(w_in[r], 16)

            for e in range(WRING):
                load_w(e, e)
            out_v = out.rearrange("(n j p) c -> n p j c", j=2, p=P)
            with sp.Fori(0, BLOCKS) as n:
                for k in range(2):
                    sp.wait_ge(res_done, n * 2 + (k + 1))
                    sp.dma_start(out_v[n * 2 + k, :, :, :], OUTB[:, 0, k, :].rearrange("p (j c) -> p j c", j=2)).then_inc(res_stored[k], 16)
            with sp.Fori(0, E // WRING - 1) as n:
                for r in range(WRING):
                    sp.wait_ge(ye_ps, n * WRING + (r + 1))
                    load_w(n * WRING + (WRING + r), r)

        @block.gpsimd
        def _(pool):
            pool.memset(VBD[:, :, :, :, :, :], 0.0).then_inc(zero_done, 1)
            pool.memset(GW[:, :, E:2 * E], 0.0).then_inc(zero_done, 1)
            pool.memset(neghalf[:, :], -0.5).then_inc(setup_pool, 1)
            pool.memset(zero[:, :], 0.0).then_inc(setup_pool, 1)
            pool.wait_ge(setup_pool, 2)

            def body(t, p, i2):
                if active(t, 1):
                    key_blocks(pool, t - 1, (p + 1) % 2, 1)
                if active(t, -1):
                    u, q = t + 1, (p + 1) % 2
                    pool.wait_ge(xhat_done, u + 1)
                    after(pool, qk_transposed, u - 1)
                    xs = XH[:, q, 0, :].rearrange("p (n h d) -> p n h d", h=2, d=8)
                    hs = XH[:, q, 1, :].rearrange("p (n h d) -> p n h d", h=2, d=8)
                    for h in range(2):
                        pool.tensor_tensor(hs[:, :, 1 - h, :], xs[:, :, h, :], zero[:, :].unsqueeze(1).to_broadcast([P, 16, 8]), ALU.add).then_inc(swap_done, 1)
                lo = 0 if active(t, -2) else 2
                hi = 3 if active(t, 6) else 2
                if lo < hi:
                    q = (p + 1) % 2
                    if lo == 0:
                        pool.wait_ge(var_done, (t + 3) * 3)
                    if hi == 3:
                        pool.wait_ge(z_var, (t - 5) * 2)
                    after(pool, z_done, t - 7)
                    pool.tensor_tensor(rstd[:, q, lo:hi], var_in[:, q, lo:hi], neghalf[:, lo:hi], ALU.pow).then_inc(rstd_done, 1)
                    pool.wait_ge(rstd_done, t + 3)
                    pool.tensor_tensor(shift[:, q, lo:hi], negmean[:, q, lo:hi], rstd[:, q, lo:hi], ALU.mult).then_inc(shift_done, 1)
                if active(t, 0):
                    u, q = t, p
                    pool.wait_ge(roped, (u + 1) * 2)
                    after(pool, scored, u - 1)
                    after(pool, qa_done, (u - 1) * 2)
                    after(pool, kbd_done[0], u - 1)
                    pool.tensor_tensor(QKT[:, q, :, :].rearrange("p a b -> p (a b)"), rp[:, 0, :], rp[:, 1, :], ALU.add).then_inc(qkt_done, 1)
            pipeline(pool, body)

            def block_h(m, q):
                pool.wait_ge(silu_done, m * 4 + 4)
                after(pool, dn_done, m - 1)
                pool.tensor_tensor(H[0:IA, q, 0, :], GA[0:IA, 0, :], UA[0:IA, 0, :], ALU.mult).then_inc(h_done, 1)
                pool.tensor_tensor(H[0:IB, q, 1, :], GA[0:IB, 1, :], UA[0:IB, 1, :], ALU.mult).then_inc(h_done, 1)

            def block_res(m, first):
                for k in range(2):
                    pool.wait_ge(dn_copied, m * 2 + (k + 1))
                    if not first:
                        pool.wait_ge(res_stored[k], m * 16)
                    pool.tensor_tensor(OUTB[:, 0, k, :].rearrange("p (j c) -> p j c", j=2),
                                       DS[:, 0, k, :].rearrange("p (j c) -> p j c", j=2),
                                       X[:, bass.ds(m * 4 + 2 * k, 2), :] if not isinstance(m, int) else X[:, m * 4 + 2 * k:m * 4 + 2 * k + 2, :],
                                       ALU.add).then_inc(res_done, 1)

            pool.wait_ge(zt_done, TILES)
            for k in range(2):
                pool.wait_ge(z_stored[k], 16 * (TILES // 2))
            block_h(0, 0)
            block_h(1, 1)
            block_res(0, True)
            with pool.Fori(0, BLOCKS // 2 - 1) as n:
                for k in range(2):
                    block_h(n * 2 + (2 + k), k)
                    block_res(n * 2 + (1 + k), False)
            block_res(BLOCKS - 1, False)

            def gather(e):
                if e >= WRING:
                    pool.wait_ge(xe_t, e - WRING + 1)
                pool.indirect_dma_start(out=XG[:, e % WRING, :], out_offset=None, in_=z_rows,
                                        in_offset=bass.IndirectOffsetOnAxis(ap=idx[:, e:e + 1], axis=0)).then_inc(xg_in[e % WRING], 16)

            pool.wait_ge(lists_done, 2)
            pool.wait_ge(z_stored[0], 16 * (TILES // 2))
            pool.wait_ge(z_stored[1], 16 * (TILES // 2))
            for e in range(WRING):
                gather(e)
            for k in range(2):
                pool.wait_ge(res_stored[k], 16 * BLOCKS)
            for e in range(E):
                if WRING + e < E:
                    gather(WRING + e)
                pool.wait_ge(ye_done, e + 1)
                if e:
                    pool.wait_ge(added, 16 * e)
                pool.indirect_dma_start(out=out, out_offset=bass.IndirectOffsetOnAxis(ap=idx[:, e:e + 1], axis=0),
                                        in_=YE[:, e % WRING, :], in_offset=None, compute_op=ALU.add).then_inc(added, 16)
            pool.wait_ge(added, 16 * E)

        @block.scalar
        def _(act):
            nc.scalar.preload_act_table_set("natural_log_exp_and_others")
            def constants():
                act.wait_ge(rope_in, 80)
                act.activation(identb[:, :], ident[:, :], ACT.Copy).then_inc(const_b, 1)
                act.wait_ge(attc_in, 32)
                act.activation(pick[:, :, :].rearrange("p a b -> p (a b)"), pickf[:, :], ACT.Copy).then_inc(const_b, 1)
                for q in range(2):
                    for b in range(2):
                        act.activation(KA[S:P, q, b, :], attc[S:P, 0:256], ACT.Copy).then_inc(const_b, 1)
                        for nh in range(NH):
                            act.activation(QA[S:P, q, nh, b, :], attc[S:P, 256:384], ACT.Copy).then_inc(const_b, 1)
                    act.activation(MM[0:S, q, :], attc[0:S, 384:512], ACT.Copy).then_inc(const_b, 1)

            def body(t, p, i2):
                if active(t, -1):
                    u, q = t + 1, (p + 1) % 2
                    act.wait_ge(shift_done, t + 2)
                    after(act, qk_transposed, u - 1)
                    after(act, swap_done, (u - 1) * 2)
                    act.activation(XH[:, q, 0, :], X[:, u, :], ACT.Identity, bias=shift[:, p, 0:1], scale=rstd[:, p, 0:1]).then_inc(xhat_done, 1)
                if isinstance(t, int) and t == 0:
                    constants()
                if active(t, 2):
                    u, q = t - 2, p
                    act.wait_ge(max_transposed, u + 1)
                    after(act, scored, u - 1)
                    act.activation(MM[S:S + 16, q, :], mixb[0:16, :], ACT.Copy, scale=-1.0).then_inc(mm_done, 1)
                if active(t, 7):
                    u = t - 7
                    act.wait_ge(z_transposed, u + 1)
                    zt = ZT[:, :, bass.ds(u * P, P)] if not isinstance(u, int) else ZT[:, :, u * P:(u + 1) * P]
                    act.activation(zt, mix_ps[:, 0:2 * P].rearrange("p (a b) -> p a b", a=2), ACT.Copy).then_inc(zt_done, 1)
                if active(t, 1):
                    u, q = t - 1, (p + 1) % 2
                    for b in range(2):
                        act.wait_ge(kbd_done[b], u + 1)
                    after(act, max_scored, u - 1)
                    act.activation(KA[0:S, q, :, :], KBD[0:S, q, :, :], ACT.Copy).then_inc(ka_done, 1)
                if active(t, 6):
                    u, q = t - 6, p
                    act.wait_ge(shift_done, t + 3)
                    after(act, z_transposed, u - 1)
                    if not isinstance(u, int):
                        act.wait_ge(z_stored[q], (i2 - 3) * 16)
                    elif u >= 2:
                        act.wait_ge(z_stored[q], 16 * (u // 2))
                    act.activation(Z[:, q, :], X[:, u, :], ACT.Identity, bias=shift[:, 1 - q, 2:3], scale=rstd[:, 1 - q, 2:3]).then_inc(z_done, 1)
                if active(t, 2):
                    u, q = t - 2, p
                    act.wait_ge(scored, u + 1)
                    after(act, pv_done, u - 1)
                    act.activation(PT[:, q, :, :, :, :].rearrange("p n a b c -> p (n a b c)"),
                                   PS[:, 4:6, :].rearrange("p n c -> p (n c)"), ACT.Exp).then_inc(probs_done, 1)
                if active(t, 0):
                    u, q = t, p
                    act.wait_ge(qkt_done, u + 1)
                    after(act, max_scored, u - 1)
                    for nh in range(NH):
                        act.activation(QA[0:S, q, nh, :, :].rearrange("p b (nl s) -> p b nl s", nl=NL),
                                       QKT[nh * S:(nh + 1) * S, q, 0:NL, :].rearrange("p nl (b s) -> p b nl s", b=2),
                                       ACT.Copy).then_inc(qa_done, 1)
                if active(t, 3):
                    u = t - 3
                    act.wait_ge(pv_done, u + 1)
                    act.activation(logsum[:, :], pv_ps[:, 2 * P:4 * P], ACT.Ln).then_inc(log_done, 1)
                    act.wait_ge(log_done, u + 1)
                    after(act, ot_done, u)
                    act.activation(rsum[:, :], logsum[:, :], ACT.Exp, scale=-1.0).then_inc(rsum_done, 1)

            pipeline(act, body)

            for q in range(2):
                act.wait_ge(z_stored[q], 16 * (TILES // 2))
            act.wait_ge(rt, 1)
            act.activation(RW[2][:, :], RW[1][:, :], ACT.Exp).then_inc(exp_done, 1)
            act.wait_ge(exp_done, 1)
            act.activation(RW[3][:, :], RW[2][:, :], ACT.Ln, bias=1.0).then_inc(ln_done, 1)
            act.wait_ge(rt, 10)
            act.activation(RW[5][:, :], RW[1][:, :], ACT.Sqrt).then_inc(sqrt_done, 1)

            def block_silu(m):
                act.wait_ge(gu_done, m * 3 + 3)
                after(act, h_done, m * 2)
                act.activation(GA[0:IA, 0, :], B[0][0:IA, :], ACT.Silu).then_inc(silu_done, 1)
                act.activation(UA[0:IA, 0, :], B[1][0:IA, :], ACT.Copy).then_inc(silu_done, 1)
                act.activation(GA[0:IB, 1, :], B[2][0:IB, :], ACT.Silu).then_inc(silu_done, 1)
                act.activation(UA[0:IB, 1, :], B[2][IB:2 * IB, :], ACT.Copy).then_inc(silu_done, 1)

            def block_dn(m):
                act.wait_ge(dn_done, m + 1)
                after(act, res_done, m * 2)
                for k in range(2):
                    act.activation(DS[:, 0, k, :], B[3 + k][:, :], ACT.Copy).then_inc(dn_copied, 1)

            block_silu(0)
            block_silu(1)
            block_dn(0)
            with act.Fori(0, BLOCKS // 2 - 1) as n:
                for k in range(2):
                    block_silu(n * 2 + (2 + k))
                    block_dn(n * 2 + (1 + k))
            block_dn(BLOCKS - 1)

            with act.Fori(0, E // WRING) as n:
                for r in range(WRING):
                    q = r % 2
                    act.wait_ge(ge_done, n * WRING + (r + 1))
                    act.activation(SE[0:IA, q, 0, :], B[2 + q][0:IA, 0:P], ACT.Silu).then_inc(se_done, 1)
                    act.activation(SE[0:IB, q, 1, :], B[2 + q][0:IB, 2 * P:3 * P], ACT.Silu).then_inc(se_done, 1)

        @block.tensor
        def _(pe):
            pe.wait_ge(rope_in, 80)

            def body(t, p, i2):
                if active(t, 0):
                    u, q = t, p
                    pe.wait_ge(swap_done, (u + 1) * 2)
                    pe.wait_ge(khat_done, (u + 1) * 3)
                    after(pe, roped, u * 2)
                    for v, bank in ((0, plain_ps), (1, swap_ps)):
                        for nl in range(NL):
                            pe.transpose(bank[:, nl * P:(nl + 1) * P], XH[:, q, v, nl * P:(nl + 1) * P], ident[:, :])
                        last = pe.transpose(bank[:, 2 * P:3 * P], KH[:, q, v, :], ident[:, :])
                    last.then_inc(qk_transposed, 1)
                def score(nh):
                    u, q = t - 2, p
                    rows = slice(nh * S, (nh + 1) * S)
                    for b in range(2):
                        for gp in range(2):
                            col = (b * 2 + gp) * P
                            pe.matmul(sc_ps[nh][:, col:col + P], KBD[rows, q, b, gp * P:(gp + 1) * P],
                                      QKT[rows, q, 0:NL, b * S:(b + 1) * S], start=(b == 0 and gp == 0), stop=False,
                                      skip_group_check=True)

                if active(t, 2):
                    after(pe, probs_done, t - 2)
                    score(0)
                if (active(t, 7) or active(t, 2)) and active(t, 5):
                    after(pe, x1_done, t - 4)
                if active(t, 7):
                    u, q = t - 7, (p + 1) % 2
                    pe.wait_ge(z_done, u + 1)
                    for c in range(2):
                        last = pe.transpose(mix_ps[:, c * P:(c + 1) * P], Z[:, q, c * P:(c + 1) * P], ident[:, :])
                    last.then_inc(z_transposed, 1)
                if active(t, 2):
                    u, q = t - 2, p
                    pe.wait_ge(max_done, u + 1)
                    pe.transpose(mixb[0:16, 0:P], MX[:, q, :], identb[:, :]).then_inc(max_transposed, 1)
                if active(t, 2):
                    score(1)
                    pe.wait_ge(mm_done, t - 1)
                    for nh in range(NH):
                        for b in range(2):
                            for gp in range(2):
                                col = (b * 2 + gp) * P
                                last = pe.matmul(sc_ps[nh][:, col:col + P], pick[:, (nh * 2 + b) * 2 + gp, :], MM[:, p, :],
                                                 start=False, stop=True, skip_group_check=True)
                    last.then_inc(scored, 1)
                if active(t, 1):
                    u, q = t - 1, (p + 1) % 2
                    if isinstance(t, int) and u == 0:
                        pe.wait_ge(const_b, 16)
                    pe.wait_ge(ka_done, u + 1)
                    pe.wait_ge(qa_done, (u + 1) * 2)
                    after(pe, max_done, u)
                    for nh in range(NH):
                        for b in range(2):
                            last = pe.matmul(max_ps[nh][:, b * 256:(b + 1) * 256], QA[:, q, nh, b, :], KA[:, q, b, :],
                                             start=True, stop=True)
                    last.then_inc(max_scored, 1)
                if active(t, 3):
                    u, q = t - 3, (p + 1) % 2
                    pe.wait_ge(probs_done, u + 1)
                    if isinstance(u, int):
                        pe.wait_ge(v_in[q], 64 * (u // 2 + 1))
                    else:
                        pe.wait_ge(v_in[q], (i2 * 2 - 3 + p - q) * 32 + 64)
                    after(pe, ot_done, u)
                    for nh in range(NH):
                        for gp in range(2):
                            r0 = 32 * (2 * nh + gp)
                            for b in range(2):
                                probs = PT[:, q, nh, b, gp, :]
                                pe.matmul(pv_ps[r0:r0 + 32, b * P:(b + 1) * P],
                                          VBD[:, q, b, gp, :, :].rearrange("p a b -> p (a b)"), probs, start=True, stop=True)
                                last = pe.matmul(pv_ps[r0:r0 + 32, (2 + b) * P:(3 + b) * P], attc[:, 512:544], probs,
                                                 start=True, stop=True)
                    last.then_inc(pv_done, 1)
                if active(t, 4):
                    u, q = t - 4, p
                    if isinstance(t, int) and u == 0:
                        pe.wait_ge(wout_in, 16)
                    pe.wait_ge(ot_done, u + 1)
                    if active(t, 2):
                        pe.wait_ge(mm_done, t - 1)
                    if active(t, 7):
                        pe.wait_ge(zt_done, t - 6)
                    if active(t, 5):
                        pe.wait_ge(x1_done, t - 4)
                    for nl in range(NL):
                        last = pe.matmul(mix_ps[:, 0:D], OT[:, q, nl, :, :].rearrange("p a b -> p (a b)"), WO[:, nl, :],
                                         start=(nl == 0), stop=(nl == NL - 1))
                    last.then_inc(projected, 1)

            pipeline(pe, body)

            pe.wait_ge(ws_in, 64)
            pe.wait_ge(zt_done, TILES)
            pe.wait_ge(zero_done, 2)
            for k in range(2):
                for c in range(2):
                    for j in range(4):
                        n = k * 4 + j
                        last = pe.matmul(B[5 + k][32 * j:32 * j + 32, :], GW[:, c, :], ZT[:, c, n * 512:(n + 1) * 512],
                                         start=(c == 0), stop=(c == 1), skip_group_check=True)
                last.then_inc(lg_done, 1)
            for k in range(2):
                pe.wait_ge(ls_done, k + 1)
                for c in range(4):
                    last = pe.transpose(B[3 + k][:, c * P:(c + 1) * P], LS[:, k, c * P:(c + 1) * P], ident[:, :])
                last.then_inc(lt_done, 1)

            def block_gu(m, q):
                after(pe, silu_done, m * 4)
                cols = slice(m * 512, (m + 1) * 512) if isinstance(m, int) else bass.ds(m * 512, 512)
                for bank, lo, hi in ((0, 0, IA), (1, IA, 2 * IA), (2, 2 * IA, I2)):
                    for c in range(2):
                        last = pe.matmul(B[bank][0:hi - lo, :], WS13[:, c, lo:hi], ZT[:, c, cols], start=(c == 0), stop=(c == 1))
                    last.then_inc(gu_done, 1)

            def block_down(m, q):
                pe.wait_ge(h_done, m * 2 + 2)
                after(pe, dn_copied, m * 2)
                for j in range(4):
                    o = B[3 + j // 2][:, (j % 2) * D:(j % 2 + 1) * D]
                    pe.matmul(o, H[0:IA, q, 0, j * P:(j + 1) * P], WS2[0:IA, 0, :], start=True, stop=False)
                    last = pe.matmul(o, H[0:IB, q, 1, j * P:(j + 1) * P], WS2[0:IB, 1, :], start=False, stop=True)
                last.then_inc(dn_done, 1)

            block_gu(0, 0)
            pe.wait_ge(l_done, 2)
            block_gu(1, 1)
            block_down(0, 0)
            for m in (2, 3):
                block_gu(m, m % 2)
                block_down(m - 1, 1 - m % 2)
            pe.wait_ge(mask_done, 3)
            pe.matmul(B[5][:, :], trib[:, :], MB[:, :], start=True, stop=False, skip_group_check=True)
            for i in range(TILES - 1):
                later = B[5][:, (i + 1) * E:TILES * E].rearrange("p (n e) -> p n e", e=E)
                rep = MB[:, i * E:(i + 1) * E].unsqueeze(1).to_broadcast([P, TILES - 1 - i, E])
                pe.matmul(later, onesb[:, :], rep, start=False, stop=(i == TILES - 2), skip_group_check=True)
            pe.matmul(B[6][:, :], onesb[:, :], MB[:, :], start=True, stop=True).then_inc(prefix_done, 1)
            for m in (4, 5):
                block_gu(m, m % 2)
                block_down(m - 1, 1 - m % 2)
            for c in range(4):
                pe.wait_ge(hot_done, c + 1)
                for i in range(HT):
                    for h in range(2):
                        last = pe.matmul(B[7][:, h * P:(h + 1) * P],
                                         OA[:, c % 2, i * E + h * 8:i * E + h * 8 + 8, :].rearrange("p e a -> p (e a)"),
                                         OBV[:, c % 2, :, i * E + h * 8:i * E + h * 8 + 8, :].rearrange("p v e b -> p v (e b)"),
                                         start=(c == 0 and i == 0 and h == 0), stop=(c == 3 and i == HT - 1), skip_group_check=True)
                last.then_inc(dispatched, 1)
            for m in (6, 7):
                block_gu(m, m % 2)
                block_down(m - 1, 1 - m % 2)
                if m == 6:
                    pe.wait_ge(lay_done, 1)
                    for hv in range(4):
                        h, v = hv // 2, hv % 2
                        last = pe.matmul(B[6][:, v * E + h * 8:v * E + h * 8 + 8], lay[:, hv, :, :].rearrange("p b a -> p (b a)"),
                                         rc[:, RC["blk"]:RC["blk"] + 8], start=True, stop=True)
                    last.then_inc(listed, 1)
            block_down(BLOCKS - 1, 1)

            def expert_t(n, r):
                q = r % 2
                pe.wait_ge(xg_in[r], n * 16 + 16)
                e = n * WRING + r
                after(pe, xe_done, e - 1)
                for c in range(2):
                    last = pe.transpose(B[q][:, c * P:(c + 1) * P], XG[:, r, c * P:(c + 1) * P], ident[:, :])
                last.then_inc(xe_t, 1)

            def expert_gu(n, r):
                q = r % 2
                e = n * WRING + r
                pe.wait_ge(w_in[r], n * 48 + 48)
                pe.wait_ge(xe_done, e + 1)
                after(pe, he_done, (e - 1) * 2)
                for k, (lo, hi) in enumerate(((0, IA), (IA, 2 * IA), (2 * IA, I2))):
                    for c in range(2):
                        last = pe.matmul(B[2 + q][0:hi - lo, k * P:(k + 1) * P], W13[:, r, c, lo:hi], XE[:, q, c, :],
                                         start=(c == 0), stop=(c == 1))
                last.then_inc(ge_done, 1)

            def expert_down(n, r):
                q = r % 2
                e = n * WRING + r
                pe.wait_ge(he_done, e * 2 + 2)
                after(pe, ye_done, e - 1)
                pe.matmul(B[4 + q][:, 0:D], HE[0:IA, q, 0, :], W2[0:IA, r, 0, :], start=True, stop=False)
                pe.matmul(B[4 + q][:, 0:D], HE[0:IB, q, 1, :], W2[0:IB, r, 1, :], start=False, stop=True).then_inc(ye_ps, 1)

            def experts(n):
                for r in range(WRING):
                    if r < WRING - 1:
                        expert_t(n, r + 1)
                    else:
                        expert_t(n + 1, 0) if not (isinstance(n, int) and n == E // WRING - 1) else None
                    expert_gu(n, r)
                    if r > 0:
                        expert_down(n, r - 1)
                    elif not (isinstance(n, int) and n == 0):
                        expert_down(n - 1, WRING - 1)

            pe.wait_ge(dn_copied, 2 * BLOCKS)
            pe.wait_ge(lists_done, 2)
            expert_t(0, 0)
            experts(0)
            with pe.Fori(1, E // WRING - 1) as n:
                experts(n)
            experts(E // WRING - 1)
            expert_down(E // WRING - 1, WRING - 1)

        @block.vector
        def _(dve):
            dve.wait_ge(rope_in, 80)
            for v in range(2):
                for nl in range(NL):
                    dve.tensor_scalar(ropet[:, v, nl, :], ropec[:, v, :], wqn[:, v, nl:nl + 1], HD ** -0.5, ALU.mult, ALU.mult).then_inc(tables, 1)
                dve.tensor_scalar(ropet[:, v, NL, :], ropec[:, v, :], wkn[:, v:v + 1], None, ALU.mult).then_inc(tables, 1)
            dve.memset(negmean[:, :, :], 0.0).then_inc(tables, 1)
            dve.wait_ge(tables, 7)

            def body(t, p, i2):
                rolled = not isinstance(t, int)
                q = (p + 1) % 2

                def stats_ready():
                    if active(t, -2):
                        dve.wait_ge(stats_done, (t + 3) * 2)
                    if active(t, 6):
                        dve.wait_ge(z_stats, t - 5)

                if active(t, -2):
                    x_loaded(dve, t, -2)
                    dve.bn_stats(stats[:, q, 0, :], X[:, t + 2, :]).then_inc(stats_done, 1)
                    dve.bn_stats(stats[:, q, 1, :], C[:, t + 2, :]).then_inc(stats_done, 1)
                if active(t, 5):
                    u = t - 5
                    dve.wait_ge(projected, u + 1)
                    dve.tensor_tensor(X[:, u, :], X[:, u, :], mix_ps[:, 0:D], ALU.add).then_inc(x1_done, 1)
                if rolled:
                    stats_ready()
                if active(t, 1):
                    key_blocks(dve, t - 1, q, 0)
                if not rolled:
                    stats_ready()
                if active(t, -2):
                    for k in range(2):
                        dve.bn_aggr(mv[:, q, k, :], stats[:, q, k, :]).then_inc(aggr_done, 1)
                if active(t, 6):
                    dve.bn_aggr(mv[:, q, 2, :], stats[:, p, 2, :]).then_inc(z_aggr, 1)
                if active(t, 4):
                    u = t - 4
                    dve.wait_ge(rsum_done, u + 1)
                    after(dve, projected, u - 1)
                    if rolled:
                        dve.wait_ge(x1_done, t - 4)
                    dve.tensor_tensor(OT[:, p, :, :, :].rearrange("p nl b s -> p b nl s"),
                                      pv_ps[:, 0:2 * P].rearrange("p (b nl s) -> p b nl s", b=2, nl=NL),
                                      rsum[:, :].rearrange("p (b nl s) -> p b nl s", b=2, nl=NL), ALU.mult).then_inc(ot_done, 1)
                if active(t, -2):
                    dve.wait_ge(aggr_done, (t + 3) * 2)
                    after(dve, shift_done, t + 1)
                    dve.tensor_scalar(veps[:, q:q + 1], mv[:, q, 1, 1:2], RMS_EPS, None, ALU.add).then_inc(veps_done, 1)
                    dve.tensor_scalar(var_in[:, q, 0:1], mv[:, q, 0, 1:2], 1.0 + RMS_EPS, LN_EPS * RMS_EPS, ALU.mult, ALU.add).then_inc(var_done, 1)
                    dve.tensor_scalar(negmean[:, q, 0:1], mv[:, q, 0, 0:1], -1.0, None, ALU.mult).then_inc(var_done, 1)
                if active(t, 6):
                    dve.wait_ge(z_aggr, t - 5)
                    after(dve, shift_done, t + 1)
                    dve.tensor_scalar(var_in[:, q, 2:3], mv[:, q, 2, 1:2], LN_EPS, None, ALU.add).then_inc(z_var, 1)
                    dve.tensor_scalar(negmean[:, q, 2:3], mv[:, q, 2, 0:1], -1.0, None, ALU.mult).then_inc(z_var, 1)
                if active(t, -2):
                    dve.wait_ge(veps_done, t + 3)
                    dve.scalar_tensor_tensor(out=var_in[:, q, 1:2], in0=mv[:, q, 1, 0:1], scalar=mv[:, q, 1, 0:1],
                                             in1=veps[:, q:q + 1], op0=ALU.mult, op1=ALU.add).then_inc(var_done, 1)
                if active(t, 5):
                    if not rolled:
                        dve.wait_ge(x1_done, t - 4)
                    dve.bn_stats(stats[:, q, 2, :], X[:, t - 5, :]).then_inc(z_stats, 1)
                if active(t, 0):
                    u, q = t, p
                    dve.wait_ge(qk_transposed, u + 1)
                    after(dve, qkt_done, u)
                    for v, bank in ((0, plain_ps), (1, swap_ps)):
                        dve.tensor_tensor(rp[:, v, :], bank[:, 0:3 * P], ropet[:, v, :, :].rearrange("p a b -> p (a b)"), ALU.mult).then_inc(roped, 1)
                if active(t, -1):
                    u, q = t + 1, (p + 1) % 2
                    dve.wait_ge(rstd_done, u + 1)
                    cv = C[:, u, :].unsqueeze(1).to_broadcast([P, 2, KV])
                    dve.tensor_scalar(KH[:, q, 0, :].rearrange("p (a c) -> p a c", a=2), cv, rstd[:, p, 1:2], None, ALU.mult).then_inc(khat_done, 1)
                    cs = C[:, u, :].rearrange("p (g h d) -> p g h d", h=2, d=8)
                    ks = KH[:, q, 1, :].rearrange("p (a g h d) -> p a g h d", a=2, h=2, d=8)
                    for h in range(2):
                        dve.tensor_scalar(ks[:, :, :, 1 - h, :], cs[:, :, h, :].unsqueeze(1).to_broadcast([P, 2, G, 8]),
                                          rstd[:, p, 1:2], None, ALU.mult).then_inc(khat_done, 1)
                if active(t, 1):
                    u, q = t - 1, (p + 1) % 2
                    dve.wait_ge(max_scored, u + 1)
                    after(dve, max_transposed, u - 1)
                    dve.tensor_reduce(MX[:, q, :], PS[:, 2:4, :].rearrange("p n (a k) -> p (n a) k", k=S), AX.X, ALU.max).then_inc(max_done, 1)

            pipeline(dve, body)

            N = TILES * E
            step = [0]

            def link(ins):
                step[0] += 1
                ins.then_inc(rt, 1)
                dve.wait_ge(rt, step[0])

            def rcc(name, n):
                return rc[:, RC[name]:RC[name] + n]

            def te(ap):
                return ap.rearrange("p (n e) -> p n e", e=E)

            def per_tile(ap):
                return ap.unsqueeze(2).to_broadcast([P, TILES, E])

            def per_expert(ap):
                return ap.unsqueeze(1).to_broadcast([P, TILES, E])

            for k in range(2):
                dve.wait_ge(z_stored[k], 16 * (TILES // 2))
            for k in range(2):
                dve.wait_ge(lg_done, k + 1)
                dve.tensor_copy(LS[:, k, :], B[5 + k][:, :]).then_inc(ls_done, 1)
            L = RW[0]
            for k in range(2):
                dve.wait_ge(lt_done, k + 1)
                dve.tensor_copy(L[:, k * 256:(k + 1) * 256].rearrange("p (j c e) -> p j c e", j=4, c=4),
                                B[3 + k][:, :].rearrange("p (c j e) -> p j c e", c=4, j=4)[:, :, :, 0:E]).then_inc(l_done, 1)
            dve.wait_ge(l_done, 2)
            dve.wait_ge(rc_in, 32)
            link(dve.scalar_tensor_tensor(out=RW[1][:, :], in0=L[:, :], scalar=-1.0, in1=L[:, :], op0=ALU.mult, op1=ALU.min))
            ex, lg, sr = RW[2], RW[3], RW[4]
            dve.wait_ge(exp_done, 1)
            link(dve.tensor_scalar(sr[:, :], ex[:, :], 1.0 / 5, None, ALU.mult))
            for c in (-1.0 / 4, 1.0 / 3, -1.0 / 2, 1.0):
                link(dve.scalar_tensor_tensor(out=sr[:, :], in0=sr[:, :], scalar=c, in1=ex[:, :], op0=ALU.add, op1=ALU.mult))
            dve.wait_ge(ln_done, 1)
            link(dve.tensor_tensor(sr[:, :], sr[:, :], lg[:, :], ALU.subtract))
            link(dve.scalar_tensor_tensor(out=sr[:, :], in0=ex[:, :], scalar=1.0 / 16, in1=sr[:, :], op0=ALU.is_lt, op1=ALU.mult))
            link(dve.tensor_tensor(lg[:, :], lg[:, :], sr[:, :], ALU.add))
            link(dve.scalar_tensor_tensor(out=RW[1][:, :], in0=L[:, :], scalar=0.0, in1=lg[:, :], op0=ALU.max, op1=ALU.add))
            assert step[0] == 10
            dve.wait_ge(sqrt_done, 1)
            sc, key, hot1, hot2 = RW[5], RW[0], RW[1], RW[2]
            link(dve.tensor_tensor(te(key[:, :]), te(sc[:, :]), per_expert(GB[:, :]), ALU.add))
            for n, hot in enumerate((hot1, hot2)):
                if n:
                    link(dve.scalar_tensor_tensor(out=key[:, :], in0=hot1[:, :], scalar=-3e38, in1=key[:, :], op0=ALU.mult, op1=ALU.add))
                link(dve.tensor_reduce(RS[0][:, :], te(key[:, :]), AX.X, ALU.max))
                link(dve.tensor_tensor(te(hot[:, :]), te(key[:, :]), per_tile(RS[0][:, :]), ALU.is_equal))
                link(dve.tensor_tensor(te(hot[:, :]), te(hot[:, :]), per_expert(rcc("desc", E)), ALU.mult))
                link(dve.tensor_reduce(RS[0][:, :], te(hot[:, :]), AX.X, ALU.max))
                link(dve.tensor_tensor(te(hot[:, :]), te(hot[:, :]), per_tile(RS[0][:, :]), ALU.is_equal))
            M = RW[3]
            link(dve.tensor_tensor(M[:, :], hot1[:, :], hot2[:, :], ALU.add))
            dve.tensor_copy(MB[:, :], M[:, :]).then_inc(mask_done, 1)
            dve.tensor_copy(trib[:, :], rcc("tri", P)).then_inc(mask_done, 1)
            dve.memset(onesb[:, :], 1.0).then_inc(mask_done, 1)
            wd = RW[5]
            link(dve.tensor_tensor(wd[:, :], sc[:, :], M[:, :], ALU.mult))
            link(dve.tensor_reduce(RS[1][:, :], te(wd[:, :]), AX.X, ALU.add))
            link(dve.reciprocal(RS[1][:, :], RS[1][:, :]))
            link(dve.tensor_tensor(te(wd[:, :]), te(wd[:, :]), per_tile(RS[1][:, :]), ALU.mult))
            no = RW[0]
            link(dve.tensor_scalar(no[:, :], M[:, :], -1.0, 1.0, ALU.mult, ALU.add))
            off, low, place = RW[1], RW[2], RW[4]
            link(dve.tensor_tensor(te(off[:, :]), te(no[:, :]), per_tile(rcc("rev", TILES)), ALU.mult))
            dve.wait_ge(prefix_done, 1)
            link(dve.tensor_reduce(cnt[:, :], B[6][:, :].rearrange("p (n e) -> p e n", e=E), AX.X, ALU.add))
            link(dve.tensor_tensor(te(low[:, :]), te(no[:, :]), per_expert(cnt[:, :]), ALU.mult))
            link(dve.tensor_tensor(place[:, :], B[5][:, :], off[:, :], ALU.add))
            link(dve.tensor_tensor(low[:, :], place[:, :], low[:, :], ALU.is_lt))
            link(dve.scalar_tensor_tensor(out=place[:, :], in0=low[:, :], scalar=FAR, in1=place[:, :], op0=ALU.mult, op1=ALU.add))
            link(dve.tensor_copy(slot_i[:, :], place[:, :]))
            link(dve.tensor_scalar(ab_i[:, 0, :], slot_i[:, :], 3, None, ALU.logical_shift_right))
            link(dve.tensor_scalar(ab_i[:, 1, :], slot_i[:, :], 7, None, ALU.bitwise_and))
            hi, lo = RW[0], RW[1]
            link(dve.tensor_copy(hi[:, :], ab_i[:, 0, :]))
            link(dve.tensor_copy(lo[:, :], ab_i[:, 1, :]))
            HN = HT * E
            for c in range(4):
                s = slice(c * HN, (c + 1) * HN)
                if c >= 2:
                    dve.wait_ge(dispatched, c - 1)
                dve.tensor_tensor(OA[:, c % 2, :, :], hi[:, s].unsqueeze(2).to_broadcast([P, HN, 16]),
                                  rcc("ia", 16).unsqueeze(1).to_broadcast([P, HN, 16]), ALU.is_equal)
                link(dve.tensor_tensor(OBE[:, :, :], lo[:, s].unsqueeze(2).to_broadcast([P, HN, 8]),
                                       rcc("ib", 8).unsqueeze(1).to_broadcast([P, HN, 8]), ALU.is_equal))
                dve.tensor_tensor(OBV[:, c % 2, 0, :, :].rearrange("p (n e) b -> p n (e b)", e=E),
                                  OBE[:, :, :].rearrange("p (n e) b -> p n (e b)", e=E),
                                  rc[:, RC["tok"] + c * HT:RC["tok"] + (c + 1) * HT].unsqueeze(2).to_broadcast([P, HT, E * 8]), ALU.mult)
                dve.tensor_tensor(OBV[:, c % 2, 1, :, :], OBE[:, :, :], wd[:, s].unsqueeze(2).to_broadcast([P, HN, 8]), ALU.mult).then_inc(hot_done, 1)
                dve.wait_ge(hot_done, c + 1)
            dve.wait_ge(dispatched, 4)
            for h in range(2):
                ins = dve.tensor_tensor(dg[:, 2 * h:2 * h + 2, :, :], B[7][:, h * P:(h + 1) * P].rearrange("p (v e b) -> p v e b", v=2, e=8),
                                        rcc("blk", 8).unsqueeze(1).unsqueeze(3).to_broadcast([P, 2, 8, 8]), ALU.mult)
            link(ins)
            link(dve.tensor_reduce(dr[:, :, :], dg[:, :, :, :].rearrange("p a e b -> p a b e"), AX.X, ALU.add))
            dve.tensor_tensor(lay[:, :, :, :].rearrange("p v b a -> p (v b) a"),
                              dr[:, :, :].rearrange("p v b -> p (v b)").unsqueeze(2).to_broadcast([P, 32, 16]),
                              rcc("sel", 16).unsqueeze(1).to_broadcast([P, 32, 16]), ALU.mult).then_inc(lay_done, 1)
            dve.wait_ge(listed, 1)
            dve.tensor_copy(idx[:, :], B[6][:, 0:E]).then_inc(lists_done, 1)
            dve.tensor_copy(wslot[:, :], B[6][:, E:2 * E]).then_inc(lists_done, 1)
            dve.wait_ge(lists_done, 2)

            def xe(e, r):
                q = r % 2
                dve.wait_ge(xe_t, e + 1)
                after(dve, ge_done, e - 1)
                dve.tensor_copy(XE[:, q, :, :].rearrange("p a b -> p (a b)"), B[q][:, 0:2 * P]).then_inc(xe_done, 1)

            def he(e, r):
                q = r % 2
                dve.wait_ge(se_done, e * 2 + 2)
                after(dve, ye_ps, e - 1)
                dve.tensor_tensor(HE[0:IA, q, 0, :], B[2 + q][0:IA, P:2 * P], SE[0:IA, q, 0, :], ALU.mult).then_inc(he_done, 1)
                dve.tensor_tensor(HE[0:IB, q, 1, :], B[2 + q][IB:2 * IB, 2 * P:3 * P], SE[0:IB, q, 1, :], ALU.mult).then_inc(he_done, 1)

            def ye(e, r):
                q = r % 2
                dve.wait_ge(ye_ps, e + 1)
                after(dve, added, (e - WRING + 1) * 16)
                dve.tensor_scalar(YE[:, r, :], B[4 + q][:, 0:D], wslot[:, bass.ds(e, 1)] if not isinstance(e, int) else wslot[:, e:e + 1], None, ALU.mult).then_inc(ye_done, 1)

            def experts(n, first=False, last=False):
                for r in range(WRING):
                    e = n * WRING + r
                    if not (last and r == WRING - 1):
                        xe(e + 1, (r + 1) % WRING)
                    he(e, r)
                    if not (first and r == 0):
                        ye(e - 1, (r - 1) % WRING)

            xe(0, 0)
            experts(0, first=True)
            with dve.Fori(1, E // WRING - 1) as n:
                experts(n)
            experts(E // WRING - 1, last=True)
            ye(E - 1, WRING - 1)


_INS = ["x", "ctx", "wq_norm", "wk_norm", "w_out", "gate_w", "gate_b", "w13", "w2", "ws13", "ws2",
        "const_rope", "const_attn", "const_pick", "const_route"]


def _constants(np):
    p = np.arange(128)
    pos = np.arange(64)
    inv = (np.float32(1.0) / np.float32(10000.0) ** (np.arange(0, 16, 2, dtype=np.float32) / np.float32(16))).astype(np.float32)
    ang = np.outer(inv[p % 8], np.tile(pos, 2).astype(np.float32)).astype(np.float32)
    sign = np.where(p % 16 < 8, -1.0, 1.0)[:, None]
    kmask = (p[:, None] % 64 // 16 == np.arange(4)[None, :])
    rope = np.concatenate([np.eye(128), np.cos(ang), np.sin(ang) * sign, kmask], 1)

    attn = np.zeros((128, 544))
    j = np.arange(64)[:, None]
    attn[64:, 0:256] = np.tile(np.where(pos[None, :] > j, -1e30, 0.0), (1, 4))
    attn[64:, 256:384] = np.tile(np.eye(64), (1, 2))
    attn[:64, 384:512] = np.tile(np.where(j > pos[None, :], -1e30, 0.0), (1, 2))
    attn[:, 512:544] = p[:, None] // 64 == np.arange(32)[None, :] // 16

    pick = np.zeros((80, 8, 2, 64))
    pick[:64] = np.eye(64)[:, None, None, :]
    for blk in range(8):
        nb, gp = blk // 2, blk % 2
        for g2 in range(2):
            pick[64 + nb * 4 + gp * 2 + g2, blk, g2, :] = 1.0

    route = np.zeros((128, 256))
    tok = np.arange(32)[None, :] * 128 + p[:, None]
    route[:, RC["desc"]:RC["desc"] + 16] = 16 - np.arange(16)
    route[:, RC["tri"]:RC["tri"] + 128] = p[:, None] < p[None, :]
    route[:, RC["ia"]:RC["ia"] + 16] = np.arange(16)
    route[:, RC["ib"]:RC["ib"] + 8] = np.arange(8)
    route[:, RC["rev"]:RC["rev"] + 32] = 127 - tok
    route[:, RC["tok"]:RC["tok"] + 32] = tok
    route[:, RC["blk"]:RC["blk"] + 8] = p[:, None] // 16 == np.arange(8)[None, :]
    route[:, RC["sel"]:RC["sel"] + 16] = p[:, None] % 16 == np.arange(16)[None, :]
    return {"const_rope": rope, "const_attn": attn, "const_pick": pick.reshape(80, 1024), "const_route": route}


def kernel(**inputs):
    import numpy as np
    import concourse.bacc as bacc
    from concourse.bass_utils import run_bass_kernel_spmd

    a = {k: np.asarray(v) for k, v in inputs.items()}
    order = np.arange(256).reshape(4, 2, 2, 16).transpose(2, 1, 0, 3).reshape(-1)
    swap = order.reshape(-1, 2, 8)[:, ::-1].reshape(-1)
    kv = np.arange(64)
    kvswap = kv.reshape(-1, 2, 8)[:, ::-1].reshape(-1)

    def rows(w):
        return w[order].reshape(2, 128, -1).transpose(1, 0, 2)

    def gate_up(w1, w3):
        return rows(np.concatenate([w1[:112], w3[:112], w1[112:], w3[112:]], 0).T)

    wq, wk = a["L0_xattn_q_norm_w"], a["L0_xattn_k_norm_w"]
    arrays = {
        "x": a["x"].reshape(4096, 256)[:, order],
        "ctx": a["ctx_512"].reshape(4096, 64),
        "wq_norm": np.stack([wq[order].reshape(2, 128), wq[swap].reshape(2, 128)]).transpose(2, 0, 1),
        "wk_norm": np.stack([np.tile(wk[kv], 2), np.tile(wk[kvswap], 2)], 1),
        "w_out": rows(a["L0_xattn_w_out"].T[:, order]),
        "gate_w": rows(a["L0_ffn_gate_w"].T),
        "gate_b": a["L0_ffn_gate_b"].reshape(1, 16),
        "w13": np.stack([gate_up(a["L0_ffn_W1"][e], a["L0_ffn_W3"][e]) for e in range(16)]),
        "w2": a["L0_ffn_W2"].transpose(0, 2, 1)[:, :, order],
        "ws13": gate_up(a["L0_ffn_Ws1"], a["L0_ffn_Ws3"]),
        "ws2": a["L0_ffn_Ws2"].T[:, order],
    }
    arrays.update({k: v.astype(np.float32) for k, v in _constants(np).items()})

    nc = bacc.Bacc("TRN2", target_bir_lowering=False, num_devices=1)
    feed, args = {}, []
    for name in _INS:
        v = np.ascontiguousarray(arrays[name])
        feed[name] = v
        args.append(nc.dram_tensor(name, v.shape, mybir.dt.from_np(v.dtype), kind="ExternalInput").ap())
    args.append(nc.dram_tensor("out", (4096, 256), mybir.dt.float32, kind="ExternalOutput").ap())
    xattn_moe_kernel(nc, *args)
    r = run_bass_kernel_spmd(nc, [feed], core_ids=[0])
    y = r.results[0]["out"]
    return y.reshape(64, 64, 2, 2, 4, 16).transpose(0, 1, 4, 3, 2, 5).reshape(64, 64, 256)
```

```python
import concourse.bass as bass
from concourse import mybir
from contextlib import ExitStack


RC = {"desc": 0, "tri": 16, "ia": 144, "ib": 160, "rev": 168, "tile": 200, "pos": 232, "blk": 240, "sel": 248}


def xattn_moe_kernel(
    nc: bass.Bass,
    x: bass.AP,
    ctx: bass.AP,
    wq_norm: bass.AP,
    wk_norm: bass.AP,
    w_out: bass.AP,
    gate_w: bass.AP,
    gate_b: bass.AP,
    w13: bass.AP,
    w2: bass.AP,
    ws13: bass.AP,
    ws2: bass.AP,
    const_rope: bass.AP,
    const_attn: bass.AP,
    const_pick: bass.AP,
    const_route: bass.AP,
    out: bass.AP,
):
    f32, bf16, i32 = mybir.dt.float32, mybir.dt.bfloat16, mybir.dt.int32
    ALU = mybir.AluOpType
    ACT = mybir.ActivationFunctionType
    AX = mybir.AxisListType

    P = 128
    TOK, D = x.shape
    TILES = TOK // P
    S = 64
    G, NH, NL, HD = 4, 2, 2, 16
    KV = G * HD
    E = gate_b.shape[-1]
    CAP = 128
    I2 = w13.shape[-1]
    I = I2 // 2
    IA, IB = 112, I - 112
    LN_EPS = 1e-5
    RMS_EPS = 1e-5
    FAR = 8192.0
    BLOCKS = TOK // 512
    LATE = 3
    WRING = 4

    with ExitStack() as ctx_all:
        def keep(stack, name, shape, dt):
            return stack.enter_context(nc.sbuf_tensor(name, shape, dt))

        def sem(name):
            return ctx_all.enter_context(nc.semaphore(name))

        z_rows = nc.dram_tensor("z_rows", [TOK, D], f32).ap()
        X = keep(ctx_all, "X", [P, TILES, D], f32)
        ZT = keep(ctx_all, "ZT", [P, 2, TOK], f32)
        ident = keep(ctx_all, "ident", [P, P], f32)
        GW = keep(ctx_all, "GW", [P, 2, 32], f32)
        WS13 = keep(ctx_all, "WS13", [P, 2, I2], f32)
        WS2 = keep(ctx_all, "WS2", [P, 2, D], f32)
        rc = keep(ctx_all, "rc", [P, const_route.shape[1]], f32)

        at = ExitStack()
        C = keep(at, "C", [P, TILES, KV], f32)
        ropec = keep(at, "ropec", [P, 2, P], f32)
        wqn = keep(at, "wqn", [P, 2, NL], f32)
        wkn = keep(at, "wkn", [P, 2], f32)
        kmask = keep(at, "kmask", [P, G], f32)
        ropet = keep(at, "ropet", [P, 2, 3, P], f32)
        attc = keep(at, "attc", [P, const_attn.shape[1]], f32)
        pickf = keep(at, "pickf", [80, const_pick.shape[1]], f32)
        identb = keep(at, "identb", [P, P], bf16)
        pick = keep(at, "pick", [80, 8, P], bf16)
        WO = keep(at, "WO", [P, NL, D], f32)
        stats = keep(at, "stats", [P, 2, 3, 6], f32)
        mv = keep(at, "mv", [P, 2, 3, 2], f32)
        var_in = keep(at, "var_in", [P, 2, 3], f32)
        negmean = keep(at, "negmean", [P, 2, 3], f32)
        shift = keep(at, "shift", [P, 2, 3], f32)
        zero = keep(at, "zero", [P, 8], f32)
        veps = keep(at, "veps", [P, 2], f32)
        rstd = keep(at, "rstd", [P, 2, 3], f32)
        neghalf = keep(at, "neghalf", [P, 3], f32)
        XH = keep(at, "XH", [P, 2, 2, D], f32)
        KH = keep(at, "KH", [P, 2, 2, P], f32)
        rp = keep(at, "rp", [P, 2, 3 * P], f32)
        QKT = keep(at, "QKT", [P, 2, 3, P], f32)
        KBD = keep(at, "KBD", [P, 2, 2, G * S], f32)
        QA = keep(at, "QA", [P, 2, NH, 2, P], bf16)
        KA = keep(at, "KA", [P, 2, 2, G * S], bf16)
        MX = keep(at, "MX", [P, 2, 16], bf16)
        MM = keep(at, "MM", [80, 2, P], bf16)
        PT = keep(at, "PT", [P, 2, NH, 2, 2, P], f32)
        VBD = keep(at, "VBD", [P, 2, 2, 2, 2, HD], f32)
        logsum = keep(at, "logsum", [P, 2 * P], f32)
        rsum = keep(at, "rsum", [P, 2 * P], f32)
        OT = keep(at, "OT", [P, 2, NL, 2, S], f32)
        Z = keep(at, "Z", [P, 2, D], f32)
        at.close()

        ff = ctx_all.enter_context(ExitStack())
        GA = keep(ff, "GA", [P, 2, 512], f32)
        UA = keep(ff, "UA", [P, 2, 512], f32)
        H = keep(ff, "H", [P, 2, 2, 512], f32)
        DS = keep(ff, "DS", [P, 2, 2, 512], f32)
        OUTB = keep(ff, "OUTB", [P, 2, 2, 512], f32)
        LS = keep(ff, "LS", [P, 2, 512], f32)
        GB = keep(ff, "GB", [P, E], f32)
        RW = [keep(ff, f"RW{i}", [P, TILES * E], f32) for i in range(7)]
        RS = [keep(ff, f"RS{i}", [P, TILES], f32) for i in range(4)]
        MB = keep(ff, "MB", [P, TILES * E], bf16)
        trib = keep(ff, "trib", [P, P], bf16)
        onesb = keep(ff, "onesb", [P, P], bf16)
        cnt = keep(ff, "cnt", [P, E], f32)
        slot_i = keep(ff, "slot_i", [P, TILES * E], i32)
        ab_i = keep(ff, "ab_i", [P, 2, TILES * E], i32)
        HT = TILES // 4
        HN = HT * 2
        NV = 5
        OA = keep(ff, "OA", [P, 2, HN, 16, 8], bf16)
        OBE = keep(ff, "OBE", [P, HN, 8, 8], bf16)
        OBV = keep(ff, "OBV", [P, 2, HN, NV, 64], bf16)
        iat = keep(ff, "iat", [P, 16, 8], bf16)
        ibt = keep(ff, "ibt", [P, 8, 8], bf16)
        hib = keep(ff, "hib", [P, TILES * E], bf16)
        lob = keep(ff, "lob", [P, TILES * E], bf16)
        wv = [keep(ff, f"wv{i}", [P, TILES * E], bf16) for i in range(4)]
        dg = keep(ff, "dg", [P, 2, NV * 8, 8], f32)
        dv = keep(ff, "dv", [P, 2, NV, 8], f32)
        dr = keep(ff, "dr", [P, 4, 8], f32)
        lay = keep(ff, "lay", [P, 4, 8, 16], f32)
        idx = keep(ff, "idx", [P, E], i32)
        wslot = keep(ff, "wslot", [P, E], f32)
        W13 = keep(ff, "W13", [P, WRING, 2, I2], f32)
        W2 = keep(ff, "W2", [P, WRING, 2, D], f32)
        XG = keep(ff, "XG", [P, WRING, D], f32)
        XE = keep(ff, "XE", [P, 2, 2, P], f32)
        SE = keep(ff, "SE", [P, 2, 2, P], f32)
        HE = keep(ff, "HE", [P, 2, 2, P], f32)
        YE = keep(ff, "YE", [P, WRING, D], f32)

        PS = ctx_all.enter_context(nc.psum_tensor("PS", [P, 8, 512], f32))
        B = [PS[:, i, :] for i in range(8)]

        plain_ps, swap_ps, max_ps, sc_ps, pv_ps, mix_ps = B[0], B[1], (B[2], B[3]), (B[4], B[5]), B[6], B[7]
        mixb = mix_ps[:, 256:320].bitcast(bf16)

        x_in = [sem(f"x_in{i}") for i in range(4)]
        rope_in, attc_in, wout_in, ws_in, rc_in = (sem(n) for n in ("rope_in", "attc_in", "wout_in", "ws_in", "rc_in"))
        v_in = [sem(f"v_in{i}") for i in range(2)]
        zero_done, setup_pool = sem("zero_done"), sem("setup_pool")
        const_b, tables = sem("const_b"), sem("tables")
        stats_done, aggr_done, var_done = sem("stats_done"), sem("aggr_done"), sem("var_done")
        veps_done = sem("veps_done")
        rstd_done, xhat_done, khat_done = sem("rstd_done"), sem("xhat_done"), sem("khat_done")
        shift_done, swap_done = sem("shift_done"), sem("swap_done")
        qk_transposed, roped, qkt_done = sem("qk_transposed"), sem("roped"), sem("qkt_done")
        kbd_done = [sem(f"kbd_done{b}") for b in range(2)]
        ka_done, qa_done, max_scored, max_done = sem("ka_done"), sem("qa_done"), sem("max_scored"), sem("max_done")
        max_transposed, mm_done, scored, probs_done = sem("max_transposed"), sem("mm_done"), sem("scored"), sem("probs_done")
        pv_done, log_done, rsum_done, ot_done = sem("pv_done"), sem("log_done"), sem("rsum_done"), sem("ot_done")
        projected, x1_done, z_stats, z_aggr, z_var = sem("projected"), sem("x1_done"), sem("z_stats"), sem("z_aggr"), sem("z_var")
        z_done, z_transposed, zt_done = sem("z_done"), sem("z_transposed"), sem("zt_done")
        z_stored = [sem(f"z_stored{i}") for i in range(2)]

        def after(eng, s, n):
            if not isinstance(n, int) or n > 0:
                eng.wait_ge(s, n)

        FIRST, LOOP0, LOOP1, LAST = -2, 8, 30, TILES + 7
        X_CHUNKS = [(0, 1), (1, 4), (4, 8), (8, TILES)]

        def pipeline(eng, body):
            for t in range(FIRST, LOOP0):
                body(t, t % 2, t // 2)
            with eng.Fori(0, (LOOP1 - LOOP0) // 2) as i:
                for p in range(2):
                    body(i * 2 + (LOOP0 + p), p, i + LOOP0 // 2)
            for t in range(LOOP1, LAST):
                body(t, t % 2, t // 2)

        def active(t, lag):
            return not isinstance(t, int) or 0 <= t - lag < TILES

        def x_loaded(eng, t, lag):
            if isinstance(t, int):
                for c, (lo, _) in enumerate(X_CHUNKS):
                    if t - lag == lo:
                        eng.wait_ge(x_in[c], 32)

        def key_blocks(eng, u, q, b):
            eng.wait_ge(qkt_done, u + 1)
            after(eng, scored, u - 1)
            after(eng, ka_done, u - 1)
            eng.tensor_tensor(KBD[:, q, b, :].rearrange("p (g k) -> p g k", g=G),
                              QKT[:, q, NL, b * S:(b + 1) * S].unsqueeze(1).to_broadcast([P, G, S]),
                              kmask[:, :].unsqueeze(2).to_broadcast([P, G, S]), ALU.mult).then_inc(kbd_done[b], 1)

        xe_ps, ge_ps, ye_bank = (B[6], B[7]), (B[5], B[0]), (B[1], B[2])

        block = ctx_all.enter_context(nc.Block())

        lg_done, ls_done, lt_done, l_done = sem("lg_done"), sem("ls_done"), sem("lt_done"), sem("l_done")
        rt = sem("rt")
        exp_done, ln_done, sqrt_done = sem("exp_done"), sem("ln_done"), sem("sqrt_done")
        mask_done, prefix_done, cnt_done = sem("mask_done"), sem("prefix_done"), sem("cnt_done")
        hot_done, dispatched, lay_done, listed, lists_done = (
            sem("hot_done"), sem("dispatched"), sem("lay_done"), sem("listed"), sem("lists_done"))
        gu_done, silu_done, h_done, dn_done, dn_copied, res_done, late_res_done = (
            sem("gu_done"), sem("silu_done"), sem("h_done"), sem("dn_done"), sem("dn_copied"), sem("res_done"),
            sem("late_res_done"))
        res_stored = [sem(f"res_stored{i}") for i in range(2)]
        late_stored = [sem(f"late_stored{i}") for i in range(LATE)]
        w_in = [sem(f"w_in{i}") for i in range(WRING)]
        xg_in = [sem(f"xg_in{i}") for i in range(WRING)]
        xe_t, xe_done, ge_done, se_done, he_done, ye_ps, ye_done = (
            sem("xe_t"), sem("xe_done"), sem("ge_done"), sem("se_done"), sem("he_done"), sem("ye_ps"), sem("ye_done"))
        added = sem("added")

        ctx_v = ctx.rearrange("(n k) (gp g2 d) -> n k gp g2 d", k=S, gp=2, g2=2)

        @block.sync
        def _(sp):
            x_v = x.rearrange("(n p) c -> p n c", p=P)
            c_v = ctx.rearrange("(n p) c -> p n c", p=P)

            def load_x(c):
                lo, hi = X_CHUNKS[c]
                sp.dma_start(C[:, lo:hi, :], c_v[:, lo:hi, :]).then_inc(x_in[c], 16)
                sp.dma_start(X[:, lo:hi, :], x_v[:, lo:hi, :]).then_inc(x_in[c], 16)

            load_x(0)
            sp.dma_start(ident[:, :], const_rope[:, 0:P]).then_inc(rope_in, 16)
            sp.dma_start(ropec[:, :, :], const_rope[:, P:3 * P].rearrange("p (a b) -> p a b", a=2)).then_inc(rope_in, 16)
            sp.dma_start(kmask[:, :], const_rope[:, 3 * P:3 * P + G]).then_inc(rope_in, 16)
            sp.dma_start(wqn[:, :, :], wq_norm).then_inc(rope_in, 16)
            sp.dma_start(wkn[:, :], wk_norm).then_inc(rope_in, 16)
            load_x(1)
            sp.dma_start(attc[:, :], const_attn).then_inc(attc_in, 16)
            sp.dma_start(pickf[:, :], const_pick).then_inc(attc_in, 16)
            load_x(2)
            sp.dma_start(WO[:, :, :], w_out).then_inc(wout_in, 16)
            load_x(3)
            sp.dma_start(rc[:, :], const_route).then_inc(rc_in, 16)
            sp.dma_start(WS13[:, :, :], ws13).then_inc(ws_in, 16)
            sp.dma_start(WS2[0:IA, 0, :], ws2[0:IA, :]).then_inc(ws_in, 16)
            sp.dma_start(WS2[0:IB, 1, :], ws2[IA:I, :]).then_inc(ws_in, 16)
            sp.dma_start(GW[:, :, 0:E], gate_w).then_inc(ws_in, 16)

            def body(t, p, i2):
                if active(t, 2):
                    u, q = t - 2, p
                    if isinstance(t, int) and t == 2:
                        sp.wait_ge(zero_done, 1)
                    after(sp, pv_done, u - 1)
                    for g2 in range(2):
                        for b in range(2):
                            sp.dma_start(VBD[g2 * S:(g2 + 1) * S, q, b, :, g2, :],
                                         ctx_v[u * 2 + b, :, :, g2, :]).then_inc(v_in[q], 16)
                if active(t, 6):
                    u, q = t - 6, p
                    sp.wait_ge(z_done, u + 1)
                    sp.dma_start(z_rows[bass.ds(u * P, P), :] if not isinstance(u, int) else z_rows[u * P:(u + 1) * P, :],
                                 Z[:, q, :]).then_inc(z_stored[q], 16)

            pipeline(sp, body)
            sp.wait_ge(zt_done, TILES)
            sp.wait_ge(z_stored[0], 16 * (TILES // 2))
            sp.wait_ge(z_stored[1], 16 * (TILES // 2))
            sp.dma_start(GB[:, :], gate_b.to_broadcast([P, E])).then_inc(rc_in, 16)

            def load_w(e, r):
                sp.dma_start(W13[:, r, :, :], w13[e, :, :, :]).then_inc(w_in[r], 16)
                sp.dma_start(W2[0:IA, r, 0, :], w2[e, 0:IA, :]).then_inc(w_in[r], 16)
                sp.dma_start(W2[0:IB, r, 1, :], w2[e, IA:I, :]).then_inc(w_in[r], 16)

            for e in range(WRING):
                load_w(e, e)
            out_v = out.rearrange("(n j p) c -> n p j c", j=2, p=P)

            def store_res(n, k, slot, stored):
                sp.dma_start(out_v[n * 2 + k, :, :, :], OUTB[:, slot, k, :].rearrange("p (j c) -> p j c", j=2)).then_inc(stored, 16)

            with sp.Fori(0, BLOCKS - LATE) as n:
                for k in range(2):
                    sp.wait_ge(res_done, n * 2 + (k + 1))
                    store_res(n, k, 0, res_stored[k])
            for n in range(LATE):
                for k in range(2):
                    sp.wait_ge(late_res_done, n * 2 + (k + 1))
                    store_res(BLOCKS - LATE + n, k, (n + 1) % 2, late_stored[n])
            with sp.Fori(0, E // WRING - 1) as n:
                for r in range(WRING):
                    sp.wait_ge(ye_ps, n * WRING + (r + 1))
                    load_w(n * WRING + (WRING + r), r)

        @block.gpsimd
        def _(pool):
            pool.memset(VBD[:, :, :, :, :, :], 0.0).then_inc(zero_done, 1)
            pool.memset(GW[:, :, E:2 * E], 0.0).then_inc(zero_done, 1)
            pool.memset(neghalf[:, :], -0.5).then_inc(setup_pool, 1)
            pool.memset(zero[:, :], 0.0).then_inc(setup_pool, 1)
            pool.wait_ge(setup_pool, 2)

            def body(t, p, i2):
                if active(t, 1):
                    key_blocks(pool, t - 1, (p + 1) % 2, 1)
                if active(t, -1):
                    u, q = t + 1, (p + 1) % 2
                    pool.wait_ge(xhat_done, u + 1)
                    after(pool, qk_transposed, u - 1)
                    xs = XH[:, q, 0, :].rearrange("p (n h d) -> p n h d", h=2, d=8)
                    hs = XH[:, q, 1, :].rearrange("p (n h d) -> p n h d", h=2, d=8)
                    for h in range(2):
                        pool.tensor_tensor(hs[:, :, 1 - h, :], xs[:, :, h, :], zero[:, :].unsqueeze(1).to_broadcast([P, 16, 8]), ALU.add).then_inc(swap_done, 1)
                lo = 0 if active(t, -2) else 2
                hi = 3 if active(t, 6) else 2
                if lo < hi:
                    q = (p + 1) % 2
                    if lo == 0:
                        pool.wait_ge(var_done, (t + 3) * 3)
                    if hi == 3:
                        pool.wait_ge(z_var, (t - 5) * 2)
                    after(pool, z_done, t - 7)
                    pool.tensor_tensor(rstd[:, q, lo:hi], var_in[:, q, lo:hi], neghalf[:, lo:hi], ALU.pow).then_inc(rstd_done, 1)
                    pool.wait_ge(rstd_done, t + 3)
                    pool.tensor_tensor(shift[:, q, lo:hi], negmean[:, q, lo:hi], rstd[:, q, lo:hi], ALU.mult).then_inc(shift_done, 1)
                if active(t, 0):
                    u, q = t, p
                    pool.wait_ge(roped, (u + 1) * 2)
                    after(pool, scored, u - 1)
                    after(pool, qa_done, (u - 1) * 2)
                    after(pool, kbd_done[0], u - 1)
                    pool.tensor_tensor(QKT[:, q, :, :].rearrange("p a b -> p (a b)"), rp[:, 0, :], rp[:, 1, :], ALU.add).then_inc(qkt_done, 1)
            pipeline(pool, body)

            def block_h(m, q):
                pool.wait_ge(silu_done, m * 4 + 4)
                after(pool, dn_done, m - 1)
                pool.tensor_tensor(H[0:IA, q, 0, :], GA[0:IA, 0, :], UA[0:IA, 0, :], ALU.mult).then_inc(h_done, 1)
                pool.tensor_tensor(H[0:IB, q, 1, :], GA[0:IB, 1, :], UA[0:IB, 1, :], ALU.mult).then_inc(h_done, 1)

            def block_res(m, first):
                for k in range(2):
                    pool.wait_ge(dn_copied, m * 2 + (k + 1))
                    if not first:
                        pool.wait_ge(res_stored[k], m * 16)
                    pool.tensor_tensor(OUTB[:, 0, k, :].rearrange("p (j c) -> p j c", j=2),
                                       DS[:, 0, k, :].rearrange("p (j c) -> p j c", j=2),
                                       X[:, bass.ds(m * 4 + 2 * k, 2), :] if not isinstance(m, int) else X[:, m * 4 + 2 * k:m * 4 + 2 * k + 2, :],
                                       ALU.add).then_inc(res_done, 1)

            pool.wait_ge(zt_done, TILES)
            for k in range(2):
                pool.wait_ge(z_stored[k], 16 * (TILES // 2))
            block_h(0, 0)
            block_h(1, 1)
            block_res(0, True)
            with pool.Fori(0, BLOCKS // 2 - 2) as n:
                for k in range(2):
                    block_h(n * 2 + (2 + k), k)
                    block_res(n * 2 + (1 + k), False)

            def gather(e):
                if e >= WRING:
                    pool.wait_ge(xe_t, e - WRING + 1)
                pool.indirect_dma_start(out=XG[:, e % WRING, :], out_offset=None, in_=z_rows,
                                        in_offset=bass.IndirectOffsetOnAxis(ap=idx[:, e:e + 1], axis=0)).then_inc(xg_in[e % WRING], 16)

            pool.wait_ge(lists_done, 2)
            pool.wait_ge(z_stored[0], 16 * (TILES // 2))
            pool.wait_ge(z_stored[1], 16 * (TILES // 2))
            for e in range(WRING):
                gather(e)
            block_h(BLOCKS - 2, 0)
            block_h(BLOCKS - 1, 1)
            gather(WRING)
            for k in range(2):
                pool.wait_ge(res_stored[k], 16 * (BLOCKS - LATE))
            for n in range(LATE):
                pool.wait_ge(late_stored[n], 32)
            for e in range(E):
                if e and WRING + e < E:
                    gather(WRING + e)
                pool.wait_ge(ye_done, e + 1)
                if e:
                    pool.wait_ge(added, 16 * e)
                pool.indirect_dma_start(out=out, out_offset=bass.IndirectOffsetOnAxis(ap=idx[:, e:e + 1], axis=0),
                                        in_=YE[:, e % WRING, :], in_offset=None, compute_op=ALU.add).then_inc(added, 16)
            pool.wait_ge(added, 16 * E)

        @block.scalar
        def _(act):
            nc.scalar.preload_act_table_set("natural_log_exp_and_others")
            def constants():
                act.wait_ge(rope_in, 80)
                act.activation(identb[:, :], ident[:, :], ACT.Copy).then_inc(const_b, 1)
                act.wait_ge(attc_in, 32)
                act.activation(pick[:, :, :].rearrange("p a b -> p (a b)"), pickf[:, :], ACT.Copy).then_inc(const_b, 1)
                for q in range(2):
                    for b in range(2):
                        act.activation(KA[S:P, q, b, :], attc[S:P, 0:256], ACT.Copy).then_inc(const_b, 1)
                        for nh in range(NH):
                            act.activation(QA[S:P, q, nh, b, :], attc[S:P, 256:384], ACT.Copy).then_inc(const_b, 1)
                    act.activation(MM[0:S, q, :], attc[0:S, 384:512], ACT.Copy).then_inc(const_b, 1)

            def body(t, p, i2):
                if active(t, -1):
                    u, q = t + 1, (p + 1) % 2
                    act.wait_ge(shift_done, t + 2)
                    after(act, qk_transposed, u - 1)
                    after(act, swap_done, (u - 1) * 2)
                    act.activation(XH[:, q, 0, :], X[:, u, :], ACT.Identity, bias=shift[:, p, 0:1], scale=rstd[:, p, 0:1]).then_inc(xhat_done, 1)
                if isinstance(t, int) and t == 0:
                    constants()
                if active(t, 2):
                    u, q = t - 2, p
                    act.wait_ge(max_transposed, u + 1)
                    after(act, scored, u - 1)
                    act.activation(MM[S:S + 16, q, :], mixb[0:16, :], ACT.Copy, scale=-1.0).then_inc(mm_done, 1)
                if active(t, 7):
                    u = t - 7
                    act.wait_ge(z_transposed, u + 1)
                    zt = ZT[:, :, bass.ds(u * P, P)] if not isinstance(u, int) else ZT[:, :, u * P:(u + 1) * P]
                    act.activation(zt, mix_ps[:, 0:2 * P].rearrange("p (a b) -> p a b", a=2), ACT.Copy).then_inc(zt_done, 1)
                if active(t, 1):
                    u, q = t - 1, (p + 1) % 2
                    for b in range(2):
                        act.wait_ge(kbd_done[b], u + 1)
                    after(act, max_scored, u - 1)
                    act.activation(KA[0:S, q, :, :], KBD[0:S, q, :, :], ACT.Copy).then_inc(ka_done, 1)
                if active(t, 6):
                    u, q = t - 6, p
                    act.wait_ge(shift_done, t + 3)
                    after(act, z_transposed, u - 1)
                    if not isinstance(u, int):
                        act.wait_ge(z_stored[q], (i2 - 3) * 16)
                    elif u >= 2:
                        act.wait_ge(z_stored[q], 16 * (u // 2))
                    act.activation(Z[:, q, :], X[:, u, :], ACT.Identity, bias=shift[:, 1 - q, 2:3], scale=rstd[:, 1 - q, 2:3]).then_inc(z_done, 1)
                if active(t, 2):
                    u, q = t - 2, p
                    act.wait_ge(scored, u + 1)
                    after(act, pv_done, u - 1)
                    act.activation(PT[:, q, :, :, :, :].rearrange("p n a b c -> p (n a b c)"),
                                   PS[:, 4:6, :].rearrange("p n c -> p (n c)"), ACT.Exp).then_inc(probs_done, 1)
                if active(t, 0):
                    u, q = t, p
                    act.wait_ge(qkt_done, u + 1)
                    after(act, max_scored, u - 1)
                    for nh in range(NH):
                        act.activation(QA[0:S, q, nh, :, :].rearrange("p b (nl s) -> p b nl s", nl=NL),
                                       QKT[nh * S:(nh + 1) * S, q, 0:NL, :].rearrange("p nl (b s) -> p b nl s", b=2),
                                       ACT.Copy).then_inc(qa_done, 1)
                if active(t, 3):
                    u = t - 3
                    act.wait_ge(pv_done, u + 1)
                    act.activation(logsum[:, :], pv_ps[:, 2 * P:4 * P], ACT.Ln).then_inc(log_done, 1)
                    act.wait_ge(log_done, u + 1)
                    after(act, ot_done, u)
                    act.activation(rsum[:, :], logsum[:, :], ACT.Exp, scale=-1.0).then_inc(rsum_done, 1)

            pipeline(act, body)

            for q in range(2):
                act.wait_ge(z_stored[q], 16 * (TILES // 2))
            act.wait_ge(rt, 1)
            act.activation(RW[2][:, :], RW[1][:, :], ACT.Exp).then_inc(exp_done, 1)
            act.wait_ge(exp_done, 1)
            act.activation(RW[3][:, :], RW[2][:, :], ACT.Ln, bias=1.0).then_inc(ln_done, 1)

            def block_silu(m, bank=0):
                act.wait_ge(gu_done, m * 3 + 3)
                after(act, h_done, m * 2)
                act.activation(GA[0:IA, 0, :], B[bank][0:IA, :], ACT.Silu).then_inc(silu_done, 1)
                act.activation(UA[0:IA, 0, :], B[bank + 1][0:IA, :], ACT.Copy).then_inc(silu_done, 1)
                act.activation(GA[0:IB, 1, :], B[bank + 2][0:IB, :], ACT.Silu).then_inc(silu_done, 1)
                act.activation(UA[0:IB, 1, :], B[bank + 2][IB:2 * IB, :], ACT.Copy).then_inc(silu_done, 1)

            def block_dn(m):
                act.wait_ge(dn_done, m + 1)
                after(act, res_done, m * 2)
                for k in range(2):
                    act.activation(DS[:, 0, k, :], B[3 + k][:, :], ACT.Copy).then_inc(dn_copied, 1)

            block_silu(0)
            act.wait_ge(rt, 10)
            act.activation(RW[5][:, :], RW[1][:, :], ACT.Sqrt).then_inc(sqrt_done, 1)
            block_silu(1, 5)
            block_dn(0)
            with act.Fori(0, BLOCKS // 2 - 2) as n:
                for k in range(2):
                    block_silu(n * 2 + (2 + k))
                    block_dn(n * 2 + (1 + k))
            block_silu(BLOCKS - 2)
            block_silu(BLOCKS - 1)

            with act.Fori(0, E // WRING) as n:
                for r in range(WRING):
                    q = r % 2
                    act.wait_ge(ge_done, n * WRING + (r + 1))
                    act.activation(SE[0:IA, q, 0, :], ge_ps[q][0:IA, 0:P], ACT.Silu).then_inc(se_done, 1)
                    act.activation(SE[0:IB, q, 1, :], ge_ps[q][0:IB, 2 * P:3 * P], ACT.Silu).then_inc(se_done, 1)

        @block.tensor
        def _(pe):
            pe.wait_ge(rope_in, 80)

            def body(t, p, i2):
                if active(t, 0):
                    u, q = t, p
                    pe.wait_ge(swap_done, (u + 1) * 2)
                    pe.wait_ge(khat_done, (u + 1) * 3)
                    after(pe, roped, u * 2)
                    for v, bank in ((0, plain_ps), (1, swap_ps)):
                        for nl in range(NL):
                            pe.transpose(bank[:, nl * P:(nl + 1) * P], XH[:, q, v, nl * P:(nl + 1) * P], ident[:, :])
                        last = pe.transpose(bank[:, 2 * P:3 * P], KH[:, q, v, :], ident[:, :])
                    last.then_inc(qk_transposed, 1)
                def score(nh):
                    u, q = t - 2, p
                    rows = slice(nh * S, (nh + 1) * S)
                    for b in range(2):
                        for gp in range(2):
                            col = (b * 2 + gp) * P
                            pe.matmul(sc_ps[nh][:, col:col + P], KBD[rows, q, b, gp * P:(gp + 1) * P],
                                      QKT[rows, q, 0:NL, b * S:(b + 1) * S], start=(b == 0 and gp == 0), stop=False,
                                      skip_group_check=True)

                if active(t, 2):
                    after(pe, probs_done, t - 2)
                    score(0)
                if (active(t, 7) or active(t, 2)) and active(t, 5):
                    after(pe, x1_done, t - 4)
                if active(t, 7):
                    u, q = t - 7, (p + 1) % 2
                    pe.wait_ge(z_done, u + 1)
                    for c in range(2):
                        last = pe.transpose(mix_ps[:, c * P:(c + 1) * P], Z[:, q, c * P:(c + 1) * P], ident[:, :])
                    last.then_inc(z_transposed, 1)
                if active(t, 2):
                    u, q = t - 2, p
                    pe.wait_ge(max_done, u + 1)
                    pe.transpose(mixb[0:16, 0:P], MX[:, q, :], identb[:, :]).then_inc(max_transposed, 1)
                if active(t, 2):
                    score(1)
                    pe.wait_ge(mm_done, t - 1)
                    for nh in range(NH):
                        for b in range(2):
                            for gp in range(2):
                                col = (b * 2 + gp) * P
                                last = pe.matmul(sc_ps[nh][:, col:col + P], pick[:, (nh * 2 + b) * 2 + gp, :], MM[:, p, :],
                                                 start=False, stop=True, skip_group_check=True)
                    last.then_inc(scored, 1)
                if active(t, 1):
                    u, q = t - 1, (p + 1) % 2
                    if isinstance(t, int) and u == 0:
                        pe.wait_ge(const_b, 16)
                    pe.wait_ge(ka_done, u + 1)
                    pe.wait_ge(qa_done, (u + 1) * 2)
                    after(pe, max_done, u)
                    for nh in range(NH):
                        for b in range(2):
                            last = pe.matmul(max_ps[nh][:, b * 256:(b + 1) * 256], QA[:, q, nh, b, :], KA[:, q, b, :],
                                             start=True, stop=True)
                    last.then_inc(max_scored, 1)
                if active(t, 3):
                    u, q = t - 3, (p + 1) % 2
                    pe.wait_ge(probs_done, u + 1)
                    if isinstance(u, int):
                        pe.wait_ge(v_in[q], 64 * (u // 2 + 1))
                    else:
                        pe.wait_ge(v_in[q], (i2 * 2 - 3 + p - q) * 32 + 64)
                    after(pe, ot_done, u)
                    for nh in range(NH):
                        for gp in range(2):
                            r0 = 32 * (2 * nh + gp)
                            for b in range(2):
                                probs = PT[:, q, nh, b, gp, :]
                                pe.matmul(pv_ps[r0:r0 + 32, b * P:(b + 1) * P],
                                          VBD[:, q, b, gp, :, :].rearrange("p a b -> p (a b)"), probs, start=True, stop=True)
                                last = pe.matmul(pv_ps[r0:r0 + 32, (2 + b) * P:(3 + b) * P], attc[:, 512:544], probs,
                                                 start=True, stop=True)
                    last.then_inc(pv_done, 1)
                if active(t, 4):
                    u, q = t - 4, p
                    if isinstance(t, int) and u == 0:
                        pe.wait_ge(wout_in, 16)
                    pe.wait_ge(ot_done, u + 1)
                    if active(t, 2):
                        pe.wait_ge(mm_done, t - 1)
                    if active(t, 7):
                        pe.wait_ge(zt_done, t - 6)
                    if active(t, 5):
                        pe.wait_ge(x1_done, t - 4)
                    for nl in range(NL):
                        last = pe.matmul(mix_ps[:, 0:D], OT[:, q, nl, :, :].rearrange("p a b -> p (a b)"), WO[:, nl, :],
                                         start=(nl == 0), stop=(nl == NL - 1))
                    last.then_inc(projected, 1)

            pipeline(pe, body)

            pe.wait_ge(ws_in, 64)
            pe.wait_ge(zt_done, TILES)
            pe.wait_ge(zero_done, 2)
            for k in range(2):
                for c in range(2):
                    for j in range(4):
                        n = k * 4 + j
                        last = pe.matmul(B[5 + k][32 * j:32 * j + 32, :], GW[:, c, :], ZT[:, c, n * 512:(n + 1) * 512],
                                         start=(c == 0), stop=(c == 1), skip_group_check=True)
                last.then_inc(lg_done, 1)
            for k in range(2):
                pe.wait_ge(ls_done, k + 1)
                for c in range(4):
                    last = pe.transpose(B[3 + k][:, c * P:(c + 1) * P], LS[:, k, c * P:(c + 1) * P], ident[:, :])
                last.then_inc(lt_done, 1)

            def block_gu(m, q, first=0):
                after(pe, silu_done, (m - (m == 1)) * 4)
                cols = slice(m * 512, (m + 1) * 512) if isinstance(m, int) else bass.ds(m * 512, 512)
                for bank, lo, hi in ((0, 0, IA), (1, IA, 2 * IA), (2, 2 * IA, I2)):
                    for c in range(2):
                        last = pe.matmul(B[first + bank][0:hi - lo, :], WS13[:, c, lo:hi], ZT[:, c, cols], start=(c == 0), stop=(c == 1))
                    last.then_inc(gu_done, 1)

            def block_down(m, q):
                pe.wait_ge(h_done, m * 2 + 2)
                if m > BLOCKS - LATE:
                    pe.wait_ge(late_res_done, (m - (BLOCKS - LATE)) * 2)
                else:
                    after(pe, dn_copied, m * 2)
                for j in range(4):
                    o = B[3 + j // 2][:, (j % 2) * D:(j % 2 + 1) * D]
                    pe.matmul(o, H[0:IA, q, 0, j * P:(j + 1) * P], WS2[0:IA, 0, :], start=True, stop=False)
                    last = pe.matmul(o, H[0:IB, q, 1, j * P:(j + 1) * P], WS2[0:IB, 1, :], start=False, stop=True)
                last.then_inc(dn_done, 1)

            def prefix():
                pe.wait_ge(mask_done, 3)
                pe.wait_ge(silu_done, 8)
                pe.matmul(B[5][:, :], trib[:, :], MB[:, :], start=True, stop=False, skip_group_check=True)
                for i in range(TILES - 1):
                    later = B[5][:, (i + 1) * E:TILES * E].rearrange("p (n e) -> p n e", e=E)
                    rep = MB[:, i * E:(i + 1) * E].unsqueeze(1).to_broadcast([P, TILES - 1 - i, E])
                    pe.matmul(later, onesb[:, :], rep, start=False, stop=(i == TILES - 2), skip_group_check=True)
                pe.matmul(B[6][:, :], onesb[:, :], MB[:, :], start=True, stop=True).then_inc(prefix_done, 1)

            def dispatch(c):
                pe.wait_ge(hot_done, c + 1)
                for i in range(HT):
                    for h, bank in ((0, B[7]), (1, B[5])):
                        last = pe.matmul(bank[:, 0:NV * 64], OA[:, c % 2, i * 2 + h, :, :].rearrange("p a e -> p (a e)"),
                                         OBV[:, c % 2, i * 2 + h, :, :].rearrange("p v b -> p (v b)"),
                                         start=(c == 0 and i == 0), stop=(c == 3 and i == HT - 1), skip_group_check=True)
                last.then_inc(dispatched, 1)

            def lists():
                pe.wait_ge(lay_done, 1)
                for hv in range(4):
                    h, v = hv // 2, hv % 2
                    last = pe.matmul(B[6][:, v * E + h * 8:v * E + h * 8 + 8], lay[:, hv, :, :].rearrange("p b a -> p (b a)"),
                                     rc[:, RC["blk"]:RC["blk"] + 8], start=True, stop=True)
                last.then_inc(listed, 1)

            block_gu(0, 0)
            block_gu(1, 1, first=5)
            pe.wait_ge(l_done, 2)
            block_down(0, 0)
            block_gu(2, 0)
            block_down(1, 1)
            prefix()
            block_gu(3, 1)
            block_down(2, 0)
            block_gu(4, 0)
            dispatch(0)
            block_down(3, 1)
            dispatch(1)
            block_gu(5, 1)
            dispatch(2)
            dispatch(3)
            block_down(4, 0)
            lists()
            block_gu(6, 0)
            block_down(5, 1)
            block_gu(7, 1)

            def expert_t(n, r):
                q = r % 2
                pe.wait_ge(xg_in[r], n * 16 + 16)
                e = n * WRING + r
                after(pe, xe_done, e - 1)
                for c in range(2):
                    last = pe.transpose(xe_ps[q][:, c * P:(c + 1) * P], XG[:, r, c * P:(c + 1) * P], ident[:, :])
                last.then_inc(xe_t, 1)

            def expert_gu(n, r):
                q = r % 2
                e = n * WRING + r
                pe.wait_ge(w_in[r], n * 48 + 48)
                pe.wait_ge(xe_done, e + 1)
                after(pe, he_done, (e - 1) * 2)
                for k, (lo, hi) in enumerate(((0, IA), (IA, 2 * IA), (2 * IA, I2))):
                    for c in range(2):
                        last = pe.matmul(ge_ps[q][0:hi - lo, k * P:(k + 1) * P], W13[:, r, c, lo:hi], XE[:, q, c, :],
                                         start=(c == 0), stop=(c == 1))
                last.then_inc(ge_done, 1)

            def expert_down(n, r):
                q = r % 2
                e = n * WRING + r
                pe.wait_ge(he_done, e * 2 + 2)
                after(pe, ye_done, e - 1)
                pe.matmul(ye_bank[q][:, 0:D], HE[0:IA, q, 0, :], W2[0:IA, r, 0, :], start=True, stop=False)
                pe.matmul(ye_bank[q][:, 0:D], HE[0:IB, q, 1, :], W2[0:IB, r, 1, :], start=False, stop=True).then_inc(ye_ps, 1)

            def experts(n):
                for r in range(WRING):
                    if r < WRING - 1:
                        expert_t(n, r + 1)
                    else:
                        expert_t(n + 1, 0) if not (isinstance(n, int) and n == E // WRING - 1) else None
                    if isinstance(n, int) and n == 0 and r < 2:
                        expert_gu(0, 1) if r else expert_down(0, 0)
                        continue
                    expert_gu(n, r)
                    if r > 0:
                        expert_down(n, r - 1)
                    elif not (isinstance(n, int) and n == 0):
                        expert_down(n - 1, WRING - 1)

            expert_t(0, 0)
            block_down(BLOCKS - 2, 0)
            expert_gu(0, 0)
            block_down(BLOCKS - 1, 1)
            experts(0)
            with pe.Fori(1, E // WRING - 1) as n:
                experts(n)
            experts(E // WRING - 1)
            expert_down(E // WRING - 1, WRING - 1)

        @block.vector
        def _(dve):
            dve.wait_ge(rope_in, 80)
            for v in range(2):
                for nl in range(NL):
                    dve.tensor_scalar(ropet[:, v, nl, :], ropec[:, v, :], wqn[:, v, nl:nl + 1], HD ** -0.5, ALU.mult, ALU.mult).then_inc(tables, 1)
                dve.tensor_scalar(ropet[:, v, NL, :], ropec[:, v, :], wkn[:, v:v + 1], None, ALU.mult).then_inc(tables, 1)
            dve.memset(negmean[:, :, :], 0.0).then_inc(tables, 1)
            dve.wait_ge(tables, 7)

            def body(t, p, i2):
                rolled = not isinstance(t, int)
                q = (p + 1) % 2

                def stats_ready():
                    if active(t, -2):
                        dve.wait_ge(stats_done, (t + 3) * 2)
                    if active(t, 6):
                        dve.wait_ge(z_stats, t - 5)

                if active(t, -2):
                    x_loaded(dve, t, -2)
                    dve.bn_stats(stats[:, q, 0, :], X[:, t + 2, :]).then_inc(stats_done, 1)
                    dve.bn_stats(stats[:, q, 1, :], C[:, t + 2, :]).then_inc(stats_done, 1)
                if active(t, 5):
                    u = t - 5
                    dve.wait_ge(projected, u + 1)
                    dve.tensor_tensor(X[:, u, :], X[:, u, :], mix_ps[:, 0:D], ALU.add).then_inc(x1_done, 1)
                if rolled:
                    stats_ready()
                if active(t, 1):
                    key_blocks(dve, t - 1, q, 0)
                if not rolled:
                    stats_ready()
                if active(t, -2):
                    for k in range(2):
                        dve.bn_aggr(mv[:, q, k, :], stats[:, q, k, :]).then_inc(aggr_done, 1)
                if active(t, 6):
                    dve.bn_aggr(mv[:, q, 2, :], stats[:, p, 2, :]).then_inc(z_aggr, 1)
                if active(t, 4):
                    u = t - 4
                    dve.wait_ge(rsum_done, u + 1)
                    after(dve, projected, u - 1)
                    if rolled:
                        dve.wait_ge(x1_done, t - 4)
                    dve.tensor_tensor(OT[:, p, :, :, :].rearrange("p nl b s -> p b nl s"),
                                      pv_ps[:, 0:2 * P].rearrange("p (b nl s) -> p b nl s", b=2, nl=NL),
                                      rsum[:, :].rearrange("p (b nl s) -> p b nl s", b=2, nl=NL), ALU.mult).then_inc(ot_done, 1)
                if active(t, -2):
                    dve.wait_ge(aggr_done, (t + 3) * 2)
                    after(dve, shift_done, t + 1)
                    dve.tensor_scalar(veps[:, q:q + 1], mv[:, q, 1, 1:2], RMS_EPS, None, ALU.add).then_inc(veps_done, 1)
                    dve.tensor_scalar(var_in[:, q, 0:1], mv[:, q, 0, 1:2], 1.0 + RMS_EPS, LN_EPS * RMS_EPS, ALU.mult, ALU.add).then_inc(var_done, 1)
                    dve.tensor_scalar(negmean[:, q, 0:1], mv[:, q, 0, 0:1], -1.0, None, ALU.mult).then_inc(var_done, 1)
                if active(t, 6):
                    dve.wait_ge(z_aggr, t - 5)
                    after(dve, shift_done, t + 1)
                    dve.tensor_scalar(var_in[:, q, 2:3], mv[:, q, 2, 1:2], LN_EPS, None, ALU.add).then_inc(z_var, 1)
                    dve.tensor_scalar(negmean[:, q, 2:3], mv[:, q, 2, 0:1], -1.0, None, ALU.mult).then_inc(z_var, 1)
                if active(t, -2):
                    dve.wait_ge(veps_done, t + 3)
                    dve.scalar_tensor_tensor(out=var_in[:, q, 1:2], in0=mv[:, q, 1, 0:1], scalar=mv[:, q, 1, 0:1],
                                             in1=veps[:, q:q + 1], op0=ALU.mult, op1=ALU.add).then_inc(var_done, 1)
                if active(t, 5):
                    if not rolled:
                        dve.wait_ge(x1_done, t - 4)
                    dve.bn_stats(stats[:, q, 2, :], X[:, t - 5, :]).then_inc(z_stats, 1)
                if active(t, 0):
                    u, q = t, p
                    dve.wait_ge(qk_transposed, u + 1)
                    after(dve, qkt_done, u)
                    for v, bank in ((0, plain_ps), (1, swap_ps)):
                        dve.tensor_tensor(rp[:, v, :], bank[:, 0:3 * P], ropet[:, v, :, :].rearrange("p a b -> p (a b)"), ALU.mult).then_inc(roped, 1)
                if active(t, -1):
                    u, q = t + 1, (p + 1) % 2
                    dve.wait_ge(rstd_done, u + 1)
                    cv = C[:, u, :].unsqueeze(1).to_broadcast([P, 2, KV])
                    dve.tensor_scalar(KH[:, q, 0, :].rearrange("p (a c) -> p a c", a=2), cv, rstd[:, p, 1:2], None, ALU.mult).then_inc(khat_done, 1)
                    cs = C[:, u, :].rearrange("p (g h d) -> p g h d", h=2, d=8)
                    ks = KH[:, q, 1, :].rearrange("p (a g h d) -> p a g h d", a=2, h=2, d=8)
                    for h in range(2):
                        dve.tensor_scalar(ks[:, :, :, 1 - h, :], cs[:, :, h, :].unsqueeze(1).to_broadcast([P, 2, G, 8]),
                                          rstd[:, p, 1:2], None, ALU.mult).then_inc(khat_done, 1)
                if active(t, 1):
                    u, q = t - 1, (p + 1) % 2
                    dve.wait_ge(max_scored, u + 1)
                    after(dve, max_transposed, u - 1)
                    dve.tensor_reduce(MX[:, q, :], PS[:, 2:4, :].rearrange("p n (a k) -> p (n a) k", k=S), AX.X, ALU.max).then_inc(max_done, 1)

            pipeline(dve, body)

            N = TILES * E
            step = [0]

            def link(ins):
                step[0] += 1
                ins.then_inc(rt, 1)
                dve.wait_ge(rt, step[0])

            def rcc(name, n):
                return rc[:, RC[name]:RC[name] + n]

            def te(ap):
                return ap.rearrange("p (n e) -> p n e", e=E)

            def per_tile(ap):
                return ap.unsqueeze(2).to_broadcast([P, TILES, E])

            def per_expert(ap):
                return ap.unsqueeze(1).to_broadcast([P, TILES, E])

            for k in range(2):
                dve.wait_ge(z_stored[k], 16 * (TILES // 2))
            for k in range(2):
                dve.wait_ge(lg_done, k + 1)
                dve.tensor_copy(LS[:, k, :], B[5 + k][:, :]).then_inc(ls_done, 1)
            L = RW[0]
            for k in range(2):
                dve.wait_ge(lt_done, k + 1)
                dve.tensor_copy(L[:, k * 256:(k + 1) * 256].rearrange("p (j c e) -> p j c e", j=4, c=4),
                                B[3 + k][:, :].rearrange("p (c j e) -> p j c e", c=4, j=4)[:, :, :, 0:E]).then_inc(l_done, 1)
            dve.wait_ge(l_done, 2)
            dve.wait_ge(rc_in, 32)
            link(dve.scalar_tensor_tensor(out=RW[1][:, :], in0=L[:, :], scalar=-1.0, in1=L[:, :], op0=ALU.mult, op1=ALU.min))
            ex, lg, sr = RW[2], RW[3], RW[4]
            dve.wait_ge(exp_done, 1)
            link(dve.tensor_scalar(sr[:, :], ex[:, :], 1.0 / 5, None, ALU.mult))
            for c in (-1.0 / 4, 1.0 / 3, -1.0 / 2, 1.0):
                link(dve.scalar_tensor_tensor(out=sr[:, :], in0=sr[:, :], scalar=c, in1=ex[:, :], op0=ALU.add, op1=ALU.mult))
            dve.wait_ge(ln_done, 1)
            link(dve.tensor_tensor(sr[:, :], sr[:, :], lg[:, :], ALU.subtract))
            link(dve.scalar_tensor_tensor(out=sr[:, :], in0=ex[:, :], scalar=1.0 / 16, in1=sr[:, :], op0=ALU.is_lt, op1=ALU.mult))
            link(dve.tensor_tensor(lg[:, :], lg[:, :], sr[:, :], ALU.add))
            link(dve.scalar_tensor_tensor(out=RW[1][:, :], in0=L[:, :], scalar=0.0, in1=lg[:, :], op0=ALU.max, op1=ALU.add))
            assert step[0] == 10
            dve.wait_ge(sqrt_done, 1)
            sc, key, hot1, hot2 = RW[5], RW[0], RW[1], RW[2]
            link(dve.tensor_tensor(te(key[:, :]), te(sc[:, :]), per_expert(GB[:, :]), ALU.add))
            for n, hot in enumerate((hot1, hot2)):
                if n:
                    link(dve.scalar_tensor_tensor(out=key[:, :], in0=hot1[:, :], scalar=-3e38, in1=key[:, :], op0=ALU.mult, op1=ALU.add))
                link(dve.tensor_reduce(RS[0][:, :], te(key[:, :]), AX.X, ALU.max))
                link(dve.tensor_tensor(te(hot[:, :]), te(key[:, :]), per_tile(RS[0][:, :]), ALU.is_equal))
                link(dve.tensor_tensor(te(hot[:, :]), te(hot[:, :]), per_expert(rcc("desc", E)), ALU.mult))
                link(dve.tensor_reduce(RS[0][:, :], te(hot[:, :]), AX.X, ALU.max))
                link(dve.tensor_tensor(te(hot[:, :]), te(hot[:, :]), per_tile(RS[0][:, :]), ALU.is_equal))
            M = RW[3]
            link(dve.tensor_tensor(M[:, :], hot1[:, :], hot2[:, :], ALU.add))
            dve.tensor_copy(MB[:, :], M[:, :]).then_inc(mask_done, 1)
            dve.tensor_copy(trib[:, :], rcc("tri", P)).then_inc(mask_done, 1)
            dve.memset(onesb[:, :], 1.0).then_inc(mask_done, 1)
            wd = RW[5]
            link(dve.tensor_tensor(wd[:, :], sc[:, :], M[:, :], ALU.mult))
            link(dve.tensor_reduce(RS[1][:, :], te(wd[:, :]), AX.X, ALU.add))
            link(dve.reciprocal(RS[1][:, :], RS[1][:, :]))
            link(dve.tensor_tensor(te(wd[:, :]), te(wd[:, :]), per_tile(RS[1][:, :]), ALU.mult))
            rest = RW[6]
            link(dve.tensor_copy(wv[0][:, :], wd[:, :]))
            link(dve.tensor_tensor(rest[:, :], wd[:, :], wv[0][:, :], ALU.subtract))
            link(dve.tensor_copy(wv[1][:, :], rest[:, :]))
            link(dve.tensor_tensor(rest[:, :], rest[:, :], wv[1][:, :], ALU.subtract))
            dve.tensor_copy(wv[2][:, :], rest[:, :])
            dve.tensor_copy(te(wv[3][:, :]), per_tile(rcc("tile", TILES)))
            dve.tensor_copy(iat[:, :, :], rcc("ia", 16).unsqueeze(2).to_broadcast([P, 16, 8]))
            link(dve.tensor_copy(ibt[:, :, :], rcc("ib", 8).unsqueeze(2).to_broadcast([P, 8, 8])))
            no = RW[0]
            link(dve.tensor_scalar(no[:, :], M[:, :], -1.0, 1.0, ALU.mult, ALU.add))
            off, low, place = RW[1], RW[2], RW[4]
            link(dve.tensor_tensor(te(off[:, :]), te(no[:, :]), per_tile(rcc("rev", TILES)), ALU.mult))
            dve.wait_ge(prefix_done, 1)
            link(dve.tensor_reduce(cnt[:, :], B[6][:, :].rearrange("p (n e) -> p e n", e=E), AX.X, ALU.add))
            link(dve.tensor_tensor(te(low[:, :]), te(no[:, :]), per_expert(cnt[:, :]), ALU.mult))
            link(dve.tensor_tensor(place[:, :], B[5][:, :], off[:, :], ALU.add))
            link(dve.tensor_tensor(low[:, :], place[:, :], low[:, :], ALU.is_lt))
            link(dve.scalar_tensor_tensor(out=place[:, :], in0=low[:, :], scalar=FAR, in1=place[:, :], op0=ALU.mult, op1=ALU.add))
            link(dve.tensor_copy(slot_i[:, :], place[:, :]))
            link(dve.tensor_scalar(ab_i[:, 0, :], slot_i[:, :], 3, None, ALU.logical_shift_right))
            link(dve.tensor_scalar(ab_i[:, 1, :], slot_i[:, :], 7, None, ALU.bitwise_and))
            link(dve.tensor_copy(hib[:, :], ab_i[:, 0, :]))
            link(dve.tensor_copy(lob[:, :], ab_i[:, 1, :]))

            def quarter(t, c, n):
                return t[:, c * HN * 8:(c + 1) * HN * 8].rearrange("p (n e) -> p n e", e=8).unsqueeze(2).to_broadcast([P, HN, n, 8])

            for c in range(4):
                if c >= 2:
                    dve.wait_ge(dispatched, c - 1)
                dve.tensor_tensor(OA[:, c % 2, :, :, :], iat[:, :, :].unsqueeze(1).to_broadcast([P, HN, 16, 8]),
                                  quarter(hib, c, 16), ALU.is_equal)
                link(dve.tensor_tensor(OBE[:, :, :, :], ibt[:, :, :].unsqueeze(1).to_broadcast([P, HN, 8, 8]),
                                       quarter(lob, c, 8), ALU.is_equal))
                for v in range(4):
                    dve.tensor_tensor(OBV[:, c % 2, :, v, :].rearrange("p n (b e) -> p n b e", e=8), OBE[:, :, :, :],
                                      quarter(wv[v], c, 8), ALU.mult)
                dve.tensor_scalar(OBV[:, c % 2, :, 4, :], OBE[:, :, :, :].rearrange("p n b e -> p n (b e)"),
                                  rcc("pos", 1), None, ALU.mult).then_inc(hot_done, 1)
                dve.wait_ge(hot_done, c + 1)
            dve.wait_ge(dispatched, 4)
            for h, bank in ((0, B[7]), (1, B[5])):
                ins = dve.tensor_tensor(dg[:, h, :, :], bank[:, 0:NV * 64].rearrange("p (v e) -> p v e", e=8),
                                        rcc("blk", 8).unsqueeze(1).to_broadcast([P, NV * 8, 8]), ALU.mult)
            link(ins)
            link(dve.tensor_reduce(dv[:, :, :, :].rearrange("p h v b -> p (h v b)"), dg[:, :, :, :].rearrange("p h v e -> p (h v) e"), AX.X, ALU.add))
            drv = dr[:, :, :].rearrange("p (h v) b -> p h v b", v=2)
            dve.scalar_tensor_tensor(out=drv[:, :, 0, :], in0=dv[:, :, 3, :], scalar=float(P), in1=dv[:, :, 4, :], op0=ALU.mult, op1=ALU.add)
            link(dve.tensor_tensor(drv[:, :, 1, :], dv[:, :, 1, :], dv[:, :, 2, :], ALU.add))
            link(dve.tensor_tensor(drv[:, :, 1, :], drv[:, :, 1, :], dv[:, :, 0, :], ALU.add))
            dve.tensor_tensor(lay[:, :, :, :].rearrange("p v b a -> p (v b) a"),
                              dr[:, :, :].rearrange("p v b -> p (v b)").unsqueeze(2).to_broadcast([P, 32, 16]),
                              rcc("sel", 16).unsqueeze(1).to_broadcast([P, 32, 16]), ALU.mult).then_inc(lay_done, 1)
            dve.wait_ge(listed, 1)
            dve.tensor_copy(idx[:, :], B[6][:, 0:E]).then_inc(lists_done, 1)
            dve.tensor_copy(wslot[:, :], B[6][:, E:2 * E]).then_inc(lists_done, 1)
            dve.wait_ge(lists_done, 2)

            def late_res(n):
                m = BLOCKS - LATE + n
                dve.wait_ge(dn_done, m + 1)
                if n == 1:
                    for k in range(2):
                        dve.wait_ge(res_stored[k], (BLOCKS - LATE) * 16)
                elif n >= 2:
                    dve.wait_ge(late_stored[n - 2], 32)
                for k in range(2):
                    dve.tensor_tensor(OUTB[:, (n + 1) % 2, k, :].rearrange("p (j c) -> p j c", j=2),
                                      B[3 + k][:, :].rearrange("p (j c) -> p j c", j=2),
                                      X[:, m * 4 + 2 * k:m * 4 + 2 * k + 2, :], ALU.add).then_inc(late_res_done, 1)

            def xe(e, r):
                q = r % 2
                dve.wait_ge(xe_t, e + 1)
                after(dve, ge_done, e - 1)
                dve.tensor_copy(XE[:, q, :, :].rearrange("p a b -> p (a b)"), xe_ps[q][:, 0:2 * P]).then_inc(xe_done, 1)

            def he(e, r):
                q = r % 2
                dve.wait_ge(se_done, e * 2 + 2)
                after(dve, ye_ps, e - 1)
                dve.tensor_tensor(HE[0:IA, q, 0, :], ge_ps[q][0:IA, P:2 * P], SE[0:IA, q, 0, :], ALU.mult).then_inc(he_done, 1)
                dve.tensor_tensor(HE[0:IB, q, 1, :], ge_ps[q][IB:2 * IB, 2 * P:3 * P], SE[0:IB, q, 1, :], ALU.mult).then_inc(he_done, 1)

            def ye(e, r):
                q = r % 2
                dve.wait_ge(ye_ps, e + 1)
                after(dve, added, (e - WRING + 1) * 16)
                dve.tensor_scalar(YE[:, r, :], ye_bank[q][:, 0:D], wslot[:, bass.ds(e, 1)] if not isinstance(e, int) else wslot[:, e:e + 1], None, ALU.mult).then_inc(ye_done, 1)

            def experts(n, first=False, last=False):
                for r in range(WRING):
                    e = n * WRING + r
                    if not (last and r == WRING - 1):
                        xe(e + 1, (r + 1) % WRING)
                    if first and r == 0:
                        ye(0, 0)
                    else:
                        he(e, r)
                    if not (first and r < 2):
                        ye(e - 1, (r - 1) % WRING)

            late_res(0)
            xe(0, 0)
            late_res(1)
            he(0, 0)
            late_res(2)
            experts(0, first=True)
            with dve.Fori(1, E // WRING - 1) as n:
                experts(n)
            experts(E // WRING - 1, last=True)
            ye(E - 1, WRING - 1)


_INS = ["x", "ctx", "wq_norm", "wk_norm", "w_out", "gate_w", "gate_b", "w13", "w2", "ws13", "ws2",
        "const_rope", "const_attn", "const_pick", "const_route"]


def _constants(np):
    p = np.arange(128)
    pos = np.arange(64)
    inv = (np.float32(1.0) / np.float32(10000.0) ** (np.arange(0, 16, 2, dtype=np.float32) / np.float32(16))).astype(np.float32)
    ang = np.outer(inv[p % 8], np.tile(pos, 2).astype(np.float32)).astype(np.float32)
    sign = np.where(p % 16 < 8, -1.0, 1.0)[:, None]
    kmask = (p[:, None] % 64 // 16 == np.arange(4)[None, :])
    rope = np.concatenate([np.eye(128), np.cos(ang), np.sin(ang) * sign, kmask], 1)

    attn = np.zeros((128, 544))
    j = np.arange(64)[:, None]
    attn[64:, 0:256] = np.tile(np.where(pos[None, :] > j, -1e30, 0.0), (1, 4))
    attn[64:, 256:384] = np.tile(np.eye(64), (1, 2))
    attn[:64, 384:512] = np.tile(np.where(j > pos[None, :], -1e30, 0.0), (1, 2))
    attn[:, 512:544] = p[:, None] // 64 == np.arange(32)[None, :] // 16

    pick = np.zeros((80, 8, 2, 64))
    pick[:64] = np.eye(64)[:, None, None, :]
    for blk in range(8):
        nb, gp = blk // 2, blk % 2
        for g2 in range(2):
            pick[64 + nb * 4 + gp * 2 + g2, blk, g2, :] = 1.0

    route = np.zeros((128, 264))
    tok = np.arange(32)[None, :] * 128 + p[:, None]
    route[:, RC["desc"]:RC["desc"] + 16] = 16 - np.arange(16)
    route[:, RC["tri"]:RC["tri"] + 128] = p[:, None] < p[None, :]
    route[:, RC["ia"]:RC["ia"] + 16] = np.arange(16)
    route[:, RC["ib"]:RC["ib"] + 8] = np.arange(8)
    route[:, RC["rev"]:RC["rev"] + 32] = 127 - tok
    route[:, RC["tile"]:RC["tile"] + 32] = np.arange(32)
    route[:, RC["pos"]] = p
    route[:, RC["blk"]:RC["blk"] + 8] = p[:, None] % 8 == np.arange(8)[None, :]
    route[:, RC["sel"]:RC["sel"] + 16] = p[:, None] // 8 == np.arange(16)[None, :]
    return {"const_rope": rope, "const_attn": attn, "const_pick": pick.reshape(80, 1024), "const_route": route}


def kernel(**inputs):
    import numpy as np
    import concourse.bacc as bacc
    from concourse.bass_utils import run_bass_kernel_spmd

    a = {k: np.asarray(v) for k, v in inputs.items()}
    order = np.arange(256).reshape(4, 2, 2, 16).transpose(2, 1, 0, 3).reshape(-1)
    swap = order.reshape(-1, 2, 8)[:, ::-1].reshape(-1)
    kv = np.arange(64)
    kvswap = kv.reshape(-1, 2, 8)[:, ::-1].reshape(-1)

    def rows(w):
        return w[order].reshape(2, 128, -1).transpose(1, 0, 2)

    def gate_up(w1, w3):
        return rows(np.concatenate([w1[:112], w3[:112], w1[112:], w3[112:]], 0).T)

    wq, wk = a["L0_xattn_q_norm_w"], a["L0_xattn_k_norm_w"]
    arrays = {
        "x": a["x"].reshape(4096, 256)[:, order],
        "ctx": a["ctx_512"].reshape(4096, 64),
        "wq_norm": np.stack([wq[order].reshape(2, 128), wq[swap].reshape(2, 128)]).transpose(2, 0, 1),
        "wk_norm": np.stack([np.tile(wk[kv], 2), np.tile(wk[kvswap], 2)], 1),
        "w_out": rows(a["L0_xattn_w_out"].T[:, order]),
        "gate_w": rows(a["L0_ffn_gate_w"].T),
        "gate_b": a["L0_ffn_gate_b"].reshape(1, 16),
        "w13": np.stack([gate_up(a["L0_ffn_W1"][e], a["L0_ffn_W3"][e]) for e in range(16)]),
        "w2": a["L0_ffn_W2"].transpose(0, 2, 1)[:, :, order],
        "ws13": gate_up(a["L0_ffn_Ws1"], a["L0_ffn_Ws3"]),
        "ws2": a["L0_ffn_Ws2"].T[:, order],
    }
    arrays.update({k: v.astype(np.float32) for k, v in _constants(np).items()})

    nc = bacc.Bacc("TRN2", target_bir_lowering=False, num_devices=1)
    feed, args = {}, []
    for name in _INS:
        v = np.ascontiguousarray(arrays[name])
        feed[name] = v
        args.append(nc.dram_tensor(name, v.shape, mybir.dt.from_np(v.dtype), kind="ExternalInput").ap())
    args.append(nc.dram_tensor("out", (4096, 256), mybir.dt.float32, kind="ExternalOutput").ap())
    xattn_moe_kernel(nc, *args)
    r = run_bass_kernel_spmd(nc, [feed], core_ids=[0])
    y = r.results[0]["out"]
    return y.reshape(64, 64, 2, 2, 4, 16).transpose(0, 1, 4, 3, 2, 5).reshape(64, 64, 256)
```

```python
import concourse.bass as bass
from concourse import mybir
from contextlib import ExitStack


RC = {"desc": 0, "tri": 16, "ia": 144, "ib": 160, "rev": 168, "tile": 200, "pos": 232, "blk": 240, "sel": 248}


def xattn_moe_kernel(
    nc: bass.Bass,
    x: bass.AP,
    ctx: bass.AP,
    qk_norm: bass.AP,
    w_out: bass.AP,
    gate_w: bass.AP,
    gate_b: bass.AP,
    w13: bass.AP,
    w2: bass.AP,
    ws13: bass.AP,
    ws2: bass.AP,
    const_rope: bass.AP,
    const_attn: bass.AP,
    const_pick: bass.AP,
    const_route: bass.AP,
    out: bass.AP,
):
    f32, bf16, i32 = mybir.dt.float32, mybir.dt.bfloat16, mybir.dt.int32
    ALU = mybir.AluOpType
    ACT = mybir.ActivationFunctionType
    AX = mybir.AxisListType

    P = 128
    TOK, D = x.shape
    TILES = TOK // P
    S = 64
    G, NH, NL, HD = 4, 2, 2, 16
    KV = G * HD
    E = gate_b.shape[-1]
    CAP = 128
    assert CAP == P
    I2 = w13.shape[-1]
    I = I2 // 2
    IA, IB = 112, I - 112
    LN_EPS = 1e-5
    RMS_EPS = 1e-5
    FAR = 8192.0
    BLOCKS = TOK // 512
    WARM = (7, 3, 4)
    LATE = 3
    WRING = 4

    with ExitStack() as ctx_all:
        def keep(stack, name, shape, dt):
            return stack.enter_context(nc.sbuf_tensor(name, shape, dt))

        def sem(name):
            return ctx_all.enter_context(nc.semaphore(name))

        z_rows = nc.dram_tensor("z_rows", [TOK, D], f32).ap()
        X = keep(ctx_all, "X", [P, TILES, D], f32)
        ZT = keep(ctx_all, "ZT", [P, 2, TOK], f32)
        ident = keep(ctx_all, "ident", [P, P], f32)
        GW = keep(ctx_all, "GW", [P, 2, 32], f32)
        WS13 = keep(ctx_all, "WS13", [P, 2, I2], f32)
        WS2 = keep(ctx_all, "WS2", [P, 2, D], f32)
        rc = keep(ctx_all, "rc", [P, const_route.shape[1]], f32)

        at = ExitStack()
        C = keep(at, "C", [P, TILES, KV], f32)
        ropec = keep(at, "ropec", [P, 2 * P + G], f32)
        ropet = keep(at, "ropet", [P, 2, 3, P], f32)
        XH = keep(at, "XH", [P, 2, 2, D], f32)
        KH = keep(at, "KH", [P, 2, 2, P], f32)
        rp = keep(at, "rp", [P, 2, 3 * P], f32)
        QKT = keep(at, "QKT", [P, 2, 3, P], f32)
        KBD = keep(at, "KBD", [P, 2, 2, G * S], f32)
        qkn = keep(at, "qkn", [P, 2, NL + 1], f32)
        attc = keep(at, "attc", [P, const_attn.shape[1]], f32)
        pickf = keep(at, "pickf", [80, const_pick.shape[1]], f32)
        identb = keep(at, "identb", [P, P], bf16)
        pick = keep(at, "pick", [80, 8, P], bf16)
        WO = keep(at, "WO", [P, NL, D], f32)
        stats = keep(at, "stats", [P, 2, 3, 6], f32)
        mv = keep(at, "mv", [P, 2, 3, 2], f32)
        var_in = keep(at, "var_in", [P, 2, 3], f32)
        negmean = keep(at, "negmean", [P, 2, 3], f32)
        shift = keep(at, "shift", [P, 2, 3], f32)
        zero = keep(at, "zero", [P, 8], f32)
        veps = keep(at, "veps", [P, 2], f32)
        rstd = keep(at, "rstd", [P, 2, 3], f32)
        neghalf = keep(at, "neghalf", [P, 3], f32)
        QA = keep(at, "QA", [P, 2, NH, 2, P], bf16)
        KA = keep(at, "KA", [P, 2, 2, G * S], bf16)
        MX = keep(at, "MX", [P, 2, 16], bf16)
        MM = keep(at, "MM", [80, 2, P], bf16)
        PT = keep(at, "PT", [P, 2, NH, 2, 2, P], f32)
        VBD = keep(at, "VBD", [P, 2, 2, 2, 2, HD], f32)
        logsum = keep(at, "logsum", [P, 2 * P], f32)
        rsum = keep(at, "rsum", [P, 2 * P], f32)
        OT = keep(at, "OT", [P, 2, NL, 2, S], f32)
        Z = keep(at, "Z", [P, 2, D], f32)
        at.close()

        ff = ctx_all.enter_context(ExitStack())
        GA = keep(ff, "GA", [P, 2, 2, 512], f32)
        UA = keep(ff, "UA", [P, 2, 2, 512], f32)
        H = keep(ff, "H", [P, 2, 2, 512], f32)
        DS = keep(ff, "DS", [P, 2, 512], f32)
        OUTB = keep(ff, "OUTB", [P, 2, 2, 512], f32)
        LS = keep(ff, "LS", [P, 2, 512], f32)
        W13 = keep(ff, "W13", [P, WRING, 2, I2], f32)
        W2 = keep(ff, "W2", [P, WRING, 2, D], f32)
        XG = keep(ff, "XG", [P, WRING, D], f32)
        GB = keep(ff, "GB", [P, E], f32)
        RW = [keep(ff, f"RW{i}", [P, TILES * E], f32) for i in range(7)]
        RS = [keep(ff, f"RS{i}", [P, TILES], f32) for i in range(4)]
        MB = keep(ff, "MB", [P, TILES * E], bf16)
        trib = keep(ff, "trib", [P, P], bf16)
        onesb = keep(ff, "onesb", [P, P], bf16)
        cnt = keep(ff, "cnt", [P, E], f32)
        slot_i = keep(ff, "slot_i", [P, TILES * E], i32)
        ab_i = keep(ff, "ab_i", [P, 2, TILES * E], i32)
        HT = TILES // 4
        HN = HT * 2
        NV = 5
        OA = keep(ff, "OA", [P, 2, HN, 16, 8], bf16)
        OBE = [LS[:, i, :].bitcast(bf16).rearrange("p (n b e) -> p n b e", b=8, e=8) for i in range(2)]
        OBV = keep(ff, "OBV", [P, 2, HN, NV, 64], bf16)
        iat = keep(ff, "iat", [P, 16, 8], bf16)
        ibt = keep(ff, "ibt", [P, 8, 8], bf16)
        hib = keep(ff, "hib", [P, TILES * E], bf16)
        lob = keep(ff, "lob", [P, TILES * E], bf16)
        wv = [keep(ff, f"wv{i}", [P, TILES * E], bf16) for i in range(4)]
        dg = keep(ff, "dg", [P, 2, NV * 8, 8], f32)
        dv = keep(ff, "dv", [P, 2, NV, 8], f32)
        dr = keep(ff, "dr", [P, 4, 8], f32)
        lay = keep(ff, "lay", [P, 4, 8, 16], f32)
        idx = keep(ff, "idx", [P, E], i32)
        wslot = keep(ff, "wslot", [P, E], f32)
        XE = keep(ff, "XE", [P, 2, 2, P], f32)
        SE = keep(ff, "SE", [P, 2, 2, P], f32)
        HE = keep(ff, "HE", [P, 2, 2, P], f32)
        YE = keep(ff, "YE", [P, WRING, D], f32)

        PS = ctx_all.enter_context(nc.psum_tensor("PS", [P, 8, 512], f32))
        B = [PS[:, i, :] for i in range(8)]

        plain_ps, swap_ps, max_ps, sc_ps, pv_ps, mix_ps = B[0], B[1], (B[2], B[3]), (B[4], B[5]), B[6], B[7]
        mixb = mix_ps[:, 256:320].bitcast(bf16)

        x_in = [sem(f"x_in{i}") for i in range(5)]
        ident_in, rope_in, attc_in, wout_in, ws_in, rc_in = (sem(n) for n in ("ident_in", "rope_in", "attc_in", "wout_in", "ws_in", "rc_in"))
        v_in = [sem(f"v_in{i}") for i in range(2)]
        zero_done, setup_pool = sem("zero_done"), sem("setup_pool")
        const_b, tables, warm_in = sem("const_b"), sem("tables"), sem("warm_in")
        stats_done, aggr_done, var_done = sem("stats_done"), sem("aggr_done"), sem("var_done")
        veps_done = sem("veps_done")
        rstd_done, xhat_done, khat_done = sem("rstd_done"), sem("xhat_done"), sem("khat_done")
        shift_done, swap_done = sem("shift_done"), sem("swap_done")
        qk_transposed, roped, qkt_done = sem("qk_transposed"), sem("roped"), sem("qkt_done")
        kbd_done = [sem(f"kbd_done{b}") for b in range(2)]
        ka_done, qa_done, max_scored, max_done = sem("ka_done"), sem("qa_done"), sem("max_scored"), sem("max_done")
        max_transposed, mm_done, scored, probs_done = sem("max_transposed"), sem("mm_done"), sem("scored"), sem("probs_done")
        pv_done, log_done, rsum_done, ot_done = sem("pv_done"), sem("log_done"), sem("rsum_done"), sem("ot_done")
        projected, x1_done, z_stats, z_aggr, z_var = sem("projected"), sem("x1_done"), sem("z_stats"), sem("z_aggr"), sem("z_var")
        z_done, z_transposed, zt_done = sem("z_done"), sem("z_transposed"), sem("zt_done")
        z_stored = [sem(f"z_stored{i}") for i in range(2)]

        def after(eng, s, n):
            if not isinstance(n, int) or n > 0:
                eng.wait_ge(s, n)

        FIRST, LOOP0, LOOP1, LAST = -2, 8, 30, TILES + 7
        DRAIN = TILES + 1
        X_CHUNKS = [(0, 1), (1, 4), (4, 8), (8, 16), (16, TILES)]

        def pipeline(eng, body):
            for t in range(FIRST, LOOP0):
                body(t, t % 2, t // 2)
            with eng.Fori(0, (LOOP1 - LOOP0) // 2) as i:
                for p in range(2):
                    body(i * 2 + (LOOP0 + p), p, i + LOOP0 // 2)
            for t in range(LOOP1, LAST):
                body(t, t % 2, t // 2)

        def active(t, lag):
            return not isinstance(t, int) or 0 <= t - lag < TILES

        def x_loaded(eng, t, lag):
            if isinstance(t, int):
                for c, (lo, _) in enumerate(X_CHUNKS):
                    if t - lag == lo or (t == LOOP0 - 1 and lo > LOOP0):
                        eng.wait_ge(x_in[c], 32)

        def quarter(t, c, n):
            return t[:, c * HN * 8:(c + 1) * HN * 8].rearrange("p (n e) -> p n e", e=8).unsqueeze(2).to_broadcast([P, HN, n, 8])

        def key_blocks(eng, u, q, b):
            eng.wait_ge(qkt_done, u + 1)
            after(eng, scored, u - 1)
            after(eng, ka_done, u - 1)
            eng.tensor_tensor(KBD[:, q, b, :].rearrange("p (g k) -> p g k", g=G),
                              QKT[:, q, NL, b * S:(b + 1) * S].unsqueeze(1).to_broadcast([P, G, S]),
                              ropec[:, 2 * P:2 * P + G].unsqueeze(2).to_broadcast([P, G, S]), ALU.mult).then_inc(kbd_done[b], 1)

        xe_ps, ge_ps, ye_bank = (B[6], B[7]), (B[5], B[0]), (B[1], B[2])

        block = ctx_all.enter_context(nc.Block())

        lg_done, ls_done, lt_done, l_done = sem("lg_done"), sem("ls_done"), sem("lt_done"), sem("l_done")
        rt = sem("rt")
        exp_done, ln_done, sqrt_done = sem("exp_done"), sem("ln_done"), sem("sqrt_done")
        mask_done, prefix_done, cnt_done = sem("mask_done"), sem("prefix_done"), sem("cnt_done")
        hot_done, dispatched, lay_done, listed, lists_done = (
            sem("hot_done"), sem("dispatched"), sem("lay_done"), sem("listed"), sem("lists_done"))
        gu_done, silu_done, h_done, dn_done, dn_copied, res_done, late_res_done = (
            sem("gu_done"), sem("silu_done"), sem("h_done"), sem("dn_done"), sem("dn_copied"), sem("res_done"),
            sem("late_res_done"))
        late_h_done = sem("late_h_done")
        weighed, part_copied, rest_done = sem("weighed"), sem("part_copied"), sem("rest_done")
        coded, tiles_hot, pos_hot = sem("coded"), sem("tiles_hot"), sem("pos_hot")
        res_stored = [sem(f"res_stored{i}") for i in range(2)]
        late_stored = [sem(f"late_stored{i}") for i in range(LATE)]
        w_in = [sem(f"w_in{i}") for i in range(WRING)]
        xg_in = [sem(f"xg_in{i}") for i in range(WRING)]
        xe_t, xe_done, ge_done, se_done, he_done, ye_ps, ye_done = (
            sem("xe_t"), sem("xe_done"), sem("ge_done"), sem("se_done"), sem("he_done"), sem("ye_ps"), sem("ye_done"))
        added = sem("added")

        ctx_v = ctx.rearrange("(n k) (gp g2 d) -> n k gp g2 d", k=S, gp=2, g2=2)

        @block.sync
        def _(sp):
            x_v = x.rearrange("(n p) c -> p n c", p=P)
            c_v = ctx.rearrange("(n p) c -> p n c", p=P)

            def load_x(c):
                lo, hi = X_CHUNKS[c]
                sp.dma_start(C[:, lo:hi, :], c_v[:, lo:hi, :]).then_inc(x_in[c], 16)
                sp.dma_start(X[:, lo:hi, :], x_v[:, lo:hi, :]).then_inc(x_in[c], 16)

            load_x(0)
            sp.dma_start(ident[:, :], const_rope[:, 0:P]).then_inc(ident_in, 16)
            load_x(1)
            sp.dma_start(ropec[:, :], const_rope[:, P:3 * P + G]).then_inc(rope_in, 16)
            sp.dma_start(qkn[:, :, :], qk_norm).then_inc(rope_in, 16)
            sp.dma_start(attc[:, :], const_attn).then_inc(attc_in, 16)
            sp.dma_start(pickf[:, :], const_pick).then_inc(attc_in, 16)
            load_x(2)
            sp.dma_start(WO[:, :, :], w_out).then_inc(wout_in, 16)

            def load_ffn_constants():
                sp.dma_start(rc[:, :], const_route).then_inc(rc_in, 16)
                sp.dma_start(WS13[:, :, :], ws13).then_inc(ws_in, 16)
                sp.dma_start(WS2[0:IA, 0, :], ws2[0:IA, :]).then_inc(ws_in, 16)
                sp.dma_start(WS2[0:IB, 1, :], ws2[IA:I, :]).then_inc(ws_in, 16)
                sp.dma_start(GW[:, :, 0:E], gate_w).then_inc(ws_in, 16)

            def load_values(u, q):
                for g2 in range(2):
                    for b in range(2):
                        sp.dma_start(VBD[g2 * S:(g2 + 1) * S, q, b, :, g2, :],
                                     ctx_v[u * 2 + b, :, :, g2, :]).then_inc(v_in[q], 16)

            sp.wait_ge(zero_done, 1)
            load_values(0, 0)
            load_values(1, 1)
            load_x(3)

            def body(t, p, i2):
                if active(t, 4) or not isinstance(t, int):
                    after(sp, pv_done, t - 3)
                if active(t, 2) and not (isinstance(t, int) and t < 4):
                    load_values(t - 2, p)
                if isinstance(t, int) and t == 4:
                    load_x(4)
                if isinstance(t, int) and t == 6:
                    load_ffn_constants()
                if active(t, 6):
                    u, q = t - 6, p
                    sp.wait_ge(z_done, u + 1)
                    sp.dma_start(z_rows[bass.ds(u * P, P), :] if not isinstance(u, int) else z_rows[u * P:(u + 1) * P, :],
                                 Z[:, q, :]).then_inc(z_stored[q], 16)

            pipeline(sp, body)
            sp.wait_ge(zt_done, TILES)
            sp.wait_ge(z_stored[0], 16 * (TILES // 2))
            sp.wait_ge(z_stored[1], 16 * (TILES // 2))
            sp.dma_start(GB[:, :], gate_b.to_broadcast([P, E])).then_inc(rc_in, 16)

            def load_w(e, r):
                sp.dma_start(W13[:, r, :, :], w13[e, :, :, :]).then_inc(w_in[r], 16)
                sp.dma_start(W2[0:IA, r, 0, :], w2[e, 0:IA, :]).then_inc(w_in[r], 16)
                sp.dma_start(W2[0:IB, r, 1, :], w2[e, IA:I, :]).then_inc(w_in[r], 16)

            for e in range(WRING):
                load_w(e, e)
            out_v = out.rearrange("(n j p) c -> n p j c", j=2, p=P)

            def store_res(n, k, slot, stored):
                sp.dma_start(out_v[n * 2 + k, :, :, :], OUTB[:, slot, k, :].rearrange("p (j c) -> p j c", j=2)).then_inc(stored, 16)

            with sp.Fori(0, BLOCKS - LATE) as n:
                for k in range(2):
                    sp.wait_ge(res_done, n * 2 + (k + 1))
                    store_res(n, k, 0, res_stored[k])
            for n in range(LATE):
                for k in range(2):
                    sp.wait_ge(late_res_done, n * 2 + (k + 1))
                    store_res(BLOCKS - LATE + n, k, (n + 1) % 2, late_stored[n])
            with sp.Fori(0, E // WRING - 1) as n:
                for r in range(WRING):
                    sp.wait_ge(ye_ps, n * WRING + (r + 1))
                    load_w(n * WRING + (WRING + r), r)

        @block.gpsimd
        def _(pool):
            pool.memset(VBD[:, :, :, :, :, :], 0.0).then_inc(zero_done, 1)
            pool.memset(GW[:, :, E:2 * E], 0.0).then_inc(zero_done, 1)
            pool.memset(neghalf[:, :], -0.5).then_inc(setup_pool, 1)
            pool.memset(zero[:, :], 0.0).then_inc(setup_pool, 1)
            pool.wait_ge(setup_pool, 2)

            def body(t, p, i2):
                if active(t, 1):
                    key_blocks(pool, t - 1, (p + 1) % 2, 1)
                if active(t, -1):
                    u, q = t + 1, (p + 1) % 2
                    pool.wait_ge(xhat_done, u + 1)
                    after(pool, qk_transposed, u - 1)
                    xs = XH[:, q, 0, :].rearrange("p (n h d) -> p n h d", h=2, d=8)
                    hs = XH[:, q, 1, :].rearrange("p (n h d) -> p n h d", h=2, d=8)
                    for h in range(2):
                        pool.tensor_tensor(hs[:, :, 1 - h, :], xs[:, :, h, :], zero[:, :].unsqueeze(1).to_broadcast([P, 16, 8]), ALU.add).then_inc(swap_done, 1)
                lo = 0 if active(t, -2) else 2
                hi = 3 if active(t, 6) else 2
                if lo < hi:
                    q = (p + 1) % 2
                    if lo == 0:
                        pool.wait_ge(var_done, (t + 3) * 3)
                    if hi == 3:
                        pool.wait_ge(z_var, (t - 5) * 2)
                    after(pool, z_done, t - 7)
                    pool.tensor_tensor(rstd[:, q, lo:hi], var_in[:, q, lo:hi], neghalf[:, lo:hi], ALU.pow).then_inc(rstd_done, 1)
                    pool.wait_ge(rstd_done, t + 3)
                    pool.tensor_tensor(shift[:, q, lo:hi], negmean[:, q, lo:hi], rstd[:, q, lo:hi], ALU.mult).then_inc(shift_done, 1)
                if active(t, 0):
                    u, q = t, p
                    pool.wait_ge(roped, (u + 1) * 2)
                    after(pool, scored, u - 1)
                    after(pool, qa_done, (u - 1) * 2)
                    after(pool, kbd_done[0], u - 1)
                    pool.tensor_tensor(QKT[:, q, :, :].rearrange("p a b -> p (a b)"), rp[:, 0, :], rp[:, 1, :], ALU.add).then_inc(qkt_done, 1)
            def block_h(m, q):
                pool.wait_ge(silu_done, m * 4 + 4)
                after(pool, dn_done, m - 1)
                pool.tensor_tensor(H[0:IA, q, 0, :], GA[0:IA, q, 0, :], UA[0:IA, q, 0, :], ALU.mult).then_inc(h_done, 1)
                pool.tensor_tensor(H[0:IB, q, 1, :], GA[0:IB, q, 1, :], UA[0:IB, q, 1, :], ALU.mult).then_inc(h_done, 1)

            def block_res(m, first):
                for k in range(2):
                    pool.wait_ge(dn_copied, m * 2 + (k + 1))
                    if not first:
                        pool.wait_ge(res_stored[k], m * 16)
                    pool.tensor_tensor(OUTB[:, 0, k, :].rearrange("p (j c) -> p j c", j=2),
                                       DS[:, k, :].rearrange("p (j c) -> p j c", j=2),
                                       X[:, bass.ds(m * 4 + 2 * k, 2), :] if not isinstance(m, int) else X[:, m * 4 + 2 * k:m * 4 + 2 * k + 2, :],
                                       ALU.add).then_inc(res_done, 1)

            def body_and_ffn(t, p, i2):
                body(t, p, i2)
                if isinstance(t, int) and t == DRAIN + 4:
                    pool.wait_ge(scored, TILES)
                    block_h(0, 0)

            pipeline(pool, body_and_ffn)

            pool.wait_ge(zt_done, TILES)
            block_h(1, 1)
            block_res(0, True)

            def tile_codes(c):
                pool.wait_ge(coded, c + 1)
                if c >= 2:
                    pool.wait_ge(dispatched, c - 1)
                pool.tensor_tensor(OBV[:, c % 2, :, 3, :].rearrange("p n (b e) -> p n b e", e=8), OBE[c % 2],
                                   quarter(wv[3], c, 8), ALU.mult).then_inc(tiles_hot, 1)

            def weight_rest(k):
                pool.wait_ge(part_copied, k + 1)
                pool.tensor_tensor(RW[3][:, :], (RW[3] if k else RW[5])[:, :], wv[k][:, :], ALU.subtract).then_inc(rest_done, 1)

            block_h(2, 0)
            block_res(1, False)
            block_h(3, 1)
            weight_rest(0)
            weight_rest(1)
            block_res(2, False)
            block_h(4, 0)
            block_res(3, False)
            tile_codes(0)
            block_h(5, 1)
            tile_codes(1)
            block_res(4, False)
            tile_codes(2)
            tile_codes(3)

            def gather(e):
                if e >= WRING:
                    pool.wait_ge(xe_t, e - WRING + 1)
                pool.indirect_dma_start(out=XG[:, e % WRING, :], out_offset=None, in_=z_rows,
                                        in_offset=bass.IndirectOffsetOnAxis(ap=idx[:, e:e + 1], axis=0)).then_inc(xg_in[e % WRING], 16)

            block_h(BLOCKS - 2, 0)
            pool.wait_ge(lists_done, 2)
            pool.wait_ge(z_stored[0], 16 * (TILES // 2))
            pool.wait_ge(z_stored[1], 16 * (TILES // 2))
            for e in range(WRING):
                gather(e)
            gather(WRING)
            for k in range(2):
                pool.wait_ge(res_stored[k], 16 * (BLOCKS - LATE))
            for n in range(LATE):
                pool.wait_ge(late_stored[n], 32)
            for e in range(E):
                if e and WRING + e < E:
                    gather(WRING + e)
                pool.wait_ge(ye_done, e + 1)
                if e:
                    pool.wait_ge(added, 16 * e)
                pool.indirect_dma_start(out=out, out_offset=bass.IndirectOffsetOnAxis(ap=idx[:, e:e + 1], axis=0),
                                        in_=YE[:, e % WRING, :], in_offset=None, compute_op=ALU.add).then_inc(added, 16)
            pool.wait_ge(added, 16 * E)

        @block.scalar
        def _(act):
            nc.scalar.preload_act_table_set("natural_log_exp_and_others")
            def constants():
                act.wait_ge(attc_in, 32)
                act.activation(KA[S:P, :, :, :].rearrange("p q b c -> p (q b) c"), attc[S:P, 0:256].unsqueeze(1).to_broadcast([S, 4, 256]),
                               ACT.Copy).then_inc(const_b, 1)
                act.activation(QA[S:P, :, :, :, :].rearrange("p q n b c -> p (q n b) c"), attc[S:P, 256:384].unsqueeze(1).to_broadcast([S, 8, P]),
                               ACT.Copy).then_inc(const_b, 1)
                act.activation(MM[0:S, :, :], attc[0:S, 384:512].unsqueeze(1).to_broadcast([S, 2, P]), ACT.Copy).then_inc(const_b, 1)

            def more_constants():
                act.wait_ge(ident_in, 16)
                act.activation(identb[:, :], ident[:, :], ACT.Copy).then_inc(const_b, 1)
                act.activation(pick[:, :, :].rearrange("p a b -> p (a b)"), pickf[:, :], ACT.Copy).then_inc(const_b, 1)

            def body(t, p, i2):
                if active(t, -1):
                    u, q = t + 1, (p + 1) % 2
                    act.wait_ge(shift_done, t + 2)
                    after(act, qk_transposed, u - 1)
                    after(act, swap_done, (u - 1) * 2)
                    act.activation(XH[:, q, 0, :], X[:, u, :], ACT.Identity, bias=shift[:, p, 0:1], scale=rstd[:, p, 0:1]).then_inc(xhat_done, 1)
                if isinstance(t, int) and t == 0:
                    constants()
                if active(t, 2):
                    u, q = t - 2, p
                    act.wait_ge(max_transposed, u + 1)
                    after(act, scored, u - 1)
                    act.activation(MM[S:S + 16, q, :], mixb[0:16, :], ACT.Copy, scale=-1.0).then_inc(mm_done, 1)
                if active(t, 7):
                    u = t - 7
                    act.wait_ge(z_transposed, u + 1)
                    zt = ZT[:, :, bass.ds(u * P, P)] if not isinstance(u, int) else ZT[:, :, u * P:(u + 1) * P]
                    act.activation(zt, mix_ps[:, 0:2 * P].rearrange("p (a b) -> p a b", a=2), ACT.Copy).then_inc(zt_done, 1)
                if active(t, 1):
                    u, q = t - 1, (p + 1) % 2
                    for b in range(2):
                        act.wait_ge(kbd_done[b], u + 1)
                    after(act, max_scored, u - 1)
                    act.activation(KA[0:S, q, :, :], KBD[0:S, q, :, :], ACT.Copy).then_inc(ka_done, 1)
                if active(t, 6):
                    u, q = t - 6, p
                    act.wait_ge(shift_done, t + 3)
                    after(act, z_transposed, u - 1)
                    if not isinstance(u, int):
                        act.wait_ge(z_stored[q], (i2 - 3) * 16)
                    elif u >= 2:
                        act.wait_ge(z_stored[q], 16 * (u // 2))
                    act.activation(Z[:, q, :], X[:, u, :], ACT.Identity, bias=shift[:, 1 - q, 2:3], scale=rstd[:, 1 - q, 2:3]).then_inc(z_done, 1)
                if active(t, 2):
                    u, q = t - 2, p
                    act.wait_ge(scored, u + 1)
                    after(act, pv_done, u - 1)
                    act.activation(PT[:, q, :, :, :, :].rearrange("p n a b c -> p (n a b c)"),
                                   PS[:, 4:6, :].rearrange("p n c -> p (n c)"), ACT.Exp).then_inc(probs_done, 1)
                if active(t, 0):
                    u, q = t, p
                    act.wait_ge(qkt_done, u + 1)
                    after(act, max_scored, u - 1)
                    for nh in range(NH):
                        act.activation(QA[0:S, q, nh, :, :].rearrange("p b (nl s) -> p b nl s", nl=NL),
                                       QKT[nh * S:(nh + 1) * S, q, 0:NL, :].rearrange("p nl (b s) -> p b nl s", b=2),
                                       ACT.Copy).then_inc(qa_done, 1)
                if isinstance(t, int) and t == 1:
                    more_constants()
                if active(t, 3):
                    u = t - 3
                    act.wait_ge(pv_done, u + 1)
                    act.activation(logsum[:, :], pv_ps[:, 2 * P:4 * P], ACT.Ln).then_inc(log_done, 1)
                    act.wait_ge(log_done, u + 1)
                    after(act, ot_done, u)
                    act.activation(rsum[:, :], logsum[:, :], ACT.Exp, scale=-1.0).then_inc(rsum_done, 1)

            def block_silu(m, q, bank=0):
                act.wait_ge(gu_done, m * 3 + 3)
                after(act, h_done, (m - 1) * 2)
                act.activation(GA[0:IA, q, 0, :], B[bank][0:IA, :], ACT.Silu).then_inc(silu_done, 1)
                act.activation(UA[0:IA, q, 0, :], B[bank + 1][0:IA, :], ACT.Copy).then_inc(silu_done, 1)
                act.activation(GA[0:IB, q, 1, :], B[bank + 2][0:IB, :], ACT.Silu).then_inc(silu_done, 1)
                act.activation(UA[0:IB, q, 1, :], B[bank + 2][IB:2 * IB, :], ACT.Copy).then_inc(silu_done, 1)

            def block_dn(m):
                act.wait_ge(dn_done, m + 1)
                after(act, res_done, m * 2)
                for k in range(2):
                    act.activation(DS[:, k, :], B[3 + k][:, :], ACT.Copy).then_inc(dn_copied, 1)

            def body_and_ffn(t, p, i2):
                body(t, p, i2)
                if isinstance(t, int) and t == DRAIN + 1:
                    nc.scalar.preload_act_table_set("silu_and_others")
                elif isinstance(t, int) and t == DRAIN + 3:
                    act.wait_ge(roped, TILES * 2)
                    block_silu(0, 0)

            pipeline(act, body_and_ffn)

            block_silu(1, 1, 3)
            act.wait_ge(rt, 1)
            act.activation(RW[2][:, :], RW[1][:, :], ACT.Exp).then_inc(exp_done, 1)
            act.wait_ge(exp_done, 1)
            act.activation(RW[3][:, :], RW[2][:, :], ACT.Ln, bias=1.0).then_inc(ln_done, 1)
            block_dn(0)
            act.wait_ge(rt, 11)
            act.activation(RW[5][:, :], RW[1][:, :], ACT.Sqrt).then_inc(sqrt_done, 1)

            def pos_codes(c):
                act.wait_ge(coded, c + 1)
                if c >= 2:
                    act.wait_ge(dispatched, c - 1)
                act.activation(OBV[:, c % 2, :, 4, :], OBE[c % 2].rearrange("p n b e -> p n (b e)"), ACT.Identity,
                               bias=0.0, scale=rc[:, RC["pos"]:RC["pos"] + 1]).then_inc(pos_hot, 1)

            def weight_part(k):
                if k:
                    act.wait_ge(rest_done, k)
                else:
                    act.wait_ge(weighed, 1)
                act.activation(wv[k][:, :], (RW[3] if k else RW[5])[:, :], ACT.Copy).then_inc(part_copied, 1)

            block_silu(2, 0)
            block_dn(1)
            block_silu(3, 1)
            weight_part(0)
            block_dn(2)
            weight_part(1)
            weight_part(2)
            block_silu(4, 0)
            block_dn(3)
            pos_codes(0)
            block_silu(5, 1)
            pos_codes(1)
            block_dn(4)
            pos_codes(2)
            pos_codes(3)
            block_silu(BLOCKS - 2, 0)
            block_silu(BLOCKS - 1, 1)

            with act.Fori(0, E // WRING) as n:
                for r in range(WRING):
                    q = r % 2
                    act.wait_ge(ge_done, n * WRING + (r + 1))
                    act.activation(SE[0:IA, q, 0, :], ge_ps[q][0:IA, 0:P], ACT.Silu).then_inc(se_done, 1)
                    act.activation(SE[0:IB, q, 1, :], ge_ps[q][0:IB, 2 * P:3 * P], ACT.Silu).then_inc(se_done, 1)

        @block.tensor
        def _(pe):
            pe.wait_ge(warm_in, 1)
            zeros = PT[:, 0, 0, 0, :, :].rearrange("p a b -> p (a b)")

            def keep_warm(n):
                for _ in range(n):
                    pe.matmul(pv_ps[:, 0:2 * P], zeros[:, 0:P], zeros, start=True, stop=True)

            keep_warm(WARM[0])
            pe.wait_ge(ident_in, 16)

            def body(t, p, i2):
                if active(t, 0):
                    u, q = t, p
                    if isinstance(t, int) and t == 1:
                        keep_warm(WARM[1])
                    pe.wait_ge(swap_done, (u + 1) * 2)
                    pe.wait_ge(khat_done, (u + 1) * 3)
                    after(pe, roped, u * 2)
                    for v, bank in ((0, plain_ps), (1, swap_ps)):
                        for nl in range(NL):
                            pe.transpose(bank[:, nl * P:(nl + 1) * P], XH[:, q, v, nl * P:(nl + 1) * P], ident[:, :])
                        last = pe.transpose(bank[:, 2 * P:3 * P], KH[:, q, v, :], ident[:, :])
                    last.then_inc(qk_transposed, 1)
                def score(nh):
                    u, q = t - 2, p
                    rows = slice(nh * S, (nh + 1) * S)
                    for b in range(2):
                        for gp in range(2):
                            col = (b * 2 + gp) * P
                            pe.matmul(sc_ps[nh][:, col:col + P], KBD[rows, q, b, gp * P:(gp + 1) * P],
                                      QKT[rows, q, 0:NL, b * S:(b + 1) * S], start=(b == 0 and gp == 0), stop=False,
                                      skip_group_check=True)

                if active(t, 2):
                    after(pe, probs_done, t - 2)
                    score(0)
                if (active(t, 7) or active(t, 2)) and active(t, 5):
                    after(pe, x1_done, t - 4)
                if active(t, 7):
                    u, q = t - 7, (p + 1) % 2
                    pe.wait_ge(z_done, u + 1)
                    for c in range(2):
                        last = pe.transpose(mix_ps[:, c * P:(c + 1) * P], Z[:, q, c * P:(c + 1) * P], ident[:, :])
                    last.then_inc(z_transposed, 1)
                if active(t, 2):
                    u, q = t - 2, p
                    pe.wait_ge(max_done, u + 1)
                    if isinstance(t, int) and u == 0:
                        pe.wait_ge(const_b, 5)
                    pe.transpose(mixb[0:16, 0:P], MX[:, q, :], identb[:, :]).then_inc(max_transposed, 1)
                if active(t, 2):
                    score(1)
                    pe.wait_ge(mm_done, t - 1)
                    for nh in range(NH):
                        for b in range(2):
                            for gp in range(2):
                                col = (b * 2 + gp) * P
                                last = pe.matmul(sc_ps[nh][:, col:col + P], pick[:, (nh * 2 + b) * 2 + gp, :], MM[:, p, :],
                                                 start=False, stop=True, skip_group_check=True)
                    last.then_inc(scored, 1)
                if active(t, 1):
                    u, q = t - 1, (p + 1) % 2
                    if isinstance(t, int) and u == 0:
                        keep_warm(WARM[2])
                        pe.wait_ge(const_b, 3)
                    pe.wait_ge(ka_done, u + 1)
                    pe.wait_ge(qa_done, (u + 1) * 2)
                    after(pe, max_done, u)
                    for nh in range(NH):
                        for b in range(2):
                            last = pe.matmul(max_ps[nh][:, b * 256:(b + 1) * 256], QA[:, q, nh, b, :], KA[:, q, b, :],
                                             start=True, stop=True)
                    last.then_inc(max_scored, 1)
                if active(t, 3):
                    u, q = t - 3, (p + 1) % 2
                    pe.wait_ge(probs_done, u + 1)
                    if isinstance(u, int):
                        pe.wait_ge(v_in[q], 64 * (u // 2 + 1))
                    else:
                        pe.wait_ge(v_in[q], (i2 * 2 - 3 + p - q) * 32 + 64)
                    after(pe, ot_done, u)
                    for nh in range(NH):
                        for gp in range(2):
                            r0 = 32 * (2 * nh + gp)
                            for b in range(2):
                                probs = PT[:, q, nh, b, gp, :]
                                pe.matmul(pv_ps[r0:r0 + 32, b * P:(b + 1) * P],
                                          VBD[:, q, b, gp, :, :].rearrange("p a b -> p (a b)"), probs, start=True, stop=True)
                                last = pe.matmul(pv_ps[r0:r0 + 32, (2 + b) * P:(3 + b) * P], attc[:, 512:544], probs,
                                                 start=True, stop=True)
                    last.then_inc(pv_done, 1)
                if active(t, 4):
                    u, q = t - 4, p
                    if isinstance(t, int) and u == 0:
                        pe.wait_ge(wout_in, 16)
                    pe.wait_ge(ot_done, u + 1)
                    if active(t, 2):
                        pe.wait_ge(mm_done, t - 1)
                    if active(t, 7):
                        pe.wait_ge(zt_done, t - 6)
                    if active(t, 5):
                        pe.wait_ge(x1_done, t - 4)
                    for nl in range(NL):
                        last = pe.matmul(mix_ps[:, 0:D], OT[:, q, nl, :, :].rearrange("p a b -> p (a b)"), WO[:, nl, :],
                                         start=(nl == 0), stop=(nl == NL - 1))
                    last.then_inc(projected, 1)

            GU = ((0, IA), (IA, 2 * IA), (2 * IA, I2))

            def gu_part(m, k, bank):
                cols = slice(m * 512, (m + 1) * 512)
                lo, hi = GU[k]
                for c in range(2):
                    last = pe.matmul(B[bank][0:hi - lo, :], WS13[:, c, lo:hi], ZT[:, c, cols], start=(c == 0), stop=(c == 1))
                last.then_inc(gu_done, 1)

            def body_and_ffn(t, p, i2):
                if isinstance(t, int) and t >= DRAIN:
                    part = t - DRAIN
                    if part == 0:
                        pe.wait_ge(ws_in, 64)
                        pe.wait_ge(zt_done, 8)
                        pe.wait_ge(roped, TILES * 2)
                    elif part == 2:
                        pe.wait_ge(max_done, TILES)
                    elif part == 4:
                        pe.wait_ge(probs_done, TILES)
                    gu_part(part // 3, part % 3, part)
                body(t, p, i2)

            pipeline(pe, body_and_ffn)

            pe.wait_ge(zt_done, TILES)
            pe.wait_ge(zero_done, 2)
            for k in range(2):
                for c in range(2):
                    for j in range(4):
                        n = k * 4 + j
                        last = pe.matmul(B[6 + k][32 * j:32 * j + 32, :], GW[:, c, :], ZT[:, c, n * 512:(n + 1) * 512],
                                         start=(c == 0), stop=(c == 1), skip_group_check=True)
                last.then_inc(lg_done, 1)
            pe.wait_ge(silu_done, 4)
            for k in range(2):
                pe.wait_ge(ls_done, k + 1)
                for c in range(4):
                    last = pe.transpose(B[k][:, c * P:(c + 1) * P], LS[:, k, c * P:(c + 1) * P], ident[:, :])
                last.then_inc(lt_done, 1)

            def block_gu(m):
                pe.wait_ge(silu_done, 4 if m == 2 else m * 4)
                for k in range(3):
                    gu_part(m, k, k)

            def block_down(m, q):
                if m == BLOCKS - 1:
                    pe.wait_ge(late_h_done, 2)
                else:
                    pe.wait_ge(h_done, m * 2 + 2)
                if m > BLOCKS - LATE:
                    pe.wait_ge(late_res_done, (m - (BLOCKS - LATE)) * 2)
                else:
                    after(pe, dn_copied, m * 2)
                for j in range(4):
                    o = B[3 + j // 2][:, (j % 2) * D:(j % 2 + 1) * D]
                    pe.matmul(o, H[0:IA, q, 0, j * P:(j + 1) * P], WS2[0:IA, 0, :], start=True, stop=False)
                    last = pe.matmul(o, H[0:IB, q, 1, j * P:(j + 1) * P], WS2[0:IB, 1, :], start=False, stop=True)
                last.then_inc(dn_done, 1)

            def prefix():
                pe.wait_ge(mask_done, 1)
                pe.matmul(B[5][:, :], trib[:, :], MB[:, :], start=True, stop=True)
                pe.matmul(B[6][:, :], onesb[:, :], MB[:, :], start=True, stop=True).then_inc(prefix_done, 1)

            def dispatch(c):
                pe.wait_ge(hot_done, c + 1)
                pe.wait_ge(tiles_hot, c + 1)
                pe.wait_ge(pos_hot, c + 1)
                for i in range(HT):
                    for h, bank in ((0, B[7]), (1, B[5])):
                        last = pe.matmul(bank[:, 0:NV * 64], OA[:, c % 2, i * 2 + h, :, :].rearrange("p a e -> p (a e)"),
                                         OBV[:, c % 2, i * 2 + h, :, :].rearrange("p v b -> p (v b)"),
                                         start=(c == 0 and i == 0), stop=(c == 3 and i == HT - 1), skip_group_check=True)
                last.then_inc(dispatched, 1)

            def lists():
                pe.wait_ge(lay_done, 1)
                for hv in range(4):
                    h, v = hv // 2, hv % 2
                    last = pe.matmul(B[6][:, v * E + h * 8:v * E + h * 8 + 8], lay[:, hv, :, :].rearrange("p b a -> p (b a)"),
                                     rc[:, RC["blk"]:RC["blk"] + 8], start=True, stop=True)
                last.then_inc(listed, 1)

            pe.wait_ge(silu_done, 8)
            block_down(0, 0)
            pe.wait_ge(l_done, 2)
            block_gu(2)
            block_down(1, 1)
            block_gu(3)
            block_down(2, 0)
            prefix()
            block_gu(4)
            block_down(3, 1)
            block_gu(5)
            dispatch(0)
            block_down(4, 0)
            dispatch(1)
            block_gu(6)
            dispatch(2)
            dispatch(3)
            block_down(5, 1)
            lists()
            block_gu(7)

            def expert_t(n, r):
                q = r % 2
                pe.wait_ge(xg_in[r], n * 16 + 16)
                e = n * WRING + r
                after(pe, xe_done, e - 1)
                for c in range(2):
                    last = pe.transpose(xe_ps[q][:, c * P:(c + 1) * P], XG[:, r, c * P:(c + 1) * P], ident[:, :])
                last.then_inc(xe_t, 1)

            def expert_gu(n, r):
                q = r % 2
                e = n * WRING + r
                pe.wait_ge(w_in[r], n * 48 + 48)
                pe.wait_ge(xe_done, e + 1)
                after(pe, he_done, (e - 1) * 2)
                for k, (lo, hi) in enumerate(((0, IA), (IA, 2 * IA), (2 * IA, I2))):
                    for c in range(2):
                        last = pe.matmul(ge_ps[q][0:hi - lo, k * P:(k + 1) * P], W13[:, r, c, lo:hi], XE[:, q, c, :],
                                         start=(c == 0), stop=(c == 1))
                last.then_inc(ge_done, 1)

            def expert_down(n, r):
                q = r % 2
                e = n * WRING + r
                pe.wait_ge(he_done, e * 2 + 2)
                after(pe, ye_done, e - 1)
                pe.matmul(ye_bank[q][:, 0:D], HE[0:IA, q, 0, :], W2[0:IA, r, 0, :], start=True, stop=False)
                pe.matmul(ye_bank[q][:, 0:D], HE[0:IB, q, 1, :], W2[0:IB, r, 1, :], start=False, stop=True).then_inc(ye_ps, 1)

            def experts(n):
                for r in range(WRING):
                    if r < WRING - 1:
                        expert_t(n, r + 1)
                    else:
                        expert_t(n + 1, 0) if not (isinstance(n, int) and n == E // WRING - 1) else None
                    if isinstance(n, int) and n == 0 and r < 2:
                        expert_gu(0, 1) if r else expert_down(0, 0)
                        continue
                    expert_gu(n, r)
                    if r > 0:
                        expert_down(n, r - 1)
                    elif not (isinstance(n, int) and n == 0):
                        expert_down(n - 1, WRING - 1)

            expert_t(0, 0)
            block_down(BLOCKS - 2, 0)
            expert_gu(0, 0)
            block_down(BLOCKS - 1, 1)
            experts(0)
            with pe.Fori(1, E // WRING - 1) as n:
                experts(n)
            experts(E // WRING - 1)
            expert_down(E // WRING - 1, WRING - 1)

        @block.vector
        def _(dve):
            dve.memset(PT[:, 0, 0, 0, :, :], 0.0).then_inc(warm_in, 1)
            dve.memset(negmean[:, :, :], 0.0).then_inc(tables, 1)
            dve.wait_ge(tables, 1)

            def rope_tables():
                dve.wait_ge(rope_in, 32)
                for v in range(2):
                    for nl in range(NL):
                        dve.tensor_scalar(ropet[:, v, nl, :], ropec[:, v * P:(v + 1) * P], qkn[:, v, nl:nl + 1], HD ** -0.5, ALU.mult, ALU.mult).then_inc(tables, 1)
                    dve.tensor_scalar(ropet[:, v, NL, :], ropec[:, v * P:(v + 1) * P], qkn[:, v, NL:NL + 1], None, ALU.mult).then_inc(tables, 1)
                dve.wait_ge(tables, 7)

            def body(t, p, i2):
                rolled = not isinstance(t, int)
                q = (p + 1) % 2

                def stats_ready():
                    if active(t, -2):
                        dve.wait_ge(stats_done, (t + 3) * 2)
                    if active(t, 6):
                        dve.wait_ge(z_stats, t - 5)

                if active(t, -2):
                    x_loaded(dve, t, -2)
                    dve.bn_stats(stats[:, q, 0, :], X[:, t + 2, :]).then_inc(stats_done, 1)
                    dve.bn_stats(stats[:, q, 1, :], C[:, t + 2, :]).then_inc(stats_done, 1)
                if active(t, 5):
                    u = t - 5
                    dve.wait_ge(projected, u + 1)
                    dve.tensor_tensor(X[:, u, :], X[:, u, :], mix_ps[:, 0:D], ALU.add).then_inc(x1_done, 1)
                if rolled:
                    stats_ready()
                if active(t, 1):
                    key_blocks(dve, t - 1, q, 0)
                if not rolled:
                    stats_ready()
                if active(t, -2):
                    for k in range(2):
                        dve.bn_aggr(mv[:, q, k, :], stats[:, q, k, :]).then_inc(aggr_done, 1)
                if active(t, 6):
                    dve.bn_aggr(mv[:, q, 2, :], stats[:, p, 2, :]).then_inc(z_aggr, 1)
                if active(t, 4):
                    u = t - 4
                    dve.wait_ge(rsum_done, u + 1)
                    after(dve, projected, u - 1)
                    if rolled:
                        dve.wait_ge(x1_done, t - 4)
                    dve.tensor_tensor(OT[:, p, :, :, :].rearrange("p nl b s -> p b nl s"),
                                      pv_ps[:, 0:2 * P].rearrange("p (b nl s) -> p b nl s", b=2, nl=NL),
                                      rsum[:, :].rearrange("p (b nl s) -> p b nl s", b=2, nl=NL), ALU.mult).then_inc(ot_done, 1)
                if active(t, -2):
                    dve.wait_ge(aggr_done, (t + 3) * 2)
                    after(dve, shift_done, t + 1)
                    dve.tensor_scalar(veps[:, q:q + 1], mv[:, q, 1, 1:2], RMS_EPS, None, ALU.add).then_inc(veps_done, 1)
                    dve.tensor_scalar(var_in[:, q, 0:1], mv[:, q, 0, 1:2], 1.0 + RMS_EPS, LN_EPS * RMS_EPS, ALU.mult, ALU.add).then_inc(var_done, 1)
                    dve.tensor_scalar(negmean[:, q, 0:1], mv[:, q, 0, 0:1], -1.0, None, ALU.mult).then_inc(var_done, 1)
                if active(t, 6):
                    dve.wait_ge(z_aggr, t - 5)
                    after(dve, shift_done, t + 1)
                    dve.tensor_scalar(var_in[:, q, 2:3], mv[:, q, 2, 1:2], LN_EPS, None, ALU.add).then_inc(z_var, 1)
                    dve.tensor_scalar(negmean[:, q, 2:3], mv[:, q, 2, 0:1], -1.0, None, ALU.mult).then_inc(z_var, 1)
                if active(t, -2):
                    dve.wait_ge(veps_done, t + 3)
                    dve.scalar_tensor_tensor(out=var_in[:, q, 1:2], in0=mv[:, q, 1, 0:1], scalar=mv[:, q, 1, 0:1],
                                             in1=veps[:, q:q + 1], op0=ALU.mult, op1=ALU.add).then_inc(var_done, 1)
                if active(t, 5):
                    if not rolled:
                        dve.wait_ge(x1_done, t - 4)
                    dve.bn_stats(stats[:, q, 2, :], X[:, t - 5, :]).then_inc(z_stats, 1)
                if active(t, 0):
                    u, q = t, p
                    dve.wait_ge(qk_transposed, u + 1)
                    after(dve, qkt_done, u)
                    for v, bank in ((0, plain_ps), (1, swap_ps)):
                        dve.tensor_tensor(rp[:, v, :], bank[:, 0:3 * P], ropet[:, v, :, :].rearrange("p a b -> p (a b)"), ALU.mult).then_inc(roped, 1)
                if active(t, -1):
                    u, q = t + 1, (p + 1) % 2
                    dve.wait_ge(rstd_done, u + 1)
                    cv = C[:, u, :].unsqueeze(1).to_broadcast([P, 2, KV])
                    dve.tensor_scalar(KH[:, q, 0, :].rearrange("p (a c) -> p a c", a=2), cv, rstd[:, p, 1:2], None, ALU.mult).then_inc(khat_done, 1)
                    cs = C[:, u, :].rearrange("p (g h d) -> p g h d", h=2, d=8)
                    ks = KH[:, q, 1, :].rearrange("p (a g h d) -> p a g h d", a=2, h=2, d=8)
                    for h in range(2):
                        dve.tensor_scalar(ks[:, :, :, 1 - h, :], cs[:, :, h, :].unsqueeze(1).to_broadcast([P, 2, G, 8]),
                                          rstd[:, p, 1:2], None, ALU.mult).then_inc(khat_done, 1)
                if isinstance(t, int) and t == -1:
                    rope_tables()
                if active(t, 1):
                    u, q = t - 1, (p + 1) % 2
                    dve.wait_ge(max_scored, u + 1)
                    after(dve, max_transposed, u - 1)
                    dve.tensor_reduce(MX[:, q, :], PS[:, 2:4, :].rearrange("p n (a k) -> p (n a) k", k=S), AX.X, ALU.max).then_inc(max_done, 1)

            pipeline(dve, body)

            step = [0]

            def link(ins):
                step[0] += 1
                ins.then_inc(rt, 1)
                dve.wait_ge(rt, step[0])

            def rcc(name, n):
                return rc[:, RC[name]:RC[name] + n]

            def te(ap):
                return ap.rearrange("p (n e) -> p n e", e=E)

            def per_tile(ap):
                return ap.unsqueeze(2).to_broadcast([P, TILES, E])

            def per_expert(ap):
                return ap.unsqueeze(1).to_broadcast([P, TILES, E])

            def et(ap):
                return ap.rearrange("p (e n) -> p e n", e=E)

            for k in range(2):
                dve.wait_ge(lg_done, k + 1)
                dve.tensor_copy(LS[:, k, :], B[6 + k][:, :]).then_inc(ls_done, 1)
            L = RW[0]
            for k in range(2):
                dve.wait_ge(lt_done, k + 1)
                dve.tensor_copy(L[:, k * 256:(k + 1) * 256].rearrange("p (j c e) -> p j c e", j=4, c=4),
                                B[k][:, :].rearrange("p (c j e) -> p j c e", c=4, j=4)[:, :, :, 0:E]).then_inc(l_done, 1)
            dve.wait_ge(l_done, 2)
            dve.wait_ge(rc_in, 32)
            link(dve.scalar_tensor_tensor(out=RW[1][:, :], in0=L[:, :], scalar=-1.0, in1=L[:, :], op0=ALU.mult, op1=ALU.min))
            anew, tots = ab_i[:, 0, :].bitcast(f32), ab_i[:, 1, :].bitcast(f32)
            link(dve.memset(anew, 1.0))
            dve.memset(et(anew)[:, :, 0:1], 0.0)
            dve.memset(et(tots)[:, :, 0:1], 0.0)
            ex, lg, sr = RW[2], RW[3], RW[4]
            dve.wait_ge(exp_done, 1)
            link(dve.tensor_scalar(sr[:, :], ex[:, :], 1.0 / 5, None, ALU.mult))
            for c in (-1.0 / 4, 1.0 / 3, -1.0 / 2, 1.0):
                link(dve.scalar_tensor_tensor(out=sr[:, :], in0=sr[:, :], scalar=c, in1=ex[:, :], op0=ALU.add, op1=ALU.mult))
            dve.wait_ge(ln_done, 1)
            link(dve.tensor_tensor(sr[:, :], sr[:, :], lg[:, :], ALU.subtract))
            link(dve.scalar_tensor_tensor(out=sr[:, :], in0=ex[:, :], scalar=1.0 / 16, in1=sr[:, :], op0=ALU.is_lt, op1=ALU.mult))
            link(dve.tensor_tensor(lg[:, :], lg[:, :], sr[:, :], ALU.add))
            link(dve.scalar_tensor_tensor(out=RW[1][:, :], in0=L[:, :], scalar=0.0, in1=lg[:, :], op0=ALU.max, op1=ALU.add))
            assert step[0] == 11
            dve.tensor_copy(trib[:, :], rcc("tri", P))
            dve.memset(onesb[:, :], 1.0)
            dve.tensor_copy(te(wv[3][:, :]), per_tile(rcc("tile", TILES)))
            dve.tensor_copy(iat[:, :, :], rcc("ia", 16).unsqueeze(2).to_broadcast([P, 16, 8]))
            dve.tensor_copy(ibt[:, :, :], rcc("ib", 8).unsqueeze(2).to_broadcast([P, 8, 8]))
            dve.wait_ge(sqrt_done, 1)
            sc, key, hot1, hot2 = RW[5], RW[0], RW[1], RW[2]
            link(dve.tensor_tensor(te(key[:, :]), te(sc[:, :]), per_expert(GB[:, :]), ALU.add))
            for n, hot in enumerate((hot1, hot2)):
                if n:
                    link(dve.scalar_tensor_tensor(out=key[:, :], in0=hot1[:, :], scalar=-3e38, in1=key[:, :], op0=ALU.mult, op1=ALU.add))
                link(dve.tensor_reduce(RS[0][:, :], te(key[:, :]), AX.X, ALU.max))
                link(dve.tensor_tensor(te(hot[:, :]), te(key[:, :]), per_tile(RS[0][:, :]), ALU.is_equal))
                link(dve.tensor_tensor(te(hot[:, :]), te(hot[:, :]), per_expert(rcc("desc", E)), ALU.mult))
                link(dve.tensor_reduce(RS[0][:, :], te(hot[:, :]), AX.X, ALU.max))
                link(dve.tensor_tensor(te(hot[:, :]), te(hot[:, :]), per_tile(RS[0][:, :]), ALU.is_equal))
            M = RW[3]
            link(dve.tensor_tensor(M[:, :], hot1[:, :], hot2[:, :], ALU.add))
            dve.tensor_copy(MB[:, :], M[:, :]).then_inc(mask_done, 1)
            wd = RW[5]
            link(dve.tensor_tensor(wd[:, :], sc[:, :], M[:, :], ALU.mult))
            link(dve.tensor_reduce(RS[1][:, :], te(wd[:, :]), AX.X, ALU.add))
            link(dve.reciprocal(RS[1][:, :], RS[1][:, :]))
            no = RW[0]
            dve.tensor_scalar(no[:, :], M[:, :], -1.0, 1.0, ALU.mult, ALU.add)
            dve.tensor_tensor(te(wd[:, :]), te(wd[:, :]), per_tile(RS[1][:, :]), ALU.mult).then_inc(weighed, 1)
            dve.wait_ge(weighed, 1)
            off, low, place = RW[1], RW[2], RW[4]
            link(dve.tensor_tensor(te(off[:, :]), te(no[:, :]), per_tile(rcc("rev", TILES)), ALU.mult))
            before = RW[6]
            dve.wait_ge(prefix_done, 1)
            link(dve.tensor_copy(et(tots)[:, :, 1:TILES], B[6][:, 0:(TILES - 1) * E].rearrange("p (n e) -> p e n", e=E)))
            dve.tensor_tensor(place[:, :], B[5][:, :], off[:, :], ALU.add)
            link(dve.tensor_tensor_scan(before[:, :], anew, tots, 0.0, ALU.mult, ALU.add))
            link(dve.tensor_tensor(cnt[:, :].unsqueeze(2), et(before[:, :])[:, :, TILES - 1:TILES],
                                   B[6][:, (TILES - 1) * E:TILES * E].unsqueeze(2), ALU.add))
            link(dve.tensor_tensor(te(low[:, :]), te(no[:, :]), per_expert(cnt[:, :]), ALU.mult))
            link(dve.tensor_tensor(te(place[:, :]), te(place[:, :]), before[:, :].rearrange("p (e n) -> p n e", e=E), ALU.add))
            link(dve.tensor_tensor(low[:, :], place[:, :], low[:, :], ALU.is_lt))
            link(dve.scalar_tensor_tensor(out=place[:, :], in0=low[:, :], scalar=FAR, in1=place[:, :], op0=ALU.mult, op1=ALU.add))
            link(dve.tensor_copy(slot_i[:, :], place[:, :]))
            link(dve.tensor_scalar(ab_i[:, 0, :], slot_i[:, :], 3, None, ALU.logical_shift_right))
            link(dve.tensor_scalar(ab_i[:, 1, :], slot_i[:, :], 7, None, ALU.bitwise_and))
            link(dve.tensor_copy(hib[:, :], ab_i[:, 0, :]))
            link(dve.tensor_copy(lob[:, :], ab_i[:, 1, :]))

            dve.wait_ge(part_copied, 3)
            for c in range(4):
                if c >= 2:
                    dve.wait_ge(dispatched, c - 1)
                dve.tensor_tensor(OA[:, c % 2, :, :, :], iat[:, :, :].unsqueeze(1).to_broadcast([P, HN, 16, 8]),
                                  quarter(hib, c, 16), ALU.is_equal)
                if c >= 2:
                    dve.wait_ge(tiles_hot, c - 1)
                    dve.wait_ge(pos_hot, c - 1)
                dve.tensor_tensor(OBE[c % 2], ibt[:, :, :].unsqueeze(1).to_broadcast([P, HN, 8, 8]),
                                  quarter(lob, c, 8), ALU.is_equal).then_inc(coded, 1)
                dve.wait_ge(coded, c + 1)
                for v in range(3):
                    last = dve.tensor_tensor(OBV[:, c % 2, :, v, :].rearrange("p n (b e) -> p n b e", e=8), OBE[c % 2],
                                             quarter(wv[v], c, 8), ALU.mult)
                last.then_inc(hot_done, 1)
            dve.wait_ge(dispatched, 4)
            for h, bank in ((0, B[7]), (1, B[5])):
                ins = dve.tensor_tensor(dg[:, h, :, :], bank[:, 0:NV * 64].rearrange("p (v e) -> p v e", e=8),
                                        rcc("blk", 8).unsqueeze(1).to_broadcast([P, NV * 8, 8]), ALU.mult)
            link(ins)
            link(dve.tensor_reduce(dv[:, :, :, :].rearrange("p h v b -> p (h v b)"), dg[:, :, :, :].rearrange("p h v e -> p (h v) e"), AX.X, ALU.add))
            drv = dr[:, :, :].rearrange("p (h v) b -> p h v b", v=2)
            dve.scalar_tensor_tensor(out=drv[:, :, 0, :], in0=dv[:, :, 3, :], scalar=float(P), in1=dv[:, :, 4, :], op0=ALU.mult, op1=ALU.add)
            link(dve.tensor_tensor(drv[:, :, 1, :], dv[:, :, 1, :], dv[:, :, 2, :], ALU.add))
            link(dve.tensor_tensor(drv[:, :, 1, :], drv[:, :, 1, :], dv[:, :, 0, :], ALU.add))
            dve.tensor_tensor(lay[:, :, :, :].rearrange("p v b a -> p (v b) a"),
                              dr[:, :, :].rearrange("p v b -> p (v b)").unsqueeze(2).to_broadcast([P, 32, 16]),
                              rcc("sel", 16).unsqueeze(1).to_broadcast([P, 32, 16]), ALU.mult).then_inc(lay_done, 1)
            dve.wait_ge(listed, 1)
            dve.tensor_copy(idx[:, :], B[6][:, 0:E]).then_inc(lists_done, 1)
            dve.tensor_copy(wslot[:, :], B[6][:, E:2 * E]).then_inc(lists_done, 1)
            dve.wait_ge(lists_done, 2)

            def late_res(n):
                m = BLOCKS - LATE + n
                dve.wait_ge(dn_done, m + 1)
                if n == 1:
                    for k in range(2):
                        dve.wait_ge(res_stored[k], (BLOCKS - LATE) * 16)
                elif n >= 2:
                    dve.wait_ge(late_stored[n - 2], 32)
                for k in range(2):
                    dve.tensor_tensor(OUTB[:, (n + 1) % 2, k, :].rearrange("p (j c) -> p j c", j=2),
                                      B[3 + k][:, :].rearrange("p (j c) -> p j c", j=2),
                                      X[:, m * 4 + 2 * k:m * 4 + 2 * k + 2, :], ALU.add).then_inc(late_res_done, 1)

            def xe(e, r):
                q = r % 2
                dve.wait_ge(xe_t, e + 1)
                after(dve, ge_done, e - 1)
                dve.tensor_copy(XE[:, q, :, :].rearrange("p a b -> p (a b)"), xe_ps[q][:, 0:2 * P]).then_inc(xe_done, 1)

            def he(e, r):
                q = r % 2
                dve.wait_ge(se_done, e * 2 + 2)
                after(dve, ye_ps, e - 1)
                dve.tensor_tensor(HE[0:IA, q, 0, :], ge_ps[q][0:IA, P:2 * P], SE[0:IA, q, 0, :], ALU.mult).then_inc(he_done, 1)
                dve.tensor_tensor(HE[0:IB, q, 1, :], ge_ps[q][IB:2 * IB, 2 * P:3 * P], SE[0:IB, q, 1, :], ALU.mult).then_inc(he_done, 1)

            def ye(e, r):
                q = r % 2
                dve.wait_ge(ye_ps, e + 1)
                after(dve, added, (e - WRING + 1) * 16)
                dve.tensor_scalar(YE[:, r, :], ye_bank[q][:, 0:D], wslot[:, bass.ds(e, 1)] if not isinstance(e, int) else wslot[:, e:e + 1], None, ALU.mult).then_inc(ye_done, 1)

            def experts(n, first=False, last=False):
                for r in range(WRING):
                    e = n * WRING + r
                    if not (last and r == WRING - 1):
                        xe(e + 1, (r + 1) % WRING)
                    if first and r == 0:
                        ye(0, 0)
                    else:
                        he(e, r)
                    if not (first and r < 2):
                        ye(e - 1, (r - 1) % WRING)

            late_res(0)
            dve.wait_ge(silu_done, 4 * BLOCKS)
            dve.wait_ge(dn_done, BLOCKS - 2)
            for c, n in ((0, IA), (1, IB)):
                dve.tensor_tensor(H[0:n, 1, c, :], GA[0:n, 1, c, :], UA[0:n, 1, c, :], ALU.mult).then_inc(late_h_done, 1)
            xe(0, 0)
            late_res(1)
            he(0, 0)
            late_res(2)
            experts(0, first=True)
            with dve.Fori(1, E // WRING - 1) as n:
                experts(n)
            experts(E // WRING - 1, last=True)
            ye(E - 1, WRING - 1)


_INS = ["x", "ctx", "qk_norm", "w_out", "gate_w", "gate_b", "w13", "w2", "ws13", "ws2",
        "const_rope", "const_attn", "const_pick", "const_route"]


def _constants(np):
    p = np.arange(128)
    pos = np.arange(64)
    inv = (np.float32(1.0) / np.float32(10000.0) ** (np.arange(0, 16, 2, dtype=np.float32) / np.float32(16))).astype(np.float32)
    ang = np.outer(inv[p % 8], np.tile(pos, 2).astype(np.float32)).astype(np.float32)
    sign = np.where(p % 16 < 8, -1.0, 1.0)[:, None]
    kmask = (p[:, None] % 64 // 16 == np.arange(4)[None, :])
    rope = np.concatenate([np.eye(128), np.cos(ang), np.sin(ang) * sign, kmask], 1)

    attn = np.zeros((128, 544))
    j = np.arange(64)[:, None]
    attn[64:, 0:256] = np.tile(np.where(pos[None, :] > j, -1e30, 0.0), (1, 4))
    attn[64:, 256:384] = np.tile(np.eye(64), (1, 2))
    attn[:64, 384:512] = np.tile(np.where(j > pos[None, :], -1e30, 0.0), (1, 2))
    attn[:, 512:544] = p[:, None] // 64 == np.arange(32)[None, :] // 16

    pick = np.zeros((80, 8, 2, 64))
    pick[:64] = np.eye(64)[:, None, None, :]
    for blk in range(8):
        nb, gp = blk // 2, blk % 2
        for g2 in range(2):
            pick[64 + nb * 4 + gp * 2 + g2, blk, g2, :] = 1.0

    route = np.zeros((128, 264))
    tok = np.arange(32)[None, :] * 128 + p[:, None]
    route[:, RC["desc"]:RC["desc"] + 16] = 16 - np.arange(16)
    route[:, RC["tri"]:RC["tri"] + 128] = p[:, None] < p[None, :]
    route[:, RC["ia"]:RC["ia"] + 16] = np.arange(16)
    route[:, RC["ib"]:RC["ib"] + 8] = np.arange(8)
    route[:, RC["rev"]:RC["rev"] + 32] = 127 - tok
    route[:, RC["tile"]:RC["tile"] + 32] = np.arange(32)
    route[:, RC["pos"]] = p
    route[:, RC["blk"]:RC["blk"] + 8] = p[:, None] % 8 == np.arange(8)[None, :]
    route[:, RC["sel"]:RC["sel"] + 16] = p[:, None] // 8 == np.arange(16)[None, :]
    return {"const_rope": rope, "const_attn": attn, "const_pick": pick.reshape(80, 1024), "const_route": route}


def kernel(**inputs):
    import numpy as np
    import concourse.bacc as bacc
    from concourse.bass_utils import run_bass_kernel_spmd

    a = {k: np.asarray(v) for k, v in inputs.items()}
    order = np.arange(256).reshape(4, 2, 2, 16).transpose(2, 1, 0, 3).reshape(-1)
    swap = order.reshape(-1, 2, 8)[:, ::-1].reshape(-1)
    kv = np.arange(64)
    kvswap = kv.reshape(-1, 2, 8)[:, ::-1].reshape(-1)

    def rows(w):
        return w[order].reshape(2, 128, -1).transpose(1, 0, 2)

    def gate_up(w1, w3):
        return rows(np.concatenate([w1[:112], w3[:112], w1[112:], w3[112:]], 0).T)

    wq, wk = a["L0_xattn_q_norm_w"], a["L0_xattn_k_norm_w"]
    arrays = {
        "x": a["x"].reshape(4096, 256)[:, order],
        "ctx": a["ctx_512"].reshape(4096, 64),
        "qk_norm": np.concatenate([np.stack([wq[order].reshape(2, 128), wq[swap].reshape(2, 128)]).transpose(2, 0, 1),
                                   np.stack([np.tile(wk[kv], 2), np.tile(wk[kvswap], 2)], 1)[:, :, None]], 2),
        "w_out": rows(a["L0_xattn_w_out"].T[:, order]),
        "gate_w": rows(a["L0_ffn_gate_w"].T),
        "gate_b": a["L0_ffn_gate_b"].reshape(1, 16),
        "w13": np.stack([gate_up(a["L0_ffn_W1"][e], a["L0_ffn_W3"][e]) for e in range(16)]),
        "w2": a["L0_ffn_W2"].transpose(0, 2, 1)[:, :, order],
        "ws13": gate_up(a["L0_ffn_Ws1"], a["L0_ffn_Ws3"]),
        "ws2": a["L0_ffn_Ws2"].T[:, order],
    }
    arrays.update({k: v.astype(np.float32) for k, v in _constants(np).items()})

    nc = bacc.Bacc("TRN2", target_bir_lowering=False, num_devices=1)
    feed, args = {}, []
    for name in _INS:
        v = np.ascontiguousarray(arrays[name])
        feed[name] = v
        args.append(nc.dram_tensor(name, v.shape, mybir.dt.from_np(v.dtype), kind="ExternalInput").ap())
    args.append(nc.dram_tensor("out", (4096, 256), mybir.dt.float32, kind="ExternalOutput").ap())
    xattn_moe_kernel(nc, *args)
    r = run_bass_kernel_spmd(nc, [feed], core_ids=[0])
    y = r.results[0]["out"]
    return y.reshape(64, 64, 2, 2, 4, 16).transpose(0, 1, 4, 3, 2, 5).reshape(64, 64, 256)
```
